# Optimizing a Trainium2 kernel written in Bass

```python
import numpy as np
import jax
import jax.numpy as jnp

def _softmax(x, axis=-1):
    return jax.nn.softmax(x, axis=axis)

def _gelu(x):
    return jax.nn.gelu(x, approximate=True)

def _silu(x):
    return jax.nn.silu(x)

def _sigmoid(x):
    return jax.nn.sigmoid(x)

def _layernorm(x, axis=-1, eps=1e-05):
    m = jnp.mean(x, axis=axis, keepdims=True)
    v = jnp.var(x, axis=axis, keepdims=True)
    return (x - m) / jnp.sqrt(v + eps)

def _scatter_add(tgt, idx, src, axis=0):
    return tgt.at[idx].add(src)

def _segment_sum(src, seg, n):
    return jax.ops.segment_sum(src, seg, n)
kernel_name = 'mk_adaln_d1_jaxref_r8_084329'

def setup_inputs(seed: int=0):
    np.random.seed(seed)
    _w = jnp.asarray

    def _L0_attn_setup():
        import jax, jax.numpy as jnp
        import numpy as np
        B, L, D, H = (4, 256, 128, 16)
        DK = D // H
        key = jax.random.key(seed)
        ks = jax.random.split(key, 5)
        x = jax.random.normal(ks[0], (B, L, D), dtype=jnp.float32)
        scale = 1.0 / np.sqrt(D)
        W_qkv = jax.random.normal(ks[1], (D, 3 * D), dtype=jnp.float32) * scale
        b_qkv = jnp.zeros((3 * D,), dtype=jnp.float32)
        W_out = jax.random.normal(ks[2], (D, D), dtype=jnp.float32) * scale
        b_out = jnp.zeros((D,), dtype=jnp.float32)
        return {'x': x, 'W_qkv': W_qkv, 'b_qkv': b_qkv, 'W_out': W_out, 'b_out': b_out}
    _L0_attn_in = _L0_attn_setup()

    def _L0_ffn_setup():
        import jax, jax.numpy as jnp
        import numpy as np
        JITTER_EPS = 0.01

        def phi_routing(logits, jitter_eps=JITTER_EPS):
            m, sel = jax.lax.top_k(logits, 2)
            T, E = logits.shape
            m1 = m[:, :1]
            factor1 = jnp.maximum(jnp.abs(logits), m1)
            mask1 = (m1 - logits) / factor1 > 2.0 * jitter_eps
            p1 = jax.nn.softmax(jnp.where(mask1, -jnp.inf, logits), axis=-1)
            mult1 = jnp.take_along_axis(p1, sel[:, :1], axis=-1)
            m2 = m[:, 1:2]
            factor2 = jnp.maximum(jnp.abs(logits), m2)
            mask2 = (m2 - logits) / factor2 > 2.0 * jitter_eps
            drop_top1 = jnp.arange(E)[None, :] == sel[:, :1]
            p2 = jax.nn.softmax(jnp.where(mask2 | drop_top1, -jnp.inf, logits), axis=-1)
            mult2 = jnp.take_along_axis(p2, sel[:, 1:2], axis=-1)
            return (jnp.concatenate([mult1, mult2], axis=-1), sel)
        key = jax.random.key(seed)
        k = jax.random.split(key, 5)
        B, S, H, F, E = (1, 64, 128, 512, 8)
        return {'hidden_states': jax.random.normal(k[0], (B, S, H), jnp.float32), 'gate_w': jax.random.normal(k[1], (E, H), jnp.float32) * 0.02, 'w1': jax.random.normal(k[2], (E, F, H), jnp.float32) * 0.02, 'w2': jax.random.normal(k[3], (E, H, F), jnp.float32) * 0.02, 'w3': jax.random.normal(k[4], (E, F, H), jnp.float32) * 0.02}
    _L0_ffn_in = _L0_ffn_setup()
    _L0_c = _w((lambda *s: np.random.randn(*s).astype(np.float32) * 0.05)(8, 128))
    _L0_wmod = _w((lambda *s: np.random.randn(*s).astype(np.float32) * 0.05)(128, 6 * 128) * 128 ** (-0.5))
    _d = {'L0_attn_x': _L0_attn_in['x'], 'L0_attn_W_qkv': _L0_attn_in['W_qkv'], 'L0_attn_b_qkv': _L0_attn_in['b_qkv'], 'L0_attn_W_out': _L0_attn_in['W_out'], 'L0_attn_b_out': _L0_attn_in['b_out'], 'L0_ffn_gate_w': _L0_ffn_in['gate_w'], 'L0_ffn_w1': _L0_ffn_in['w1'], 'L0_ffn_w2': _L0_ffn_in['w2'], 'L0_ffn_w3': _L0_ffn_in['w3'], 'L0_c': _L0_c, 'L0_wmod': _L0_wmod}
    _x0 = _d['L0_attn_x']
    _d['L0_attn_x'] = jax.random.normal(jax.random.fold_in(jax.random.key(seed), 1), (8, 512, 128), dtype=_x0.dtype)
    del _x0
    return _d

def reference(L0_attn_x, L0_attn_W_qkv, L0_attn_b_qkv, L0_attn_W_out, L0_attn_b_out, L0_ffn_gate_w, L0_ffn_w1, L0_ffn_w2, L0_ffn_w3, L0_c, L0_wmod):

    def _L0_attn_ref(x, W_qkv, b_qkv, W_out, b_out):
        import jax, jax.numpy as jnp
        import numpy as np
        B, L, D, H = (4, 256, 128, 16)
        DK = D // H
        Bx, Lx, Dx = x.shape
        qkv = x @ W_qkv + b_qkv
        q, k, v = jnp.split(qkv, 3, axis=-1)
        q = q.reshape(Bx, Lx, H, DK).transpose(0, 2, 1, 3)
        k = k.reshape(Bx, Lx, H, DK).transpose(0, 2, 1, 3)
        v = v.reshape(Bx, Lx, H, DK).transpose(0, 2, 1, 3)
        scores = jnp.einsum('bhqd,bhkd->bhqk', q, k) / np.sqrt(DK)
        causal = jnp.tril(jnp.ones((Lx, Lx), dtype=bool))
        scores = jnp.where(causal[None, None], scores, -jnp.inf)
        attn = jax.nn.softmax(scores, axis=-1)
        out = jnp.einsum('bhqk,bhkd->bhqd', attn, v)
        out = out.transpose(0, 2, 1, 3).reshape(Bx, Lx, Dx)
        return out @ W_out + b_out

    def _L0_ffn_ref(hidden_states, gate_w, w1, w2, w3):
        import jax, jax.numpy as jnp
        import numpy as np
        JITTER_EPS = 0.01

        def phi_routing(logits, jitter_eps=JITTER_EPS):
            m, sel = jax.lax.top_k(logits, 2)
            T, E = logits.shape
            m1 = m[:, :1]
            factor1 = jnp.maximum(jnp.abs(logits), m1)
            mask1 = (m1 - logits) / factor1 > 2.0 * jitter_eps
            p1 = jax.nn.softmax(jnp.where(mask1, -jnp.inf, logits), axis=-1)
            mult1 = jnp.take_along_axis(p1, sel[:, :1], axis=-1)
            m2 = m[:, 1:2]
            factor2 = jnp.maximum(jnp.abs(logits), m2)
            mask2 = (m2 - logits) / factor2 > 2.0 * jitter_eps
            drop_top1 = jnp.arange(E)[None, :] == sel[:, :1]
            p2 = jax.nn.softmax(jnp.where(mask2 | drop_top1, -jnp.inf, logits), axis=-1)
            mult2 = jnp.take_along_axis(p2, sel[:, 1:2], axis=-1)
            return (jnp.concatenate([mult1, mult2], axis=-1), sel)
        B, S, H = hidden_states.shape
        E = w1.shape[0]
        x = hidden_states.reshape(-1, H)
        logits = x @ gate_w.T
        routing_weights, selected = phi_routing(logits)
        T = x.shape[0]
        wte = jnp.zeros((T, E), x.dtype).at[jnp.arange(T)[:, None], selected].add(routing_weights)
        out = jnp.zeros_like(x)
        for e in range(E):
            h = jax.nn.silu(x @ w1[e].T) * (x @ w3[e].T)
            out = out + wte[:, e:e + 1] * (h @ w2[e].T)
        return out.reshape(B, S, H)
    x = L0_attn_x
    mod = (_silu(L0_c) @ L0_wmod).reshape(L0_c.shape[0], 6, 1, -1)
    sa, ca, ga, sb, cb, gb = (mod[:, 0], mod[:, 1], mod[:, 2], mod[:, 3], mod[:, 4], mod[:, 5])
    ga = (2 * (ga >= 0) - 1) * jnp.maximum(jnp.abs(ga), 0.25)
    gb = (2 * (gb >= 0) - 1) * jnp.maximum(jnp.abs(gb), 0.25)
    h = _layernorm(x, axis=-1) * (1 + ca) + sa
    x = x + ga * _L0_attn_ref(h, L0_attn_W_qkv, L0_attn_b_qkv, L0_attn_W_out, L0_attn_b_out)
    h = _layernorm(x, axis=-1) * (1 + cb) + sb
    x = x + gb * _L0_ffn_ref(h, L0_ffn_gate_w, L0_ffn_w1, L0_ffn_w2, L0_ffn_w3)
    return x

_drawn_inputs = setup_inputs


def setup_inputs(seed=0):
    import zlib

    import numpy as np

    out = dict(_drawn_inputs(seed))
    spreads = {'L0_attn_b_qkv': (0.0, 0.308), 'L0_attn_b_out': (0.0, 0.341)}
    factors = {'L0_ffn_gate_w': 8.0, 'L0_ffn_w1': 8.0, 'L0_ffn_w2': 8.0, 'L0_ffn_w3': 8.0}
    for name, (base, spread) in spreads.items():
        noise = np.random.default_rng([zlib.crc32(name.encode()), seed]).standard_normal(out[name].shape)
        drawn = base * np.exp(spread * noise) if base else spread * noise
        out[name] = jnp.asarray(drawn.astype(out[name].dtype))
    for name, factor in factors.items():
        out[name] = (out[name] * factor).astype(out[name].dtype)
    return out
```

```python
import concourse.bass as bass
from concourse import mybir
from contextlib import ExitStack

F32 = mybir.dt.float32
F32R = mybir.dt.float32r
BF16 = mybir.dt.bfloat16
ALU = mybir.AluOpType
ACT = mybir.ActivationFunctionType
AX = mybir.AxisListType

NB, L, D = 8, 512, 128
H, DK = 16, 8
T = NB * L
TB = L // 128
NT = T // 128
G, HG = 4, 4
E, FF = 8, 512
FB = FF // 128
EPS = 1e-5
SA, CA, GA, SB_, CB, GB = range(6)
BIG = 1e30
S_ROW = HG * DK


def clamp_gate(nc, dve, step, gate, sign, mag):
    step(nc.vector.tensor_scalar(sign, gate, 0.0, 2.0, ALU.is_ge, ALU.mult))
    step(nc.vector.tensor_scalar(mag, gate, -1.0, None, ALU.mult))
    step(nc.vector.tensor_tensor(mag, mag, gate, ALU.max))
    step(nc.vector.tensor_scalar(mag, mag, 0.25, None, ALU.max))
    step(nc.vector.scalar_tensor_tensor(gate, sign, -1.0, mag, ALU.add, ALU.mult))


def newton_rstd(nc, step, root, var, half):
    step(nc.vector.reciprocal(root, root))
    step(nc.vector.tensor_tensor(half, root, root, ALU.mult))
    step(nc.vector.tensor_tensor(half, half, var, ALU.mult))
    step(nc.vector.tensor_scalar(half, half, -0.5, 1.5, ALU.mult, ALU.add))
    step(nc.vector.tensor_tensor(root, root, half, ALU.mult))


def qkv_phase(nc, io, keep):
    ctx = ExitStack()
    with ctx:
        sb = lambda n, s, d=F32: ctx.enter_context(nc.sbuf_tensor("a_" + n, s, d))
        sem = lambda n: ctx.enter_context(nc.semaphore("a_" + n))
        ps = [ctx.enter_context(nc.psum_tensor(f"a_ps{i}", [128, 512], F32)) for i in range(8)]
        trans_ps, q_ps, k_ps, v_ps = ps[0:2], ps[2:4], ps[4:6], ps[6:8]
        mod, csil, ident = keep["mod"], keep["csil"], keep["ident"]
        q_hi, q_lo, k_hi, k_lo = (keep[n] for n in ("q_hi", "q_lo", "k_hi", "k_lo"))
        q_bf, k_bf, v_all = keep["q_bf"], keep["k_bf"], keep["v_all"]
        x = sb("x", [128, NT, D])
        norm = sb("norm", [128, 2, TB, D])
        stats = sb("stats", [128, TB, 6])
        mean_var = sb("mean_var", [128, NT, 2])
        var, root, half = sb("var", [128, NT]), sb("root", [128, NT]), sb("half", [128, NT])
        hT = sb("hT", [128, 2, L])
        wqkv, wmod = sb("wqkv", [128, 3 * D]), sb("wmod", [128, 6 * D])
        c_T = sb("c_T", [128, NB])
        bias_qk, bias_v = sb("bias_qk", [128, 2]), sb("bias_v", [128, D])
        sign, mag = sb("sign", [128, NB]), sb("mag", [128, NB])

        x_in = [sem(f"x_in{b}") for b in range(2)]
        w_in, c_in = sem("w_in"), sem("c_in")
        silu_done, mod_done, mod_copied = sem("silu_done"), sem("mod_done"), sem("mod_copied")
        chain = sem("dve_chain")
        stats_done, root_done, norm_done = sem("stats_done"), sem("root_done"), sem("norm_done")
        trans_done, hT_done = sem("trans_done"), sem("hT_done")
        q_done, k_done, v_done = sem("q_done"), sem("k_done"), sem("v_done")
        hi_done, lo_done = sem("hi_done"), sem("lo_done")
        set_in, zeroed = sem("set_in"), sem("zeroed")
        one_rows = sb("one_rows", [128, 1])
        block = ctx.enter_context(nc.Block())

        @block.gpsimd
        def _(pool):
            v_aug = keep["v_aug"]
            pool.dma_start(keep["head_mask"][:], io["head_mask"]).then_inc(set_in, 16)
            pool.dma_start(one_rows[:], io["one_rows"]).then_inc(set_in, 16)
            nc.gpsimd.memset(keep["q_own"][:].bitcast(F32), 0.0)
            nc.gpsimd.memset(keep["q_pack"][:].bitcast(F32), 0.0)
            for part, value in ((slice(0, DK), 0.0), (slice(DK, 2 * DK), 1.0), (slice(2 * DK, 32), 0.0)):
                nc.gpsimd.memset(v_aug[:, :, :, :, part].rearrange("p a t j d -> p (a t j) d"), value)
            nc.gpsimd.memset(keep["k_pack"][:], 0.0).then_inc(zeroed, 1)
            pool.wait_ge(set_in, 32)
            pool.wait_ge(zeroed, 1)
            nc.gpsimd.tensor_scalar(keep["k_pack"][:].rearrange("p a n -> p (a n)"),
                                    keep["k_pack"][:].rearrange("p a n -> p (a n)"), one_rows[:], None, ALU.add)

        @block.sync
        def _(sp):
            sp.dma_start(c_T[:], io["c_T"]).then_inc(c_in, 16)
            sp.dma_start(wmod[:], io["wmod"]).then_inc(c_in, 16)
            for half_ in range(2):
                for b in range(4 * half_, 4 * half_ + 4):
                    sp.dma_start(x[:, TB * b:TB * b + TB, :], io["x"][:, TB * b:TB * b + TB, :]).then_inc(x_in[half_], 16)
            sp.wait_ge(x_in[1], 64)

        @block.scalar
        def _(act):
            act.dma_start(wqkv[:], io["wqkv"]).then_inc(w_in, 16)
            act.dma_start(bias_qk[:], io["bias_qk"]).then_inc(w_in, 16)
            act.dma_start(bias_v[:], io["bias_v"].partition_broadcast(128)).then_inc(w_in, 16)
            act.dma_start(ident[:], io["ident"]).then_inc(w_in, 16)
            act.wait_ge(c_in, 32)
            nc.scalar.activation(csil[:], c_T[:], ACT.Silu).then_inc(silu_done, 1)
            act.wait_ge(stats_done, 1)
            nc.scalar.activation(root[:], var[:], ACT.Sqrt).then_inc(root_done, 1)
            act.wait_ge(mod_copied, 1)
            act.wait_ge(w_in, 64)

            def batch(b, par, first):
                act.wait_ge(trans_done, b + 1)
                if not first:
                    act.wait_ge(v_done, b - 1)
                nc.scalar.activation(hT[:, par, :], trans_ps[par][:], ACT.Identity,
                                     bias=mod[:, SA, bass.ds(b, 1)], scale=mod[:, CA, bass.ds(b, 1)]).then_inc(hT_done, 1)
                cols = bass.ds(b * L, L)
                act.wait_ge(q_done, b + 1)
                nc.scalar.activation(q_hi[:, cols].bitcast(F32R), q_ps[par][:], ACT.Identity,
                                     bias=bias_qk[:, 0:1]).then_inc(hi_done, 1)
                act.wait_ge(k_done, b + 1)
                nc.scalar.activation(k_hi[:, cols].bitcast(F32R), k_ps[par][:], ACT.Identity,
                                     bias=bias_qk[:, 1:2]).then_inc(hi_done, 1)

            batch(0, 0, True)
            batch(1, 1, True)
            with act.Fori(1, NB // 2) as pair:
                for par in range(2):
                    batch(pair * 2 + par, par, False)

        @block.vector
        def _(dve):
            n = [0]

            def step(ins):
                n[0] += 1
                ins.then_inc(chain, 1)
                dve.wait_ge(chain, n[0])

            for b in range(NB):
                dve.wait_ge(x_in[b // 4], 64)
                for t in range(TB):
                    last = nc.vector.bn_stats(stats[:, t, :], x[:, TB * b + t, :])
                step(last)
                for t in range(TB):
                    last = nc.vector.bn_aggr(mean_var[:, TB * b + t, :], stats[:, t, :])
                step(last)
            step(nc.vector.tensor_scalar(var[:], mean_var[:, :, 1], EPS, None, ALU.add))
            nc.vector.engine_nop().then_inc(stats_done, 1)
            dve.wait_ge(mod_done, 1)
            step(nc.vector.tensor_copy(mod[:].rearrange("p a b -> p (a b)"), ps[7][:, 0:6 * NB]))
            step(nc.vector.tensor_scalar(mod[:, CA, :], mod[:, CA, :], 1.0, None, ALU.add))
            step(nc.vector.tensor_scalar(mod[:, CB, :], mod[:, CB, :], 1.0, None, ALU.add))
            clamp_gate(nc, dve, step, mod[:, GB, :], sign[:], mag[:])
            nc.vector.engine_nop().then_inc(mod_copied, 1)
            dve.wait_ge(root_done, 1)
            newton_rstd(nc, step, root[:], var[:], half[:])
            dve.wait_ge(w_in, 64)

            def normalize(b, par):
                for t in range(TB):
                    tile = bass.ds(b * TB + t, 1)
                    last = nc.vector.tensor_scalar(norm[:, par, t, :], x[:, tile, :].rearrange("p a c -> p (a c)"),
                                                   mean_var[:, tile, 0], root[:, tile], ALU.subtract, ALU.mult)
                last.then_inc(norm_done, 1)

            def batch(b, par):
                cols = bass.ds(b * L, L)
                dve.wait_ge(hi_done, 2 * b + 1)
                nc.vector.scalar_tensor_tensor(q_lo[:, cols].bitcast(F32R), q_ps[par][:], bias_qk[:, 0:1],
                                               q_hi[:, cols], ALU.add, ALU.subtract)
                nc.vector.tensor_copy(q_bf[:, cols], q_hi[:, cols])
                dve.wait_ge(hi_done, 2 * b + 2)
                nc.vector.scalar_tensor_tensor(k_lo[:, cols].bitcast(F32R), k_ps[par][:], bias_qk[:, 1:2],
                                               k_hi[:, cols], ALU.add, ALU.subtract)
                nc.vector.tensor_copy(k_bf[:, cols], k_hi[:, cols])
                dve.wait_ge(v_done, b + 1)
                nc.vector.tensor_tensor(v_all[:, bass.ds(b * TB, TB), :],
                                        v_ps[par][:].rearrange("p (t c) -> p t c", c=D),
                                        bias_v[:, None, :].broadcast_to([128, TB, D]), ALU.add).then_inc(lo_done, 1)

            for par in range(2):
                normalize(par, par)
            with dve.Fori(0, NB // 2 - 1) as pair:
                for par in range(2):
                    dve.wait_ge(trans_done, pair * 2 + par + 1)
                    normalize(pair * 2 + 2 + par, par)
                for par in range(2):
                    batch(pair * 2 + par, par)
            for par in range(2):
                batch(NB - 2 + par, par)

        @block.tensor
        def _(pe):
            pe.wait_ge(silu_done, 1)
            for part in range(6):
                last = nc.tensor.matmul(ps[7][:, part * NB:(part + 1) * NB], wmod[:, part * D:(part + 1) * D],
                                        csil[:], start=True, stop=True)
            last.then_inc(mod_done, 1)
            pe.wait_ge(w_in, 64)
            pe.wait_ge(mod_copied, 1)

            def transpose_batch(b, par, first):
                pe.wait_ge(norm_done, b + 1)
                if not first:
                    pe.wait_ge(hT_done, b - 1)
                for t in range(TB):
                    last = nc.tensor.transpose(trans_ps[par][:, t * 128:(t + 1) * 128],
                                               norm[:, par, t, :], ident[:])
                last.then_inc(trans_done, 1)

            def project_batch(b, par, first):
                pe.wait_ge(hT_done, b + 1)
                if not first:
                    pe.wait_ge(lo_done, b - 1)
                nc.tensor.matmul(q_ps[par][:], wqkv[:, 0:D], hT[:, par, :], start=True, stop=True).then_inc(q_done, 1)
                nc.tensor.matmul(k_ps[par][:], wqkv[:, D:2 * D], hT[:, par, :], start=True, stop=True).then_inc(k_done, 1)
                for t in range(TB):
                    last = nc.tensor.matmul(v_ps[par][:, t * D:(t + 1) * D], hT[:, par, t * 128:(t + 1) * 128],
                                            wqkv[:, 2 * D:3 * D], start=True, stop=True)
                last.then_inc(v_done, 1)

            for first in (True,):
                transpose_batch(0, 0, first)
                transpose_batch(1, 1, first)
                project_batch(0, 0, first)
                project_batch(1, 1, first)
            with pe.Fori(1, NB // 2) as pair:
                for par in range(2):
                    transpose_batch(pair * 2 + par, par, False)
                for par in range(2):
                    project_batch(pair * 2 + par, par, False)


FILLS = [f for a in (0, 2) for f in (
    [(a, 3, 0)], [(a, 2, 0), (a, 0, 384)],
    [(a + 1, 3, 0)], [(a + 1, 2, 0), (a + 1, 0, 384)],
    [(a, 1, 0), (a + 1, 1, 256)])]
NF = len(FILLS)
KEY_COLS = {0: (0, 512), 1: (512, 384), 3: (896, 128)}
PAIR = 2560


def attention_phase(nc, io, keep):
    ctx = ExitStack()
    with ctx:
        sb = lambda n, s, d=F32: ctx.enter_context(nc.sbuf_tensor("b_" + n, s, d))
        sem = lambda n: ctx.enter_context(nc.semaphore("b_" + n))
        pb = lambda n, w: ctx.enter_context(nc.psum_tensor("b_" + n, [128, w], F32))
        q_hi, q_lo, k_hi, k_lo = (keep[n] for n in ("q_hi", "q_lo", "k_hi", "k_lo"))
        q_bf, k_bf, v_all, ident = keep["q_bf"], keep["k_bf"], keep["v_all"], keep["ident"]
        q_own, q_pack, k_pack, v_aug = keep["q_own"], keep["q_pack"], keep["k_pack"], keep["v_aug"]
        head_mask, sums = keep["head_mask"], io["sums"]
        k_own = sb("k_own", [128, 2, HG, L], F32R)
        probs = sb("probs", [128, 2, 2, PAIR])
        out_T = sb("out_T", [128, 2, L])
        neg_max = sb("neg_max", [HG, 2, L])
        row_max = sb("row_max", [128, 2, TB, HG])
        above_f = sb("above_f", [128, 128])
        ident_bf, above = sb("ident_bf", [128, 128], BF16), sb("above", [128, 128], BF16)
        ab_ps, c_ps, o_ps = pb("ab_ps", 2048), pb("c_ps", 512), pb("o_ps", 512)
        max_ps = [pb("max_ps0", 512), pb("max_ps1", 512)]

        const_in, const_cast, waited = sem("const_in"), sem("const_cast"), sem("waited")
        k_in = [sem(f"k_in{i}") for i in range(2)]
        q_in = [sem(f"q_in{i}") for i in range(2)]
        sums_out = [sem(f"sums_out{i}") for i in range(2)]
        q_own_done, fill_done, red_done = sem("q_own_done"), sem("fill_done"), sem("red_done")
        max_T_done, neg_done = sem("max_T_done"), sem("neg_done")
        own_pool, own_act = sem("own_pool"), sem("own_act")
        ab_done, c_done, exp_ab, exp_c = sem("ab_done"), sem("c_done"), sem("exp_ab"), sem("exp_c")
        masked, v_done, pv_done, o_copied = sem("masked"), sem("v_done"), sem("pv_done"), sem("o_copied")
        block = ctx.enter_context(nc.Block())

        U = NB * G
        PRO_FILLS = 2 * NF

        def batches(eng, slot):
            for g in range(G):
                slot(0, g, g)
            with eng.Fori(1, NB - 1) as b:
                for g in range(G):
                    slot(b, g, b * G + g)
            for g in range(G):
                slot(NB - 1, g, (NB - 1) * G + g)

        def ahead(u, n):
            return not isinstance(u, int) or u + n < U

        def first(u, n):
            return isinstance(u, int) and u < n

        def where(b, g, n):
            return b + (g + n) // G, (g + n) % G

        def uses(b, g):
            return b * 2 + g // 2 + 1

        def bank_of_fill(v, par, f):
            if isinstance(v, int) and v < 2:
                return (v * (NF + 1) + f) % 2
            return (PRO_FILLS + 1 + par * (NF + 1) + 1 + f) % 2

        def bank_of_transpose(par):
            return (PRO_FILLS + 1 + par * (NF + 1)) % 2

        @block.sync
        def _(sp):
            sp.dma_start(above_f[:], io["above"]).then_inc(const_in, 16)

            def load(b, g):
                par, src, cols = g % 2, slice(S_ROW * g, S_ROW * (g + 1)), bass.ds(b * L, L)
                for slot, piece in ((1, k_hi), (2, k_lo), (3, k_hi)):
                    sp.dma_start(k_pack[S_ROW * slot:S_ROW * (slot + 1), par, :], piece[src, cols]).then_inc(k_in[par], 16)
                for slot, piece in ((1, q_hi), (2, q_hi), (3, q_lo)):
                    sp.dma_start(q_pack[S_ROW * slot:S_ROW * (slot + 1), par, :].bitcast(F32), piece[src, cols])\
                        .then_inc(q_in[par], 16)

            def load_max(g):
                sp.dma_start(q_pack[0:S_ROW:DK, g % 2, :].bitcast(F32), neg_max[:, g % 2, :]).then_inc(q_in[g % 2], 16)

            def send_sums(b, g, u):
                sp.dma_start(sums[bass.ds(u * 128, 128), :], out_T[:, g % 2, :]).then_inc(sums_out[g % 2], 16)

            load(0, 0)
            sp.wait_ge(neg_done, 1)
            load_max(0)

            def slot(b, g, u):
                if ahead(u, 1):
                    if not first(u, 1):
                        sp.wait_ge(c_done, u * 2)
                    load(*where(b, g, 1))
                    sp.wait_ge(neg_done, u + 2)
                    load_max((g + 1) % G)
                if not first(u, 1):
                    sp.wait_ge(o_copied, u)
                    send_sums(*where(b, g, -1), u - 1)

            batches(sp, slot)
            sp.wait_ge(o_copied, U)
            send_sums(NB - 1, G - 1, U - 1)
            for par in range(2):
                sp.wait_ge(sums_out[par], 16 * (U // 2))

        @block.vector
        def _(dve):
            def own_queries(b, g):
                rows = slice(S_ROW * g, S_ROW * (g + 1))
                for j in range(HG):
                    nc.vector.tensor_scalar(q_own[rows, g, j, :], q_bf[rows, bass.ds(b * L, L)],
                                            head_mask[rows, j:j + 1], None, ALU.mult).then_inc(q_own_done, 1)

            def maxima(v, par):
                for f, parts in enumerate(FILLS):
                    dve.wait_ge(fill_done, v * NF + f + 1)
                    bank = max_ps[bank_of_fill(v, par, f)]
                    if len(parts) == 2 and parts[1][1] == 1:
                        last = nc.vector.reduce_max(row_max[:, par, 1, parts[0][0]:parts[0][0] + 2],
                                                    bank[:].rearrange("p (j n) -> p j n", j=2), AX.X)
                    else:
                        for j, i, c in parts:
                            last = nc.vector.reduce_max(row_max[:, par, i, j:j + 1],
                                                        bank[:, c:c + 128 * (i + 1)], AX.X)
                    last.then_inc(red_done, 1)

            nc.vector.tensor_copy(ident_bf[:], ident[:]).then_inc(const_cast, 1)
            dve.wait_ge(const_in, 16)
            nc.vector.tensor_copy(above[:], above_f[:]).then_inc(const_cast, 1)
            for u in range(3):
                own_queries(0, u)
            maxima(0, 0)
            maxima(1, 1)

            def slot(b, g, u):
                if ahead(u, 3):
                    own_queries(*where(b, g, 3))
                if ahead(u, 2):
                    dve.wait_ge(max_T_done, u + 1)
                    maxima(u + 2, g % 2)

            batches(dve, slot)

        @block.tensor
        def _(pe):
            pe.wait_ge(const_cast, 2)

            def fill(bv, gv, v, f):
                if f == 0:
                    pe.wait_ge(q_own_done, v * HG + HG)
                if not (isinstance(v, int) and v == 0 and f < 2) and not (f == 0):
                    pe.wait_ge(red_done, v * NF + f - 1)
                if f == 1 and not (isinstance(v, int) and v == 0):
                    pe.wait_ge(neg_done, v)
                bank = max_ps[bank_of_fill(v, gv % 2, f)]
                for j, i, c in FILLS[f]:
                    nc.tensor.matmul(bank[:, c:c + 128 * (i + 1)], q_own[:, gv, j, i * 128:(i + 1) * 128],
                                     k_bf[:, bass.ds(bv * L, 128 * (i + 1))], start=True, stop=False)
                    last = nc.tensor.matmul(bank[:, c + 128 * i:c + 128 * (i + 1)], ident_bf[:], above[:],
                                            start=False, stop=True)
                last.then_inc(fill_done, 1)

            def transpose_max(v, par, bank):
                pe.wait_ge(red_done, v * NF + NF)
                for i in range(TB):
                    last = nc.tensor.transpose(max_ps[bank][0:HG, i * 128:(i + 1) * 128], row_max[:, par, i, :], ident[:])
                last.then_inc(max_T_done, 1)

            def scores(b, g, u, j):
                par, pair = g % 2, u * 2 + j // 2
                if j == 0:
                    pe.wait_ge(q_in[par], uses(b, g) * 64)
                    pe.wait_ge(own_pool, u * 2 + 2)
                if j == 2:
                    pe.wait_ge(own_act, u * 2 + 2)
                if not (first(u, 1) and j < 2):
                    pe.wait_ge(exp_ab, u * HG + j - 1)
                for kt, (c, n) in KEY_COLS.items():
                    at = 1024 * (j % 2) + c
                    last = nc.tensor.matmul(ab_ps[:, at:at + n], k_own[:, par, j, kt * 128:(kt + 1) * 128],
                                            q_pack[:, par, L - n:L], start=True, stop=True)
                last.then_inc(ab_done, 1)
                if j % 2 == 0 and not (first(u, 1) and j == 0):
                    pe.wait_ge(exp_c, pair)
                last = nc.tensor.matmul(c_ps[:, 256 * (j % 2):256 * (j % 2) + 256], k_own[:, par, j, 256:384],
                                        q_pack[:, par, 256:512], start=True, stop=True)
                if j % 2:
                    last.then_inc(c_done, 1)

            def weigh(u, par, kt):
                if kt == 0:
                    pe.wait_ge(masked, u * 10 + 10)
                    pe.wait_ge(v_done, u + 1)
                    if not first(u, 1):
                        pe.wait_ge(o_copied, u)
                for j in range(HG):
                    if kt == 2:
                        c, n = 2048 + 256 * (j % 2), 256
                    else:
                        c, n = KEY_COLS[kt][0] + 1024 * (j % 2), KEY_COLS[kt][1]
                    last = nc.tensor.matmul(o_ps[32 * j:32 * j + 32, L - n:L], v_aug[:, par, kt, j, :],
                                            probs[:, par, j // 2, c:c + n], start=(kt == 0), stop=(kt == TB - 1))
                if kt == TB - 1:
                    last.then_inc(pv_done, 1)

            for f in range(NF):
                fill(0, 0, 0, f)
            transpose_max(0, 0, NF % 2)
            for f in range(NF):
                fill(0, 1, 1, f)

            def slot(b, g, u):
                par = g % 2
                fills = list(range(NF)) if ahead(u, 2) else []

                def next_fill():
                    if fills:
                        fill(*where(b, g, 2), u + 2, fills.pop(0))

                scores(b, g, u, 0)
                if ahead(u, 1):
                    transpose_max(u + 1, 1 - par, bank_of_transpose(par))
                scores(b, g, u, 1)
                next_fill()
                for kt in range(TB):
                    if not first(u, 1):
                        weigh(u - 1, 1 - par, kt)
                    if kt != 2:
                        next_fill()
                scores(b, g, u, 2)
                next_fill()
                scores(b, g, u, 3)
                while fills:
                    next_fill()

            batches(pe, slot)
            for kt in range(TB):
                weigh(U - 1, 1, kt)

        @block.scalar
        def _(act):
            scale = DK ** -0.5

            def negate_max(v, par, bank):
                act.wait_ge(max_T_done, v + 1)
                nc.scalar.activation(neg_max[:, par, :].bitcast(F32R), max_ps[bank][0:HG, :], ACT.Copy,
                                     scale=-1.0).then_inc(neg_done, 1)

            def own_keys(b, g, u):
                act.wait_ge(k_in[g % 2], uses(b, g) * 48)
                for j in (2, 3):
                    nc.scalar.activation(k_own[:, g % 2, j, :], k_pack[:, g % 2, :], ACT.Copy,
                                         scale=head_mask[:, j:j + 1]).then_inc(own_act, 1)

            def augment(b, g, u):
                if not first(u, 2):
                    act.wait_ge(pv_done, u - 1)
                nc.scalar.activation(v_aug[:, g % 2, :, :, 0:DK],
                                     v_all[:, bass.ds(b * TB, TB), S_ROW * g:S_ROW * (g + 1)]
                                     .rearrange("p t (j d) -> p t j d", d=DK), ACT.Copy).then_inc(v_done, 1)

            def exps(b, g, u, pair):
                par = g % 2
                if pair == 0 and not first(u, 2):
                    act.wait_ge(pv_done, u - 1)
                for j in (0, 1):
                    act.wait_ge(ab_done, u * HG + 2 * pair + j + 1)
                    nc.scalar.activation(probs[:, par, pair, 1024 * j:1024 * (j + 1)], ab_ps[:, 1024 * j:1024 * (j + 1)],
                                         ACT.Exp, scale=scale).then_inc(exp_ab, 1)
                act.wait_ge(c_done, u * 2 + pair + 1)
                nc.scalar.activation(probs[:, par, pair, 2048:PAIR], c_ps[:], ACT.Exp, scale=scale).then_inc(exp_c, 1)

            def copy_sums(b, g, u):
                act.wait_ge(pv_done, u + 1)
                if not first(u, 2):
                    act.wait_ge(sums_out[g % 2], uses(b, g) * 16 - 16)
                nc.scalar.activation(out_T[:, g % 2, :], o_ps[:], ACT.Copy).then_inc(o_copied, 1)

            negate_max(0, 0, NF % 2)
            own_keys(0, 0, 0)

            def slot(b, g, u):
                if ahead(u, 1):
                    negate_max(u + 1, 1 - g % 2, bank_of_transpose(g % 2))
                exps(b, g, u, 0)
                if ahead(u, 1):
                    if not first(u, 1):
                        act.wait_ge(c_done, u * 2)
                    own_keys(*where(b, g, 1), u + 1)
                if not first(u, 1):
                    copy_sums(*where(b, g, -1), u - 1)
                exps(b, g, u, 1)
                augment(b, g, u)

            batches(act, slot)
            copy_sums(NB - 1, G - 1, U - 1)

        @block.gpsimd
        def _(pool):
            def own_keys(b, g):
                pool.wait_ge(k_in[g % 2], uses(b, g) * 48)
                for j in (0, 1):
                    nc.gpsimd.tensor_tensor(k_own[:, g % 2, j, :], k_pack[:, g % 2, :],
                                            head_mask[:, j:j + 1].broadcast_to([128, L]), ALU.mult).then_inc(own_pool, 1)

            def causal(p, n):
                pattern = [[0, n], [1, 128]] if n > 1 else [[1, 128]]
                nc.gpsimd.affine_select(out=p, in_=p, pattern=pattern, compare_op=ALU.is_ge, fill=0.0, base=0,
                                        channel_multiplier=-1).then_inc(masked, 1)

            def mask(b, g, u, pair):
                for j in (0, 1):
                    p = probs[:, g % 2, pair, 1024 * j:1024 * (j + 1)]
                    pool.wait_ge(exp_ab, u * HG + 2 * pair + j + 1)
                    pool.sem_inc(waited, 1)
                    causal(p.rearrange("p (s n) -> p s n", s=2)[:, :, 0:128], 2)
                    causal(p[:, 896:1024], 1)
                pool.wait_ge(exp_c, u * 2 + pair + 1)
                pool.sem_inc(waited, 1)
                causal(probs[:, g % 2, pair, 2048:PAIR].rearrange("p (s n) -> p s n", s=2)[:, :, 0:128], 2)

            own_keys(0, 0)

            def slot(b, g, u):
                mask(b, g, u, 0)
                if ahead(u, 1):
                    if not first(u, 1):
                        pool.wait_ge(c_done, u * 2)
                    own_keys(*where(b, g, 1))
                mask(b, g, u, 1)

            batches(pool, slot)



def route_phase(nc, io, keep):
    ctx = ExitStack()
    with ctx:
        sb = lambda n, s, d=F32: ctx.enter_context(nc.sbuf_tensor("c_" + n, s, d))
        sem = lambda n: ctx.enter_context(nc.semaphore("c_" + n))
        ps = [ctx.enter_context(nc.psum_tensor(f"c_ps{i}", [128, 512], F32)) for i in range(8)]
        proj_ps, trans_ps, gate_ps, misc_ps = ps[0:2], ps[2:4], ps[4:6], ps[6:8]
        mod, csil, ident, x1, h_hi, h_lo = (keep[n] for n in ("mod", "csil", "ident", "x1", "h_hi", "h_lo"))
        x = sb("x", [128, NT, D])
        pv, recip = sb("pv", [128, T]), sb("recip", [128, T])
        den = sb("den", [128, L])
        attn = sb("attn", [128, 2, L])
        wmod_ga, wout, gate_w = sb("wmod_ga", [128, D]), sb("wout", [128, D]), sb("gate_w", [128, E])
        bias_out = sb("bias_out", [128, D])
        ga, ga_bias = sb("ga", [128, NB, D]), sb("ga_bias", [128, NB, D])
        sign, mag = sb("sign", [128, NB * D]), sb("mag", [128, NB * D])
        x_bias, scaled = sb("x_bias", [128, 2, TB, D]), sb("scaled", [128, 2, TB, D])
        stats, mean_var = sb("stats", [128, 2, TB, 6]), sb("mean_var", [128, NT, 2])
        tile_mean_var = sb("tile_mean_var", [128, 2, TB, 2])
        var, root, half = sb("var", [128, NT]), sb("root", [128, NT]), sb("half", [128, NT])
        norm, h = sb("norm", [128, 2, TB, D]), sb("h", [128, 2, L])
        logits = sb("logits", [128, NT, E])
        rank = sb("rank", [128, NT, E])
        top = [sb(f"top{i}", [128, NT]) for i in range(2)]
        one_hot = [sb(f"one_hot{i}", [128, NT, E]) for i in range(2)]
        diff = [sb(f"diff{i}", [128, NT, E]) for i in range(2)]
        expd = [sb(f"expd{i}", [128, NT, E]) for i in range(2)]
        tmp, tmp2, pick = sb("tmp", [128, NT, E]), sb("tmp2", [128, NT, E]), sb("pick", [128, NT])
        weights, weights_T = sb("weights", [128, NT, E]), sb("weights_T", [128, 2, 128])

        w_in, x_in, den_in, recip_out = sem("w_in"), sem("x_in"), sem("den_in"), sem("recip_out")
        pv_in, recip_in, den_done = sem("pv_in"), sem("recip_in"), sem("den_done")
        ga_ps_done, ga_done, x_bias_done = sem("ga_ps_done"), sem("ga_done"), sem("x_bias_done")
        attn_done, proj_done, x1_done = sem("attn_done"), sem("proj_done"), sem("x1_done")
        stats_done = sem("stats_done")
        chain, var_done, root_done = sem("dve_chain"), sem("var_done"), sem("root_done")
        norm_done, trans_done, h_done, h_hi_done = sem("norm_done"), sem("trans_done"), sem("h_done"), sem("h_hi_done")
        h_lo_done, gate_done, logits_done = sem("h_lo_done"), sem("gate_done"), sem("logits_done")
        diff_done, exp_done, weights_done = sem("diff_done"), sem("exp_done"), sem("weights_done")
        wT_done, wT_copied, wT_out = sem("wT_done"), sem("wT_copied"), sem("wT_out")
        block = ctx.enter_context(nc.Block())
        sums, recips, routes = io["sums"], io["recips"], io["routes"]

        @block.sync
        def _(sp):
            heads = sums.rearrange("(h r) n -> h r n", r=32)
            sp.dma_start(den[:], heads[:, DK, :]).then_inc(den_in, 16)
            for b in range(NB):
                sp.dma_start(x[:, TB * b:TB * (b + 1), :], io["x"][:, TB * b:TB * (b + 1), :]).then_inc(x_in, 16)
                sp.dma_start(pv[:, L * b:L * (b + 1)], heads[H * b:H * (b + 1), 0:DK, :]).then_inc(pv_in, 16)
            sp.wait_ge(den_done, 1)
            sp.dma_start(recips, den[:]).then_inc(recip_out, 16)
            sp.wait_ge(recip_out, 16)
            for b in range(NB):
                sp.dma_start(recip[:, L * b:L * (b + 1)],
                             recips[H * b:H * (b + 1), None, :].broadcast_to([H, DK, L])).then_inc(recip_in, 16)
            for half_ in range(2):
                sp.wait_ge(wT_copied, half_ + 1)
                tiles = slice(NT // 2 * half_, NT // 2 * (half_ + 1))
                sp.dma_start(routes.rearrange("e (t p) -> t e p", p=128)[tiles, :, :], weights_T[:, half_, :]).then_inc(wT_out, 16)
            sp.wait_ge(wT_out, 32)

        @block.scalar
        def _(act):
            for dst, name in ((wmod_ga[:], "wmod_ga"), (wout[:], "wout"), (gate_w[:], "gate_T")):
                act.dma_start(dst, io[name]).then_inc(w_in, 16)
            act.dma_start(bias_out[:], io["bias_out"].partition_broadcast(128)).then_inc(w_in, 16)
            act.dma_start(rank[:].rearrange("p t e -> p (t e)"), io["rank"]).then_inc(w_in, 16)
            act.wait_ge(var_done, 1)
            nc.scalar.activation(root[:], var[:], ACT.Sqrt).then_inc(root_done, 1)

            def batch(b, par, first):
                act.wait_ge(trans_done, b + 1)
                if not first:
                    act.wait_ge(h_lo_done, b - 1)
                    act.wait_ge(gate_done, b - 1)
                affine = dict(bias=mod[:, SB_, bass.ds(b, 1)], scale=mod[:, CB, bass.ds(b, 1)])
                nc.scalar.activation(h[:, par, :], trans_ps[par][:], ACT.Identity, **affine).then_inc(h_done, 1)
                nc.scalar.activation(h_hi[:, bass.ds(b * L, L)], trans_ps[par][:], ACT.Identity, **affine).then_inc(h_hi_done, 1)

            batch(0, 0, True)
            batch(1, 1, True)
            with act.Fori(1, NB // 2) as pair:
                for par in range(2):
                    batch(pair * 2 + par, par, False)
            for i in range(2):
                act.wait_ge(diff_done, i + 1)
                nc.scalar.activation(expd[i][:], diff[i][:], ACT.Exp).then_inc(exp_done, 1)

        @block.gpsimd
        def _(pool):
            pool.wait_ge(ga_done, 1)
            pool.wait_ge(x_in, 16 * NB)

            def add_bias(b, par, first):
                if not first:
                    pool.wait_ge(x1_done, b - 1)
                nc.gpsimd.tensor_tensor(x_bias[:, par, :, :], x[:, bass.ds(b * TB, TB), :],
                                        ga_bias[:, bass.ds(b, 1), :].broadcast_to([128, TB, D]), ALU.add).then_inc(x_bias_done, 1)

            add_bias(0, 0, True)
            add_bias(1, 1, True)
            with pool.Fori(1, NB // 2) as pair:
                for par in range(2):
                    add_bias(pair * 2 + par, par, False)

            def low_part(b, par):
                pool.wait_ge(h_hi_done, b + 1)
                cols = bass.ds(b * L, L)
                nc.gpsimd.tensor_tensor(h_lo[:, cols], h[:, par, :], h_hi[:, cols].bitcast(F32), ALU.subtract).then_inc(h_lo_done, 1)

            with pool.Fori(0, NB // 2) as pair:
                for par in range(2):
                    low_part(pair * 2 + par, par)

        @block.tensor
        def _(pe):
            pe.wait_ge(w_in, 80)
            for b in range(NB):
                last = nc.tensor.matmul(misc_ps[b // 4][:, b % 4 * D:(b % 4 + 1) * D], csil[:, b:b + 1].broadcast_to([128, 128]),
                                        wmod_ga[:], start=True, stop=True)
            last.then_inc(ga_ps_done, 1)

            def project(b, par, first):
                pe.wait_ge(attn_done, b + 1)
                if not first:
                    pe.wait_ge(x1_done, b - 1)
                for t in range(TB):
                    last = nc.tensor.matmul(proj_ps[par][:, t * D:(t + 1) * D], attn[:, par, t * 128:(t + 1) * 128], wout[:],
                                            start=True, stop=True)
                last.then_inc(proj_done, 1)

            def transpose_batch(b, par, first):
                pe.wait_ge(norm_done, b + 1)
                if not first:
                    pe.wait_ge(h_hi_done, b - 1)
                for t in range(TB):
                    last = nc.tensor.transpose(trans_ps[par][:, t * 128:(t + 1) * 128], norm[:, par, t, :], ident[:])
                last.then_inc(trans_done, 1)

            def gate(b, par, first):
                pe.wait_ge(h_done, b + 1)
                if not first:
                    pe.wait_ge(logits_done, b - 1)
                for t in range(TB):
                    last = nc.tensor.matmul(gate_ps[par][:, t * E:(t + 1) * E], h[:, par, t * 128:(t + 1) * 128], gate_w[:],
                                            start=True, stop=True)
                last.then_inc(gate_done, 1)

            def pairs(stages):
                for stage in stages:
                    for par in range(2):
                        stage(par, par, True)
                with pe.Fori(1, NB // 2) as pair:
                    for stage in stages:
                        for par in range(2):
                            stage(pair * 2 + par, par, False)

            pairs([project])
            pairs([transpose_batch, gate])
            pe.wait_ge(weights_done, 1)
            for i in range(2):
                nc.tensor.transpose(misc_ps[i][:, 0:128], weights[:, NT // 2 * i:NT // 2 * (i + 1), :]
                                    .rearrange("p t e -> p (t e)"), ident[:]).then_inc(wT_done, 1)

        @block.vector
        def _(dve):
            n = [0]

            def step(ins):
                n[0] += 1
                ins.then_inc(chain, 1)
                dve.wait_ge(chain, n[0])

            ga_flat = ga[:].rearrange("p b c -> p (b c)")
            dve.wait_ge(ga_ps_done, 1)
            for i in range(2):
                last = nc.vector.tensor_copy(ga_flat[:, 512 * i:512 * (i + 1)], misc_ps[i][:])
            step(last)
            clamp_gate(nc, dve, step, ga_flat, sign[:], mag[:])
            dve.wait_ge(w_in, 80)
            nc.vector.tensor_tensor(ga_bias[:], ga[:], bias_out[:, None, :].broadcast_to([128, NB, D]), ALU.mult).then_inc(ga_done, 1)
            dve.wait_ge(den_in, 16)
            nc.vector.reciprocal(den[:], den[:]).then_inc(den_done, 1)
            dve.wait_ge(pv_in, 16 * NB)
            dve.wait_ge(recip_in, 16 * NB)

            def normalize_attention(b, par, first):
                cols = bass.ds(b * L, L)
                if not first:
                    dve.wait_ge(proj_done, b - 1)
                nc.vector.tensor_tensor(attn[:, par, :], pv[:, cols], recip[:, cols], ALU.mult).then_inc(attn_done, 1)

            def residual(b, par, step):
                tiles = bass.ds(b * TB, TB)
                dve.wait_ge(proj_done, b + 1)
                step(nc.vector.tensor_tensor(scaled[:, par, :, :], proj_ps[par][:].rearrange("p (t c) -> p t c", c=D),
                                             ga[:, bass.ds(b, 1), :].broadcast_to([128, TB, D]), ALU.mult))
                dve.wait_ge(x_bias_done, b + 1)
                nc.vector.tensor_tensor(x1[:, tiles, :], scaled[:, par, :, :], x_bias[:, par, :, :], ALU.add).then_inc(x1_done, 1)
                dve.wait_ge(ga_done, 1)
                dve.wait_ge(x1_done, b + 1)
                for t in range(TB):
                    last = nc.vector.bn_stats(stats[:, par, t, :], x1[:, bass.ds(b * TB + t, 1), :].rearrange("p a c -> p (a c)"))
                last.then_inc(stats_done, 1)
                dve.wait_ge(ga_done, 1)
                dve.wait_ge(stats_done, b + 1)
                for t in range(TB):
                    last = nc.vector.bn_aggr(tile_mean_var[:, par, t, :], stats[:, par, t, :])
                step(last)
                step(nc.vector.tensor_copy(mean_var[:, tiles, :], tile_mean_var[:, par, :, :]))

            base = n[0]
            PER = 3

            def counted(b):
                k = [0]

                def s(ins):
                    k[0] += 1
                    ins.then_inc(chain, 1)
                    dve.wait_ge(chain, b * PER + base + k[0])
                return s

            for par in range(2):
                normalize_attention(par, par, True)
            with dve.Fori(0, NB // 2 - 1) as pair:
                for par in range(2):
                    residual(pair * 2 + par, par, counted(pair * 2 + par))
                    normalize_attention(pair * 2 + 2 + par, par, False)
            for b in (NB - 2, NB - 1):
                residual(b, b % 2, counted(b))
            n[0] = base + PER * NB

            step(nc.vector.tensor_scalar(var[:], mean_var[:, :, 1], EPS, None, ALU.add))
            nc.vector.engine_nop().then_inc(var_done, 1)
            dve.wait_ge(root_done, 1)
            newton_rstd(nc, step, root[:], var[:], half[:])

            def normalize(b, par, first):
                if not first:
                    dve.wait_ge(trans_done, b - 1)
                for t in range(TB):
                    tile = bass.ds(b * TB + t, 1)
                    last = nc.vector.tensor_scalar(norm[:, par, t, :], x1[:, tile, :].rearrange("p a c -> p (a c)"),
                                                   mean_var[:, tile, 0], root[:, tile], ALU.subtract, ALU.mult)
                last.then_inc(norm_done, 1)

            def copy_logits(b, par):
                dve.wait_ge(gate_done, b + 1)
                nc.vector.tensor_copy(logits[:, bass.ds(b * TB, TB), :].rearrange("p t e -> p (t e)"),
                                      gate_ps[par][:, 0:TB * E]).then_inc(logits_done, 1)

            for par in range(2):
                normalize(par, par, True)
            with dve.Fori(0, NB // 2 - 1) as pair:
                for par in range(2):
                    normalize(pair * 2 + 2 + par, par, False)
                for par in range(2):
                    copy_logits(pair * 2 + par, par)
            for b in (NB - 2, NB - 1):
                copy_logits(b, b % 2)
            dve.wait_ge(logits_done, NB)

            wide = lambda a: a[:][:, :, None].broadcast_to([128, NT, E])
            tt, ts = nc.vector.tensor_tensor, nc.vector.tensor_scalar

            def first_of(hot, values, m):
                step(nc.vector.reduce_max(m, values, AX.X))
                step(tt(tmp[:], values, wide(m), ALU.is_equal))
                step(tt(tmp[:], tmp[:], rank[:], ALU.mult))
                step(nc.vector.reduce_max(pick[:], tmp[:], AX.X))
                step(tt(hot, tmp[:], wide(pick), ALU.is_equal))

            first_of(one_hot[0][:], logits[:], top[0][:])
            step(tt(diff[0][:], logits[:], wide(top[0]), ALU.subtract))
            nc.vector.engine_nop().then_inc(diff_done, 1)
            step(nc.vector.scalar_tensor_tensor(tmp2[:], one_hot[0][:], -3e38, logits[:], ALU.mult, ALU.add))
            first_of(one_hot[1][:], tmp2[:], top[1][:])
            step(tt(diff[1][:], logits[:], wide(top[1]), ALU.subtract))
            step(ts(diff[1][:], diff[1][:], 0.0, None, ALU.min))
            nc.vector.engine_nop().then_inc(diff_done, 1)
            step(nc.vector.scalar_tensor_tensor(tmp2[:], logits[:], -1.0, logits[:], ALU.mult, ALU.max))
            for i in range(2):
                step(tt(tmp[:], tmp2[:], wide(top[i]), ALU.max))
                step(nc.vector.reciprocal(tmp[:], tmp[:]))
                step(nc.vector.scalar_tensor_tensor(tmp[:], diff[i][:], -1.0, tmp[:], ALU.mult, ALU.mult))
                step(ts(tmp[:], tmp[:], 0.02, None, ALU.is_gt))
                if i:
                    step(tt(tmp[:], tmp[:], one_hot[0][:], ALU.max))
                step(ts(tmp[:], tmp[:], -1.0, 1.0, ALU.mult, ALU.add))
                dve.wait_ge(exp_done, i + 1)
                step(tt(tmp[:], tmp[:], expd[i][:], ALU.mult))
                step(nc.vector.reduce_sum(pick[:], tmp[:], AX.X))
                step(nc.vector.reciprocal(pick[:], pick[:]))
                step(tt(one_hot[i][:] if i else weights[:], one_hot[i][:], wide(pick), ALU.mult))
            step(tt(weights[:], weights[:], one_hot[1][:], ALU.add))
            nc.vector.engine_nop().then_inc(weights_done, 1)
            for i in range(2):
                dve.wait_ge(wT_done, i + 1)
                nc.vector.tensor_copy(weights_T[:, i, :], misc_ps[i][:, 0:128]).then_inc(wT_copied, 1)


def expert_phase(nc, io, keep, out):
    ctx = ExitStack()
    with ctx:
        sb = lambda n, s, d=F32: ctx.enter_context(nc.sbuf_tensor("d_" + n, s, d))
        sem = lambda n: ctx.enter_context(nc.semaphore("d_" + n))
        ps = [ctx.enter_context(nc.psum_tensor(f"d_ps{i}", [128, 512], F32)) for i in range(8)]
        gate_ps, up_ps, y_ps, trans_ps = ps[0:2], ps[2:4], ps[4], ps[6:8]
        mod, ident, x1, h_hi, h_lo = (keep[n] for n in ("mod", "ident", "x1", "h_hi", "h_lo"))
        W1, W3, W2 = range(3)
        raw = sb("raw", [128, 2, 3, 512])
        w_hi, w_lo = sb("w_hi", [128, 2, 3, 512], F32R), sb("w_lo", [128, 2, 3, 512], F32R)
        route = sb("route", [128, 2, T])
        silu, g = sb("silu", [128, 2, L]), sb("g", [128, 2, L])
        g_hi, g_lo = sb("g_hi", [128, FB, L], F32R), sb("g_lo", [128, FB, L], F32R)
        y_T, weighed = sb("y_T", [128, T]), sb("weighed", [128, L])
        scaled = sb("scaled", [128, 2, L])

        raw_in = [sem(f"raw_in{i}") for i in range(2)]
        route_in = [sem(f"route_in{i}") for i in range(2)]
        w_done, gate_done, up_done = sem("w_done"), sem("gate_done"), sem("up_done")
        silu_done, g_done, g_hi_done, g_lo_done = sem("silu_done"), sem("g_done"), sem("g_hi_done"), sem("g_lo_done")
        down_done, y_read, y_added = sem("down_done"), sem("y_read"), sem("y_added")
        scaled_done, trans_done, out_done, stored = sem("scaled_done"), sem("trans_done"), sem("out_done"), sem("stored")
        zeroed = sem("zeroed")
        block = ctx.enter_context(nc.Block())
        CH = NB

        def experts(eng, chunk):
            def pair(ep, start):
                for par in range(2):
                    e = ep * 2 + par
                    chunk(e, 0, par, 1 - par, start and par == 0)
                    with eng.Fori(1, CH) as c:
                        chunk(e, c, par, par, False)
            pair(0, True)
            with eng.Fori(1, E // 2) as ep:
                pair(ep, False)

        @block.sync
        def _(sp):
            def load(e, par):
                for w, name in ((W1, "w1_T"), (W3, "w3_T"), (W2, "w2_T")):
                    sp.dma_start(raw[:, par, w, :], io[name][e].rearrange("p a b -> p (a b)") if name == "w2_T" else io[name][e])\
                        .then_inc(raw_in[par], 16)
                sp.dma_start(route[:, par, :], io["routes"][e, :].partition_broadcast(128)).then_inc(route_in[par], 16)

            load(0, 0)
            load(1, 1)
            for e in range(2, E):
                sp.wait_ge(w_done, 2 * (e - 1))
                sp.wait_ge(y_added, (e - 1) * CH)
                load(e, e % 2)
            for b in range(NB):
                sp.wait_ge(out_done, b + 1)
                sp.dma_start(out[:, TB * b:TB * (b + 1), :], x1[:, TB * b:TB * (b + 1), :]).then_inc(stored, 16)
            sp.wait_ge(stored, 16 * NB)

        @block.gpsimd
        def _(pool):
            nc.gpsimd.memset(y_T[:], 0.0).then_inc(zeroed, 1)
            for e in range(E):
                par = e % 2
                pool.wait_ge(raw_in[par], 48 * (e // 2 + 1))
                if e >= 2:
                    pool.wait_ge(down_done, (e - 1) * CH * FB)
                flat = lambda t: t[:, par, :, :].rearrange("p a b -> p (a b)")
                nc.gpsimd.tensor_copy(flat(w_hi), flat(raw)).then_inc(w_done, 1)
                pool.wait_ge(w_done, 2 * e + 1)
                nc.gpsimd.tensor_tensor(flat(w_lo), flat(raw), flat(w_hi).bitcast(F32), ALU.subtract).then_inc(w_done, 1)

        @block.tensor
        def _(pe):
            def product(dst, par, w, fb, hi, lo, start, stop):
                cols = slice(fb * 128, fb * 128 + 128)
                nc.tensor.matmul(dst[:], w_hi[:, par, w, cols], hi, start=start, stop=False)
                nc.tensor.matmul(dst[:], w_hi[:, par, w, cols], lo, start=False, stop=False)
                return nc.tensor.matmul(dst[:], w_lo[:, par, w, cols], hi, start=False, stop=stop)

            def up(e, c, par, n, fb):
                cols = bass.ds(c * L, L)
                if not (isinstance(n, int) and n < 2):
                    pe.wait_ge(g_done, n - 1)
                product(gate_ps[fb % 2], par, W1, fb, h_hi[:, cols], h_lo[:, cols], True, True).then_inc(gate_done, 1)
                product(up_ps[fb % 2], par, W3, fb, h_hi[:, cols], h_lo[:, cols], True, True).then_inc(up_done, 1)

            def down(par, at, n, fb):
                pe.wait_ge(g_lo_done, n + 1)
                if fb == 0 and not (isinstance(at, int) and at == 0):
                    pe.wait_ge(y_read, at)
                last = product(y_ps, par, W2, fb, g_hi[:, fb, :], g_lo[:, fb, :], fb == 0, fb == FB - 1)
                last.then_inc(down_done, 1)

            def chunk(e, c, par, before, first):
                at = e * CH + c
                if isinstance(c, int) and c == 0:
                    pe.wait_ge(w_done, e * 2 + 2)
                for fb in range(FB):
                    n = at * FB + fb
                    up(e, c, par, n, fb)
                    if fb >= 2:
                        down(par, at, n - 2, fb - 2)
                    elif not first:
                        down(before, at, n - 2, fb + 2)

            experts(pe, chunk)
            for fb in (2, 3):
                down(1, E * CH, E * CH * FB - FB + fb, fb)

            def transpose_batch(b, par, first):
                pe.wait_ge(scaled_done, b + 1)
                if not first:
                    pe.wait_ge(out_done, b - 1)
                for t in range(TB):
                    last = nc.tensor.transpose(trans_ps[par][:, t * 128:(t + 1) * 128], scaled[:, par, t * 128:(t + 1) * 128], ident[:])
                last.then_inc(trans_done, 1)

            transpose_batch(0, 0, True)
            transpose_batch(1, 1, True)
            with pe.Fori(1, NB // 2) as pair:
                for par in range(2):
                    transpose_batch(pair * 2 + par, par, False)

        @block.scalar
        def _(act):
            def chunk(e, c, par, before, first):
                for fb in range(FB):
                    n = (e * CH + c) * FB + fb
                    act.wait_ge(gate_done, n + 1)
                    if not (first and fb < 2):
                        act.wait_ge(g_done, n - 1)
                    nc.scalar.activation(silu[:, fb % 2, :], gate_ps[fb % 2][:], ACT.Silu).then_inc(silu_done, 1)
                    act.wait_ge(g_done, n + 1)
                    if not first:
                        act.wait_ge(down_done, n - 3)
                    nc.scalar.activation(g_hi[:, fb, :], g[:, fb % 2, :], ACT.Copy).then_inc(g_hi_done, 1)

            experts(act, chunk)

            def scale(b, par, first):
                act.wait_ge(y_added, E * CH) if first else act.wait_ge(trans_done, b - 1)
                nc.scalar.activation(scaled[:, par, :], y_T[:, bass.ds(b * L, L)], ACT.Copy,
                                     scale=mod[:, GB, bass.ds(b, 1)]).then_inc(scaled_done, 1)

            scale(0, 0, True)
            scale(1, 1, True)
            with act.Fori(1, NB // 2) as pair:
                for par in range(2):
                    scale(pair * 2 + par, par, False)

        @block.vector
        def _(dve):
            def multiply(n, fb, first):
                dve.wait_ge(silu_done, n + 1)
                dve.wait_ge(up_done, n + 1)
                if not (first and fb < 2):
                    dve.wait_ge(g_lo_done, n - 1)
                nc.vector.tensor_tensor(g[:, fb % 2, :], silu[:, fb % 2, :], up_ps[fb % 2][:], ALU.mult).then_inc(g_done, 1)

            def low_part(n, fb):
                dve.wait_ge(g_hi_done, n + 1)
                nc.vector.tensor_tensor(g_lo[:, fb, :], g[:, fb % 2, :], g_hi[:, fb, :].bitcast(F32), ALU.subtract).then_inc(g_lo_done, 1)

            def collect(at, c, par):
                cols = bass.ds(c * L, L)
                dve.wait_ge(down_done, at * FB + FB)
                nc.vector.tensor_tensor(weighed[:], y_ps[:], route[:, par, cols], ALU.mult).then_inc(y_read, 1)
                dve.wait_ge(y_read, at + 1)
                nc.vector.tensor_tensor(y_T[:, cols], y_T[:, cols], weighed[:], ALU.add).then_inc(y_added, 1)

            dve.wait_ge(zeroed, 1)

            def chunk(e, c, par, before, first):
                at = e * CH + c
                if isinstance(c, int) and c == 0:
                    if isinstance(e, int):
                        dve.wait_ge(route_in[par], 16 * (e // 2 + 1))
                    else:
                        dve.wait_ge(route_in[par], e * 8 - par * 8 + 16)
                for fb in range(FB):
                    n = at * FB + fb
                    multiply(n, fb, first)
                    if not (first and fb == 0):
                        low_part(n - 1, (fb - 1) % FB)
                    if fb == 1 and not first:
                        collect(at - 1, c - 1 if not (isinstance(c, int) and c == 0) else CH - 1, before)

            experts(dve, chunk)
            low_part(E * CH * FB - 1, FB - 1)
            collect(E * CH - 1, CH - 1, 1)

            def residual(b, par):
                dve.wait_ge(trans_done, b + 1)
                tiles = bass.ds(b * TB, TB)
                nc.vector.tensor_tensor(x1[:, tiles, :], x1[:, tiles, :], trans_ps[par][:].rearrange("p (t c) -> p t c", c=D),
                                        ALU.add).then_inc(out_done, 1)

            with dve.Fori(0, NB // 2) as pair:
                for par in range(2):
                    residual(pair * 2 + par, par)


def build(nc, io, out):
    io["sums"] = nc.dram_tensor("sums", (NB * G * 128, L), F32, kind="Internal").ap()
    io["recips"] = nc.dram_tensor("recips", (NB * H, L), F32, kind="Internal").ap()
    io["routes"] = nc.dram_tensor("routes", (E, T), F32, kind="Internal").ap()
    ctx = ExitStack()
    with ctx:
        sb = lambda n, s, d=F32: ctx.enter_context(nc.sbuf_tensor(n, s, d))
        keep = dict(mod=sb("mod", [128, 6, NB]), csil=sb("csil", [128, NB]), ident=sb("ident", [128, 128]))
        with ExitStack() as attn:
            ab = lambda n, s, d=F32: attn.enter_context(nc.sbuf_tensor(n, s, d))
            for n in ("q_hi", "q_lo", "k_hi", "k_lo"):
                keep[n] = ab(n, [128, T])
            keep["q_bf"], keep["k_bf"] = ab("q_bf", [128, T], BF16), ab("k_bf", [128, T], BF16)
            keep["v_all"] = ab("v_all", [128, NT, D])
            keep["q_own"] = ab("q_own", [128, G, HG, L], BF16)
            keep["q_pack"] = ab("q_pack", [128, 2, L], F32R)
            keep["k_pack"] = ab("k_pack", [128, 2, L])
            keep["v_aug"] = ab("v_aug", [128, 2, TB, HG, 32])
            keep["head_mask"] = ab("head_mask", [128, HG])
            qkv_phase(nc, io, keep)
            if io.get("stop") == 1:
                return
            attention_phase(nc, io, keep)
            if io.get("stop") == 2:
                return
        keep.update(x1=sb("x1", [128, NT, D]), h_hi=sb("h_hi", [128, T], F32R), h_lo=sb("h_lo", [128, T], F32R))
        route_phase(nc, io, keep)
        if io.get("stop") == 3:
            return
        expert_phase(nc, io, keep, out)


def layouts(inputs):
    import numpy as np

    a = {k: np.asarray(v) for k, v in inputs.items()}
    rows = lambda m: np.ascontiguousarray(m.reshape(NT, 128, D).transpose(1, 0, 2))
    head_of = (np.arange(128) % S_ROW) // DK
    arrays = {
        "x": np.ascontiguousarray(a["L0_attn_x"]).reshape(T, D),
        "c_T": np.ascontiguousarray(a["L0_c"].T),
        "wmod": a["L0_wmod"],
        "wmod_ga": np.ascontiguousarray(a["L0_wmod"][:, GA * D:(GA + 1) * D]),
        "wqkv": a["L0_attn_W_qkv"],
        "bias_qk": np.ascontiguousarray(a["L0_attn_b_qkv"][0:2 * D].reshape(2, D).T),
        "bias_v": np.ascontiguousarray(a["L0_attn_b_qkv"][2 * D:3 * D]),
        "wout": a["L0_attn_W_out"],
        "bias_out": a["L0_attn_b_out"],
        "gate_T": np.ascontiguousarray(a["L0_ffn_gate_w"].T),
        "w1_T": np.ascontiguousarray(a["L0_ffn_w1"].transpose(0, 2, 1)),
        "w3_T": np.ascontiguousarray(a["L0_ffn_w3"].transpose(0, 2, 1)),
        "w2_T": np.ascontiguousarray(a["L0_ffn_w2"].transpose(0, 2, 1).reshape(E, FB, 128, D).transpose(0, 2, 1, 3)),
        "ident": np.eye(128, dtype=np.float32),
        "above": (np.triu(np.ones((128, 128)), 1) * -BIG).astype(np.float32),
        "head_mask": (head_of[:, None] == np.arange(HG)[None, :]).astype(np.float32),
        "one_rows": ((np.arange(128) < S_ROW) & (np.arange(128) % DK == 0)).astype(np.float32)[:, None],
        "rank": np.tile(np.arange(E, 0, -1, dtype=np.float32), NT)[None, :].repeat(128, 0),
    }
    return arrays


def kernel(**inputs):
    import numpy as np
    import concourse.bacc as bacc
    from concourse.bass_utils import run_bass_kernel_spmd

    nc = bacc.Bacc("TRN2", target_bir_lowering=False, num_devices=1)
    arrays = layouts(inputs)
    io = {n: nc.dram_tensor("in_" + n, v.shape, mybir.dt.from_np(v.dtype), kind="ExternalInput").ap() for n, v in arrays.items()}
    io["x"] = io["x"].rearrange("(t p) c -> p t c", p=128)
    out = nc.dram_tensor("out_x", (T, D), F32, kind="ExternalOutput").ap()
    build(nc, io, out.rearrange("(t p) c -> p t c", p=128))
    r = run_bass_kernel_spmd(nc, [{"in_" + n: v for n, v in arrays.items()}], core_ids=[0])
    return r.results[0]["out_x"].reshape(NB, L, D)
```

```python
import concourse.bass as bass
from concourse import mybir
from contextlib import ExitStack

F32 = mybir.dt.float32
F32R = mybir.dt.float32r
BF16 = mybir.dt.bfloat16
I32, U32 = mybir.dt.int32, mybir.dt.uint32
ALU = mybir.AluOpType
ACT = mybir.ActivationFunctionType
AX = mybir.AxisListType

NB, L, D = 8, 512, 128
H, DK = 16, 8
T = NB * L
TB = L // 128
NT = T // 128
G, HG = 4, 4
E, FF = 8, 512
FB = FF // 128
NS = 2 * NT + E
SLOTS = NS * 128
EPS = 1e-5
SA, CA, GA, SB_, CB, GB = range(6)
BIG = 1e30
S_ROW = HG * DK


def clamp_gate(nc, dve, step, gate, sign, mag):
    step(nc.vector.tensor_scalar(sign, gate, 0.0, 2.0, ALU.is_ge, ALU.mult))
    step(nc.vector.tensor_scalar(mag, gate, -1.0, None, ALU.mult))
    step(nc.vector.tensor_tensor(mag, mag, gate, ALU.max))
    step(nc.vector.tensor_scalar(mag, mag, 0.25, None, ALU.max))
    step(nc.vector.scalar_tensor_tensor(gate, sign, -1.0, mag, ALU.add, ALU.mult))


def newton_rstd(nc, step, root, var, half):
    step(nc.vector.reciprocal(root, root))
    step(nc.vector.tensor_tensor(half, root, root, ALU.mult))
    step(nc.vector.tensor_tensor(half, half, var, ALU.mult))
    step(nc.vector.tensor_scalar(half, half, -0.5, 1.5, ALU.mult, ALU.add))
    step(nc.vector.tensor_tensor(root, root, half, ALU.mult))


def qkv_phase(nc, io, keep):
    ctx = ExitStack()
    with ctx:
        sb = lambda n, s, d=F32: ctx.enter_context(nc.sbuf_tensor("a_" + n, s, d))
        sem = lambda n: ctx.enter_context(nc.semaphore("a_" + n))
        ps = [ctx.enter_context(nc.psum_tensor(f"a_ps{i}", [128, 512], F32)) for i in range(8)]
        trans_ps, q_ps, k_ps, v_ps = ps[0:2], ps[2:4], ps[4:6], ps[6:8]
        mod, ident = keep["mod"], keep["ident"]
        csil = sb("csil", [128, NB])
        q_hi, q_lo, k_hi, k_lo = (keep[n] for n in ("q_hi", "q_lo", "k_hi", "k_lo"))
        q_bf, k_bf, v_all = keep["q_bf"], keep["k_bf"], keep["v_all"]
        x = sb("x", [128, NT, D])
        norm = sb("norm", [128, 2, TB, D])
        stats = sb("stats", [128, TB, 6])
        mean_var = sb("mean_var", [128, NT, 2])
        var, root, half = sb("var", [128, NT]), sb("root", [128, NT]), sb("half", [128, NT])
        hT = sb("hT", [128, 2, L])
        wqkv, wmod = sb("wqkv", [128, 3 * D]), sb("wmod", [128, 6 * D])
        c_T = sb("c_T", [128, NB])
        bias_qk, bias_v = sb("bias_qk", [128, 2]), sb("bias_v", [128, D])
        sign, mag = sb("sign", [128, NB]), sb("mag", [128, NB])

        x_in = [sem(f"x_in{b}") for b in range(2)]
        w_in, c_in = sem("w_in"), sem("c_in")
        silu_done, mod_done, mod_copied = sem("silu_done"), sem("mod_done"), sem("mod_copied")
        chain = sem("dve_chain")
        stats_done, root_done, norm_done = sem("stats_done"), sem("root_done"), sem("norm_done")
        trans_done, hT_done = sem("trans_done"), sem("hT_done")
        q_done, k_done, v_done = sem("q_done"), sem("k_done"), sem("v_done")
        hi_done, lo_done = sem("hi_done"), sem("lo_done")
        set_in, zeroed = sem("set_in"), sem("zeroed")
        one_rows = sb("one_rows", [128, 1])
        block = ctx.enter_context(nc.Block())

        @block.gpsimd
        def _(pool):
            v_aug = keep["v_aug"]
            pool.dma_start(keep["head_mask"][:], io["head_mask"]).then_inc(set_in, 16)
            pool.dma_start(one_rows[:], io["one_rows"]).then_inc(set_in, 16)
            nc.gpsimd.memset(keep["q_own"][:].bitcast(F32), 0.0)
            nc.gpsimd.memset(keep["q_pack"][:].bitcast(F32), 0.0)
            for part, value in ((slice(0, DK), 0.0), (slice(DK, 2 * DK), 1.0), (slice(2 * DK, 32), 0.0)):
                nc.gpsimd.memset(v_aug[:, :, :, :, part].rearrange("p a t j d -> p (a t j) d"), value)
            nc.gpsimd.memset(keep["k_pack"][:], 0.0).then_inc(zeroed, 1)
            pool.wait_ge(set_in, 32)
            pool.wait_ge(zeroed, 1)
            nc.gpsimd.tensor_scalar(keep["k_pack"][:].rearrange("p a n -> p (a n)"),
                                    keep["k_pack"][:].rearrange("p a n -> p (a n)"), one_rows[:], None, ALU.add)

        @block.sync
        def _(sp):
            sp.dma_start(c_T[:], io["c_T"]).then_inc(c_in, 16)
            sp.dma_start(wmod[:], io["wmod"]).then_inc(c_in, 16)
            for half_ in range(2):
                for b in range(4 * half_, 4 * half_ + 4):
                    sp.dma_start(x[:, TB * b:TB * b + TB, :], io["x"][:, TB * b:TB * b + TB, :]).then_inc(x_in[half_], 16)
            sp.wait_ge(x_in[1], 64)

        @block.scalar
        def _(act):
            act.dma_start(wqkv[:], io["wqkv"]).then_inc(w_in, 16)
            act.dma_start(bias_qk[:], io["bias_qk"]).then_inc(w_in, 16)
            act.dma_start(bias_v[:], io["bias_v"].partition_broadcast(128)).then_inc(w_in, 16)
            act.dma_start(ident[:], io["ident"]).then_inc(w_in, 16)
            act.wait_ge(c_in, 32)
            nc.scalar.activation(csil[:], c_T[:], ACT.Silu).then_inc(silu_done, 1)
            act.wait_ge(stats_done, 1)
            nc.scalar.activation(root[:], var[:], ACT.Sqrt).then_inc(root_done, 1)
            act.wait_ge(mod_copied, 1)
            act.wait_ge(w_in, 64)

            def batch(b, par, first):
                act.wait_ge(trans_done, b + 1)
                if not first:
                    act.wait_ge(v_done, b - 1)
                nc.scalar.activation(hT[:, par, :], trans_ps[par][:], ACT.Identity,
                                     bias=mod[:, SA, bass.ds(b, 1)], scale=mod[:, CA, bass.ds(b, 1)]).then_inc(hT_done, 1)
                cols = bass.ds(b * L, L)
                act.wait_ge(q_done, b + 1)
                nc.scalar.activation(q_hi[:, cols].bitcast(F32R), q_ps[par][:], ACT.Identity,
                                     bias=bias_qk[:, 0:1]).then_inc(hi_done, 1)
                act.wait_ge(k_done, b + 1)
                nc.scalar.activation(k_hi[:, cols].bitcast(F32R), k_ps[par][:], ACT.Identity,
                                     bias=bias_qk[:, 1:2]).then_inc(hi_done, 1)

            batch(0, 0, True)
            batch(1, 1, True)
            with act.Fori(1, NB // 2) as pair:
                for par in range(2):
                    batch(pair * 2 + par, par, False)

        @block.vector
        def _(dve):
            n = [0]

            def step(ins):
                n[0] += 1
                ins.then_inc(chain, 1)
                dve.wait_ge(chain, n[0])

            for b in range(NB):
                dve.wait_ge(x_in[b // 4], 64)
                for t in range(TB):
                    last = nc.vector.bn_stats(stats[:, t, :], x[:, TB * b + t, :])
                step(last)
                for t in range(TB):
                    last = nc.vector.bn_aggr(mean_var[:, TB * b + t, :], stats[:, t, :])
                step(last)
            step(nc.vector.tensor_scalar(var[:], mean_var[:, :, 1], EPS, None, ALU.add))
            nc.vector.engine_nop().then_inc(stats_done, 1)
            dve.wait_ge(mod_done, 1)
            step(nc.vector.tensor_copy(mod[:].rearrange("p a b -> p (a b)"), ps[7][:, 0:6 * NB]))
            step(nc.vector.tensor_scalar(mod[:, CA, :], mod[:, CA, :], 1.0, None, ALU.add))
            step(nc.vector.tensor_scalar(mod[:, CB, :], mod[:, CB, :], 1.0, None, ALU.add))
            clamp_gate(nc, dve, step, mod[:, GA, :], sign[:], mag[:])
            clamp_gate(nc, dve, step, mod[:, GB, :], sign[:], mag[:])
            nc.vector.engine_nop().then_inc(mod_copied, 1)
            dve.wait_ge(root_done, 1)
            newton_rstd(nc, step, root[:], var[:], half[:])
            dve.wait_ge(w_in, 64)

            def normalize(b, par):
                for t in range(TB):
                    tile = bass.ds(b * TB + t, 1)
                    last = nc.vector.tensor_scalar(norm[:, par, t, :], x[:, tile, :].rearrange("p a c -> p (a c)"),
                                                   mean_var[:, tile, 0], root[:, tile], ALU.subtract, ALU.mult)
                last.then_inc(norm_done, 1)

            def batch(b, par):
                cols = bass.ds(b * L, L)
                dve.wait_ge(hi_done, 2 * b + 1)
                nc.vector.scalar_tensor_tensor(q_lo[:, cols].bitcast(F32R), q_ps[par][:], bias_qk[:, 0:1],
                                               q_hi[:, cols], ALU.add, ALU.subtract)
                nc.vector.tensor_copy(q_bf[:, cols], q_hi[:, cols])
                dve.wait_ge(hi_done, 2 * b + 2)
                nc.vector.scalar_tensor_tensor(k_lo[:, cols].bitcast(F32R), k_ps[par][:], bias_qk[:, 1:2],
                                               k_hi[:, cols], ALU.add, ALU.subtract)
                nc.vector.tensor_copy(k_bf[:, cols], k_hi[:, cols])
                dve.wait_ge(v_done, b + 1)
                nc.vector.tensor_tensor(v_all[:, bass.ds(b * TB, TB), :],
                                        v_ps[par][:].rearrange("p (t c) -> p t c", c=D),
                                        bias_v[:, None, :].broadcast_to([128, TB, D]), ALU.add).then_inc(lo_done, 1)

            for par in range(2):
                normalize(par, par)
            with dve.Fori(0, NB // 2 - 1) as pair:
                for par in range(2):
                    dve.wait_ge(trans_done, pair * 2 + par + 1)
                    normalize(pair * 2 + 2 + par, par)
                for par in range(2):
                    batch(pair * 2 + par, par)
            for par in range(2):
                batch(NB - 2 + par, par)

        @block.tensor
        def _(pe):
            pe.wait_ge(silu_done, 1)
            for part in range(6):
                last = nc.tensor.matmul(ps[7][:, part * NB:(part + 1) * NB], wmod[:, part * D:(part + 1) * D],
                                        csil[:], start=True, stop=True)
            last.then_inc(mod_done, 1)
            pe.wait_ge(w_in, 64)
            pe.wait_ge(mod_copied, 1)

            def transpose_batch(b, par, first):
                pe.wait_ge(norm_done, b + 1)
                if not first:
                    pe.wait_ge(hT_done, b - 1)
                for t in range(TB):
                    last = nc.tensor.transpose(trans_ps[par][:, t * 128:(t + 1) * 128],
                                               norm[:, par, t, :], ident[:])
                last.then_inc(trans_done, 1)

            def project_batch(b, par, first):
                pe.wait_ge(hT_done, b + 1)
                if not first:
                    pe.wait_ge(lo_done, b - 1)
                nc.tensor.matmul(q_ps[par][:], wqkv[:, 0:D], hT[:, par, :], start=True, stop=True).then_inc(q_done, 1)
                nc.tensor.matmul(k_ps[par][:], wqkv[:, D:2 * D], hT[:, par, :], start=True, stop=True).then_inc(k_done, 1)
                for t in range(TB):
                    last = nc.tensor.matmul(v_ps[par][:, t * D:(t + 1) * D], hT[:, par, t * 128:(t + 1) * 128],
                                            wqkv[:, 2 * D:3 * D], start=True, stop=True)
                last.then_inc(v_done, 1)

            for first in (True,):
                transpose_batch(0, 0, first)
                transpose_batch(1, 1, first)
                project_batch(0, 0, first)
                project_batch(1, 1, first)
            with pe.Fori(1, NB // 2) as pair:
                for par in range(2):
                    transpose_batch(pair * 2 + par, par, False)
                for par in range(2):
                    project_batch(pair * 2 + par, par, False)


FILLS = [f for a in (0, 2) for f in (
    [(a, 3, 0)], [(a, 2, 0), (a, 0, 384)],
    [(a + 1, 3, 0)], [(a + 1, 2, 0), (a + 1, 0, 384)],
    [(a, 1, 0), (a + 1, 1, 256)])]
NF = len(FILLS)
KEY_COLS = {0: (0, 512), 1: (512, 384), 3: (896, 128)}
PAIR = 2560


def attention_phase(nc, io, keep):
    ctx = ExitStack()
    with ctx:
        sb = lambda n, s, d=F32: ctx.enter_context(nc.sbuf_tensor("b_" + n, s, d))
        sem = lambda n: ctx.enter_context(nc.semaphore("b_" + n))
        pb = lambda n, w: ctx.enter_context(nc.psum_tensor("b_" + n, [128, w], F32))
        q_hi, q_lo, k_hi, k_lo = (keep[n] for n in ("q_hi", "q_lo", "k_hi", "k_lo"))
        q_bf, k_bf, v_all, ident = keep["q_bf"], keep["k_bf"], keep["v_all"], keep["ident"]
        q_own, q_pack, k_pack, v_aug = keep["q_own"], keep["q_pack"], keep["k_pack"], keep["v_aug"]
        head_mask, sums = keep["head_mask"], io["sums"]
        k_own = sb("k_own", [128, 2, HG, L], F32R)
        probs = sb("probs", [128, 2, 2, PAIR])
        out_T = sb("out_T", [128, 2, L])
        neg_max = sb("neg_max", [HG, 2, L])
        row_max = sb("row_max", [128, 2, TB, HG])
        above_f = sb("above_f", [128, 128])
        ident_bf, above = sb("ident_bf", [128, 128], BF16), sb("above", [128, 128], BF16)
        ab_ps, c_ps, o_ps = pb("ab_ps", 2048), pb("c_ps", 512), pb("o_ps", 512)
        max_ps = [pb("max_ps0", 512), pb("max_ps1", 512)]

        const_in, const_cast, waited = sem("const_in"), sem("const_cast"), sem("waited")
        k_in = [sem(f"k_in{i}") for i in range(2)]
        q_in = [sem(f"q_in{i}") for i in range(2)]
        sums_out = [sem(f"sums_out{i}") for i in range(2)]
        q_own_done, fill_done, red_done = sem("q_own_done"), sem("fill_done"), sem("red_done")
        max_T_done, neg_done = sem("max_T_done"), sem("neg_done")
        own_pool, own_act = sem("own_pool"), sem("own_act")
        ab_done, c_done, exp_ab, exp_c = sem("ab_done"), sem("c_done"), sem("exp_ab"), sem("exp_c")
        masked, v_done, pv_done, o_copied = sem("masked"), sem("v_done"), sem("pv_done"), sem("o_copied")
        block = ctx.enter_context(nc.Block())

        U = NB * G
        PRO_FILLS = 2 * NF

        def batches(eng, slot):
            for g in range(G):
                slot(0, g, g)
            with eng.Fori(1, NB - 1) as b:
                for g in range(G):
                    slot(b, g, b * G + g)
            for g in range(G):
                slot(NB - 1, g, (NB - 1) * G + g)

        def ahead(u, n):
            return not isinstance(u, int) or u + n < U

        def first(u, n):
            return isinstance(u, int) and u < n

        def where(b, g, n):
            return b + (g + n) // G, (g + n) % G

        def uses(b, g):
            return b * 2 + g // 2 + 1

        def bank_of_fill(v, par, f):
            if isinstance(v, int) and v < 2:
                return (v * (NF + 1) + f) % 2
            return (PRO_FILLS + 1 + par * (NF + 1) + 1 + f) % 2

        def bank_of_transpose(par):
            return (PRO_FILLS + 1 + par * (NF + 1)) % 2

        @block.sync
        def _(sp):
            sp.dma_start(above_f[:], io["above"]).then_inc(const_in, 16)

            def load(b, g):
                par, src, cols = g % 2, slice(S_ROW * g, S_ROW * (g + 1)), bass.ds(b * L, L)
                for slot, piece in ((1, k_hi), (2, k_lo), (3, k_hi)):
                    sp.dma_start(k_pack[S_ROW * slot:S_ROW * (slot + 1), par, :], piece[src, cols]).then_inc(k_in[par], 16)
                for slot, piece in ((1, q_hi), (2, q_hi), (3, q_lo)):
                    sp.dma_start(q_pack[S_ROW * slot:S_ROW * (slot + 1), par, :].bitcast(F32), piece[src, cols])\
                        .then_inc(q_in[par], 16)

            def load_max(g):
                sp.dma_start(q_pack[0:S_ROW:DK, g % 2, :].bitcast(F32), neg_max[:, g % 2, :]).then_inc(q_in[g % 2], 16)

            def send_sums(b, g, u):
                sp.dma_start(sums[bass.ds(u * 128, 128), :], out_T[:, g % 2, :]).then_inc(sums_out[g % 2], 16)

            load(0, 0)
            sp.wait_ge(neg_done, 1)
            load_max(0)

            def slot(b, g, u):
                if ahead(u, 1):
                    if not first(u, 1):
                        sp.wait_ge(c_done, u * 2)
                    load(*where(b, g, 1))
                    sp.wait_ge(neg_done, u + 2)
                    load_max((g + 1) % G)
                if not first(u, 1):
                    sp.wait_ge(o_copied, u)
                    send_sums(*where(b, g, -1), u - 1)

            batches(sp, slot)
            sp.wait_ge(o_copied, U)
            send_sums(NB - 1, G - 1, U - 1)
            for par in range(2):
                sp.wait_ge(sums_out[par], 16 * (U // 2))

        @block.vector
        def _(dve):
            def own_queries(b, g):
                rows = slice(S_ROW * g, S_ROW * (g + 1))
                for j in range(HG):
                    nc.vector.tensor_scalar(q_own[rows, g, j, :], q_bf[rows, bass.ds(b * L, L)],
                                            head_mask[rows, j:j + 1], None, ALU.mult).then_inc(q_own_done, 1)

            def maxima(v, par):
                for f, parts in enumerate(FILLS):
                    dve.wait_ge(fill_done, v * NF + f + 1)
                    bank = max_ps[bank_of_fill(v, par, f)]
                    if len(parts) == 2 and parts[1][1] == 1:
                        last = nc.vector.reduce_max(row_max[:, par, 1, parts[0][0]:parts[0][0] + 2],
                                                    bank[:].rearrange("p (j n) -> p j n", j=2), AX.X)
                    else:
                        for j, i, c in parts:
                            last = nc.vector.reduce_max(row_max[:, par, i, j:j + 1],
                                                        bank[:, c:c + 128 * (i + 1)], AX.X)
                    last.then_inc(red_done, 1)

            nc.vector.tensor_copy(ident_bf[:], ident[:]).then_inc(const_cast, 1)
            dve.wait_ge(const_in, 16)
            nc.vector.tensor_copy(above[:], above_f[:]).then_inc(const_cast, 1)
            for u in range(3):
                own_queries(0, u)
            maxima(0, 0)
            maxima(1, 1)

            def slot(b, g, u):
                if ahead(u, 3):
                    own_queries(*where(b, g, 3))
                if ahead(u, 2):
                    dve.wait_ge(max_T_done, u + 1)
                    maxima(u + 2, g % 2)

            batches(dve, slot)

        @block.tensor
        def _(pe):
            pe.wait_ge(const_cast, 2)

            def fill(bv, gv, v, f):
                if f == 0:
                    pe.wait_ge(q_own_done, v * HG + HG)
                if not (isinstance(v, int) and v == 0 and f < 2) and not (f == 0):
                    pe.wait_ge(red_done, v * NF + f - 1)
                if f == 1 and not (isinstance(v, int) and v == 0):
                    pe.wait_ge(neg_done, v)
                bank = max_ps[bank_of_fill(v, gv % 2, f)]
                for j, i, c in FILLS[f]:
                    nc.tensor.matmul(bank[:, c:c + 128 * (i + 1)], q_own[:, gv, j, i * 128:(i + 1) * 128],
                                     k_bf[:, bass.ds(bv * L, 128 * (i + 1))], start=True, stop=False)
                    last = nc.tensor.matmul(bank[:, c + 128 * i:c + 128 * (i + 1)], ident_bf[:], above[:],
                                            start=False, stop=True)
                last.then_inc(fill_done, 1)

            def transpose_max(v, par, bank):
                pe.wait_ge(red_done, v * NF + NF)
                for i in range(TB):
                    last = nc.tensor.transpose(max_ps[bank][0:HG, i * 128:(i + 1) * 128], row_max[:, par, i, :], ident[:])
                last.then_inc(max_T_done, 1)

            def scores(b, g, u, j):
                par, pair = g % 2, u * 2 + j // 2
                if j == 0:
                    pe.wait_ge(q_in[par], uses(b, g) * 64)
                    pe.wait_ge(own_pool, u * 2 + 2)
                if j == 2:
                    pe.wait_ge(own_act, u * 2 + 2)
                if not (first(u, 1) and j < 2):
                    pe.wait_ge(exp_ab, u * HG + j - 1)
                for kt, (c, n) in KEY_COLS.items():
                    at = 1024 * (j % 2) + c
                    last = nc.tensor.matmul(ab_ps[:, at:at + n], k_own[:, par, j, kt * 128:(kt + 1) * 128],
                                            q_pack[:, par, L - n:L], start=True, stop=True)
                last.then_inc(ab_done, 1)
                if j % 2 == 0 and not (first(u, 1) and j == 0):
                    pe.wait_ge(exp_c, pair)
                last = nc.tensor.matmul(c_ps[:, 256 * (j % 2):256 * (j % 2) + 256], k_own[:, par, j, 256:384],
                                        q_pack[:, par, 256:512], start=True, stop=True)
                if j % 2:
                    last.then_inc(c_done, 1)

            def weigh(u, par, kt):
                if kt == 0:
                    pe.wait_ge(masked, u * 10 + 10)
                    pe.wait_ge(v_done, u + 1)
                    if not first(u, 1):
                        pe.wait_ge(o_copied, u)
                for j in range(HG):
                    if kt == 2:
                        c, n = 2048 + 256 * (j % 2), 256
                    else:
                        c, n = KEY_COLS[kt][0] + 1024 * (j % 2), KEY_COLS[kt][1]
                    last = nc.tensor.matmul(o_ps[32 * j:32 * j + 32, L - n:L], v_aug[:, par, kt, j, :],
                                            probs[:, par, j // 2, c:c + n], start=(kt == 0), stop=(kt == TB - 1))
                if kt == TB - 1:
                    last.then_inc(pv_done, 1)

            for f in range(NF):
                fill(0, 0, 0, f)
            transpose_max(0, 0, NF % 2)
            for f in range(NF):
                fill(0, 1, 1, f)

            def slot(b, g, u):
                par = g % 2
                fills = list(range(NF)) if ahead(u, 2) else []

                def next_fill():
                    if fills:
                        fill(*where(b, g, 2), u + 2, fills.pop(0))

                scores(b, g, u, 0)
                if ahead(u, 1):
                    transpose_max(u + 1, 1 - par, bank_of_transpose(par))
                scores(b, g, u, 1)
                next_fill()
                for kt in range(TB):
                    if not first(u, 1):
                        weigh(u - 1, 1 - par, kt)
                    if kt != 2:
                        next_fill()
                scores(b, g, u, 2)
                next_fill()
                scores(b, g, u, 3)
                while fills:
                    next_fill()

            batches(pe, slot)
            for kt in range(TB):
                weigh(U - 1, 1, kt)

        @block.scalar
        def _(act):
            scale = DK ** -0.5

            def negate_max(v, par, bank):
                act.wait_ge(max_T_done, v + 1)
                nc.scalar.activation(neg_max[:, par, :].bitcast(F32R), max_ps[bank][0:HG, :], ACT.Copy,
                                     scale=-1.0).then_inc(neg_done, 1)

            def own_keys(b, g, u):
                act.wait_ge(k_in[g % 2], uses(b, g) * 48)
                for j in (2, 3):
                    nc.scalar.activation(k_own[:, g % 2, j, :], k_pack[:, g % 2, :], ACT.Copy,
                                         scale=head_mask[:, j:j + 1]).then_inc(own_act, 1)

            def augment(b, g, u):
                if not first(u, 2):
                    act.wait_ge(pv_done, u - 1)
                nc.scalar.activation(v_aug[:, g % 2, :, :, 0:DK],
                                     v_all[:, bass.ds(b * TB, TB), S_ROW * g:S_ROW * (g + 1)]
                                     .rearrange("p t (j d) -> p t j d", d=DK), ACT.Copy).then_inc(v_done, 1)

            def exps(b, g, u, pair):
                par = g % 2
                if pair == 0 and not first(u, 2):
                    act.wait_ge(pv_done, u - 1)
                for j in (0, 1):
                    act.wait_ge(ab_done, u * HG + 2 * pair + j + 1)
                    nc.scalar.activation(probs[:, par, pair, 1024 * j:1024 * (j + 1)], ab_ps[:, 1024 * j:1024 * (j + 1)],
                                         ACT.Exp, scale=scale).then_inc(exp_ab, 1)
                act.wait_ge(c_done, u * 2 + pair + 1)
                nc.scalar.activation(probs[:, par, pair, 2048:PAIR], c_ps[:], ACT.Exp, scale=scale).then_inc(exp_c, 1)

            def copy_sums(b, g, u):
                act.wait_ge(pv_done, u + 1)
                if not first(u, 2):
                    act.wait_ge(sums_out[g % 2], uses(b, g) * 16 - 16)
                nc.scalar.activation(out_T[:, g % 2, :], o_ps[:], ACT.Copy).then_inc(o_copied, 1)

            negate_max(0, 0, NF % 2)
            own_keys(0, 0, 0)

            def slot(b, g, u):
                if ahead(u, 1):
                    negate_max(u + 1, 1 - g % 2, bank_of_transpose(g % 2))
                exps(b, g, u, 0)
                if ahead(u, 1):
                    if not first(u, 1):
                        act.wait_ge(c_done, u * 2)
                    own_keys(*where(b, g, 1), u + 1)
                if not first(u, 1):
                    copy_sums(*where(b, g, -1), u - 1)
                exps(b, g, u, 1)
                augment(b, g, u)

            batches(act, slot)
            copy_sums(NB - 1, G - 1, U - 1)

        @block.gpsimd
        def _(pool):
            def own_keys(b, g):
                pool.wait_ge(k_in[g % 2], uses(b, g) * 48)
                for j in (0, 1):
                    nc.gpsimd.tensor_tensor(k_own[:, g % 2, j, :], k_pack[:, g % 2, :],
                                            head_mask[:, j:j + 1].broadcast_to([128, L]), ALU.mult).then_inc(own_pool, 1)

            def causal(p, n):
                pattern = [[0, n], [1, 128]] if n > 1 else [[1, 128]]
                nc.gpsimd.affine_select(out=p, in_=p, pattern=pattern, compare_op=ALU.is_ge, fill=0.0, base=0,
                                        channel_multiplier=-1).then_inc(masked, 1)

            def mask(b, g, u, pair):
                for j in (0, 1):
                    p = probs[:, g % 2, pair, 1024 * j:1024 * (j + 1)]
                    pool.wait_ge(exp_ab, u * HG + 2 * pair + j + 1)
                    pool.sem_inc(waited, 1)
                    causal(p.rearrange("p (s n) -> p s n", s=2)[:, :, 0:128], 2)
                    causal(p[:, 896:1024], 1)
                pool.wait_ge(exp_c, u * 2 + pair + 1)
                pool.sem_inc(waited, 1)
                causal(probs[:, g % 2, pair, 2048:PAIR].rearrange("p (s n) -> p s n", s=2)[:, :, 0:128], 2)

            own_keys(0, 0)

            def slot(b, g, u):
                mask(b, g, u, 0)
                if ahead(u, 1):
                    if not first(u, 1):
                        pool.wait_ge(c_done, u * 2)
                    own_keys(*where(b, g, 1))
                mask(b, g, u, 1)

            batches(pool, slot)



def route_phase(nc, io, keep):
    ctx = ExitStack()
    with ctx:
        sb = lambda n, s, d=F32: ctx.enter_context(nc.sbuf_tensor("c_" + n, s, d))
        sem = lambda n: ctx.enter_context(nc.semaphore("c_" + n))
        ps = [ctx.enter_context(nc.psum_tensor(f"c_ps{i}", [128, 512], F32)) for i in range(8)]
        proj_ps, trans_ps, gate_ps, slot_ps, inv_ps = ps[0:2], ps[2:4], ps[4:6], ps[6], ps[7]
        mod, ident, x1, parts, w13, w2, route_w = (keep[n] for n in ("mod", "ident", "x1", "parts", "w13", "w2", "route_w"))
        P_GA, P_SB, P_CB, P_GB = range(4)
        pv, recip = sb("pv", [128, T]), sb("recip", [128, T])
        attn = sb("attn", [128, 2, L])
        den = sb("den", [128, L])
        wout, gate_w, bias_out = sb("wout", [128, D]), sb("gate_w", [128, E]), sb("bias_out", [128, D])
        scaled = sb("scaled", [128, 2, TB, D])
        stats, mean_var = sb("stats", [128, 2, TB, 6]), sb("mean_var", [128, NT, 2])
        tile_mean_var = sb("tile_mean_var", [128, 2, TB, 2])
        var, root, half = sb("var", [128, NT]), sb("root", [128, NT]), sb("half", [128, NT])
        norm, h, hT = sb("norm", [128, 2, TB, D]), sb("h", [128, 2, TB, D]), sb("hT", [128, 2, L])
        logits = sb("logits", [128, NT, E])
        rank = sb("rank", [128, NT, E])
        top = [sb(f"top{i}", [128, NT]) for i in range(2)]
        one_hot = [sb(f"one_hot{i}", [128, NT, E]) for i in range(2)]
        diff = [sb(f"diff{i}", [128, NT, E]) for i in range(2)]
        expd = [sb(f"expd{i}", [128, NT, E]) for i in range(2)]
        tmp, tmp2, pick = sb("tmp", [128, NT, E]), sb("tmp2", [128, NT, E]), sb("pick", [128, NT])
        number, before_f = sb("number", [128, 128]), sb("before_f", [128, 128])
        number_bf, before, ones = sb("number_bf", [128, 128], BF16), sb("before", [128, 128], BF16), sb("ones", [128, 128], BF16)
        multiple, partition, spare_row = sb("multiple", [128, NT]), sb("partition", [128, 1]), sb("spare_row", [128, NS])
        chosen = sb("chosen", [128, NT * E], BF16)
        PAD = NT // 2
        scan = [sb(f"scan{i}", [128, PAD + NT, E]) for i in range(2)]
        base = [sb(f"base{i}", [128, 2 * E]) for i in range(2)]
        pos, pos_int = sb("pos", [128, 2 * NT]), sb("pos_int", [128, 2 * NT], I32)
        tile_int = sb("tile_int", [128, 2 * NT], I32)
        tile_bf, lane_bf = sb("tile_bf", [128, 2 * NT], BF16), sb("lane_bf", [128, 2 * NT], BF16)
        ident_row = sb("ident_row", [128, NS])
        row_part = sb("row_part", [128, 3 * NS])
        cmp = sb("cmp", [128, NS * E])

        w_in, x_in, den_in, recip_out = sem("w_in"), sem("x_in"), sem("den_in"), sem("recip_out")
        pv_in = [sem(f"pv_in{i}") for i in range(2)]
        recip_in = [sem(f"recip_in{i}") for i in range(2)]
        raw_in = [sem(f"raw_in{i}") for i in range(E)]
        den_done = sem("den_done")
        parts_ps_done, parts_done, ga_bias_done, biased = sem("parts_ps_done"), sem("parts_done"), sem("ga_bias_done"), sem("biased")
        attn_done, proj_done, x1_done = sem("attn_done"), sem("proj_done"), sem("x1_done")
        stats_done = sem("stats_done")
        chain, var_done, root_done = sem("dve_chain"), sem("var_done"), sem("root_done")
        norm_done, mult_done, h_done, trans_done = sem("norm_done"), sem("mult_done"), sem("h_done"), sem("trans_done")
        h_out = [sem(f"h_out{i}") for i in range(2)]
        hT_done, gate_done, logits_done = sem("hT_done"), sem("gate_done"), sem("logits_done")
        hi_done, lo_done = sem("hi_done"), sem("lo_done")
        diff_done, exp_done = sem("diff_done"), sem("exp_done")
        zeroed, chosen_done, within_done = sem("zeroed"), sem("chosen_done"), sem("within_done")
        hot_done, by_part_done, lanes_done, inv_done = (sem("hot_done"), sem("by_part_done"),
                                                                 sem("lanes_done"), sem("inv_done"))
        by_place_done = sem("by_place_done")
        ga_bias = h[:].rearrange("p a t c -> p (a t) c")
        block = ctx.enter_context(nc.Block())
        sums, recips = io["sums"], io["recips"]
        h_rows = io["h_rows"].rearrange("(t p) c -> p t c", p=128)
        W_IN = 16 * 9

        hot = [a[:].bitcast(BF16)[:, 0:NT * 3 * NS].rearrange("p (t s n) -> p t s n", s=3, n=NS) for a in (pv, recip)]
        flat4 = lambda a: a[:].rearrange("p a t c -> p (a t c)")
        lanes = [a.bitcast(BF16).rearrange("p (t n) -> p t n", n=128)
                 for a in (flat4(norm), flat4(scaled), flat4(h), hT[:].rearrange("p a c -> p (a c)"))]

        @block.sync
        def _(sp):
            heads = sums.rearrange("(h r) n -> h r n", r=32)
            sp.dma_start(den[:], heads[:, DK, :]).then_inc(den_in, 16)
            for i in range(2):
                sp.dma_start(x1[:, NT // 2 * i:NT // 2 * (i + 1), :], io["x"][:, NT // 2 * i:NT // 2 * (i + 1), :]).then_inc(x_in, 16)
            for b in range(NB):
                sp.dma_start(pv[:, L * b:L * (b + 1)], heads[H * b:H * (b + 1), 0:DK, :]).then_inc(pv_in[b // 4], 16)
            sp.wait_ge(den_done, 1)
            sp.dma_start(recips, den[:]).then_inc(recip_out, 16)
            sp.wait_ge(recip_out, 16)
            for b in range(NB):
                sp.dma_start(recip[:, L * b:L * (b + 1)],
                             recips[H * b:H * (b + 1), None, :].broadcast_to([H, DK, L])).then_inc(recip_in[b // 4], 16)
            for e in range(E):
                for w, name in enumerate(("w1_T", "w3_T")):
                    sp.dma_start(w13[:, e, 2 + w, :].bitcast(F32), io[name][e]).then_inc(raw_in[e], 16)
                sp.dma_start(w2[:, e, :, D:2 * D].bitcast(F32), io["w2_T"][e]).then_inc(raw_in[e], 16)
            for b in range(NB):
                sp.wait_ge(h_done, b + 1)
                sp.dma_start(h_rows[:, TB * b:TB * (b + 1), :], h[:, b % 2, :, :]).then_inc(h_out[b % 2], 16)
            for i in range(2):
                sp.wait_ge(h_out[i], 16 * NB // 2)

        @block.scalar
        def _(act):
            for dst, name in ((wout, "wout"), (gate_w, "gate_T"), (number, "number"), (before_f, "before"),
                              (multiple, "multiple"), (partition, "partition"), (spare_row, "spare_row")):
                act.dma_start(dst[:], io[name]).then_inc(w_in, 16)
            act.dma_start(bias_out[:], io["bias_out"].partition_broadcast(128)).then_inc(w_in, 16)
            act.dma_start(rank[:].rearrange("p t e -> p (t e)"), io["rank"]).then_inc(w_in, 16)
            for b in range(NB):
                act.wait_ge(parts_ps_done, b + 1)
                nc.scalar.activation(parts[:, b, :, :].rearrange("p a c -> p (a c)"), ps[b][:], ACT.Copy).then_inc(parts_done, 1)
            for e in range(E):
                act.wait_ge(raw_in[e], 48)
                nc.scalar.activation(w13[:, e, 0:2, :], w13[:, e, 2:4, :].bitcast(F32), ACT.Copy).then_inc(hi_done, 1)
                nc.scalar.activation(w2[:, e, :, 0:D], w2[:, e, :, D:2 * D].bitcast(F32), ACT.Copy).then_inc(hi_done, 1)
            act.wait_ge(var_done, 1)
            nc.scalar.activation(root[:], var[:], ACT.Sqrt).then_inc(root_done, 1)

            def batch(b, par, first):
                act.wait_ge(trans_done, b + 1)
                if not first:
                    act.wait_ge(gate_done, b - 1)
                nc.scalar.activation(hT[:, par, :], trans_ps[par][:], ACT.Copy).then_inc(hT_done, 1)

            batch(0, 0, True)
            batch(1, 1, True)
            with act.Fori(1, NB // 2) as pair:
                for par in range(2):
                    batch(pair * 2 + par, par, False)
            for i in range(2):
                act.wait_ge(diff_done, i + 1)
                nc.scalar.activation(expd[i][:], diff[i][:], ACT.Exp).then_inc(exp_done, 1)
            for k in range(2):
                act.wait_ge(hot_done, k + 1)
                nc.scalar.activation(hot[k][:, :, 1, :], hot[k][:, :, 2, :], ACT.Copy, scale=partition[:]).then_inc(by_part_done, 1)

        @block.gpsimd
        def _(pool):
            for a in (*scan, *base, ones):
                last = nc.gpsimd.memset(a[:], 1.0 if a is ones else 0.0)
            last.then_inc(zeroed, 1)
            pool.wait_ge(ga_bias_done, 1)
            pool.wait_ge(x_in, 32)

            with pool.Fori(0, NB) as b:
                nc.gpsimd.tensor_tensor(x1[:, bass.ds(b * TB, TB), :], x1[:, bass.ds(b * TB, TB), :],
                                        ga_bias[:, bass.ds(b, 1), :].broadcast_to([128, TB, D]), ALU.add).then_inc(biased, 1)

            def low_parts(e):
                pool.wait_ge(hi_done, 2 * e + 2)
                nc.gpsimd.tensor_tensor(w13[:, e, 2:4, :], w13[:, e, 2:4, :].bitcast(F32),
                                        w13[:, e, 0:2, :].bitcast(F32), ALU.subtract).then_inc(lo_done, 1)
                nc.gpsimd.tensor_tensor(w2[:, e, :, D:2 * D], w2[:, e, :, D:2 * D].bitcast(F32),
                                        w2[:, e, :, 0:D].bitcast(F32), ALU.subtract).then_inc(lo_done, 1)

            for e in range(E // 2):
                low_parts(e)

            def times_scale(b, par):
                pool.wait_ge(norm_done, b + 1)
                nc.gpsimd.tensor_tensor(norm[:, par, :, :], norm[:, par, :, :],
                                        parts[:, bass.ds(b, 1), P_CB, :].broadcast_to([128, TB, D]), ALU.mult).then_inc(mult_done, 1)

            with pool.Fori(0, NB // 2) as pair:
                for par in range(2):
                    times_scale(pair * 2 + par, par)
            for e in range(E // 2, E):
                low_parts(e)

        @block.tensor
        def _(pe):
            for b in range(NB):
                for part in range(4):
                    last = nc.tensor.matmul(ps[b][:, part * D:(part + 1) * D], mod[:, GA + part, b:b + 1].broadcast_to([128, 128]),
                                            ident[:], start=True, stop=True)
                last.then_inc(parts_ps_done, 1)
            pe.wait_ge(w_in, W_IN)
            pe.wait_ge(parts_done, NB)

            def project(b, par, first):
                pe.wait_ge(attn_done, b + 1)
                if not first:
                    pe.wait_ge(x1_done, b - 1)
                for t in range(TB):
                    last = nc.tensor.matmul(proj_ps[par][:, t * D:(t + 1) * D], attn[:, par, t * 128:(t + 1) * 128], wout[:],
                                            start=True, stop=True)
                last.then_inc(proj_done, 1)

            def transpose_batch(b, par, first):
                pe.wait_ge(h_done, b + 1)
                if not first:
                    pe.wait_ge(hT_done, b - 1)
                for t in range(TB):
                    last = nc.tensor.transpose(trans_ps[par][:, t * 128:(t + 1) * 128], h[:, par, t, :], ident[:])
                last.then_inc(trans_done, 1)

            def gate(b, par, first):
                pe.wait_ge(hT_done, b + 1)
                if not first:
                    pe.wait_ge(logits_done, b - 1)
                for t in range(TB):
                    last = nc.tensor.matmul(gate_ps[par][:, t * E:(t + 1) * E], hT[:, par, t * 128:(t + 1) * 128], gate_w[:],
                                            start=True, stop=True)
                last.then_inc(gate_done, 1)

            def pairs(stages):
                for stage in stages:
                    for par in range(2):
                        stage(par, par, True)
                with pe.Fori(1, NB // 2) as pair:
                    for stage in stages:
                        for par in range(2):
                            stage(pair * 2 + par, par, False)

            pairs([project])
            pairs([transpose_batch, gate])
            pe.wait_ge(chosen_done, 1)
            nc.tensor.matmul(slot_ps[:, 0:NT * E], before[:], chosen[:], start=True, stop=True)
            nc.tensor.matmul(slot_ps[:, NT * E:2 * NT * E], ones[:], chosen[:], start=True, stop=True).then_inc(within_done, 1)
            for i in range(4):
                pe.wait_ge(by_part_done, i // 2 + 1)
                pe.wait_ge(by_place_done, i // 2 + 1)
                pe.wait_ge(lanes_done, i + 1)
                for j in range(16):
                    a = 16 * i + j
                    last = nc.tensor.matmul(inv_ps[:, 0:3 * NS], lanes[i][:, j, :], hot[a // NT][:, a % NT, :, :].rearrange("p s n -> p (s n)"),
                                            start=i == 0 and j == 0, stop=i == 3 and j == 15)
            last.then_inc(inv_done, 1)

        @block.vector
        def _(dve):
            n = [0]

            def step(ins):
                n[0] += 1
                ins.then_inc(chain, 1)
                dve.wait_ge(chain, n[0])

            dve.wait_ge(w_in, W_IN)
            nc.vector.tensor_copy(number_bf[:], number[:])
            nc.vector.tensor_copy(before[:], before_f[:])
            dve.wait_ge(parts_done, NB)
            nc.vector.tensor_tensor(ga_bias, parts[:, :, P_GA, :], bias_out[:, None, :].broadcast_to([128, NB, D]),
                                    ALU.mult).then_inc(ga_bias_done, 1)
            dve.wait_ge(den_in, 16)
            nc.vector.reciprocal(den[:], den[:]).then_inc(den_done, 1)

            def normalize_attention(b, par, first):
                cols = bass.ds(b * L, L)
                if not first:
                    dve.wait_ge(proj_done, b - 1)
                nc.vector.tensor_tensor(attn[:, par, :], pv[:, cols], recip[:, cols], ALU.mult).then_inc(attn_done, 1)

            def residual(b, par, step):
                tiles = bass.ds(b * TB, TB)
                dve.wait_ge(proj_done, b + 1)
                step(nc.vector.tensor_tensor(scaled[:, par, :, :], proj_ps[par][:].rearrange("p (t c) -> p t c", c=D),
                                             parts[:, bass.ds(b, 1), P_GA, :].broadcast_to([128, TB, D]), ALU.mult))
                dve.wait_ge(biased, b + 1)
                nc.vector.tensor_tensor(x1[:, tiles, :], scaled[:, par, :, :], x1[:, tiles, :], ALU.add).then_inc(x1_done, 1)
                dve.wait_ge(ga_bias_done, 1)
                dve.wait_ge(x1_done, b + 1)
                for t in range(TB):
                    last = nc.vector.bn_stats(stats[:, par, t, :], x1[:, bass.ds(b * TB + t, 1), :].rearrange("p a c -> p (a c)"))
                last.then_inc(stats_done, 1)
                dve.wait_ge(ga_bias_done, 1)
                dve.wait_ge(stats_done, b + 1)
                for t in range(TB):
                    last = nc.vector.bn_aggr(tile_mean_var[:, par, t, :], stats[:, par, t, :])
                step(last)
                step(nc.vector.tensor_copy(mean_var[:, tiles, :], tile_mean_var[:, par, :, :]))

            chained = n[0]
            PER = 3

            def counted(b):
                k = [0]

                def s(ins):
                    k[0] += 1
                    ins.then_inc(chain, 1)
                    dve.wait_ge(chain, b * PER + chained + k[0])
                return s

            for i in range(2):
                dve.wait_ge(pv_in[i], 16 * NB // 2)
                dve.wait_ge(recip_in[i], 16 * NB // 2)
                if i == 0:
                    for par in range(2):
                        normalize_attention(par, par, True)
                    with dve.Fori(0, NB // 4 - 1) as pair:
                        for par in range(2):
                            residual(pair * 2 + par, par, counted(pair * 2 + par))
                            normalize_attention(pair * 2 + 2 + par, par, False)
                else:
                    with dve.Fori(NB // 4 - 1, NB // 2 - 1) as pair:
                        for par in range(2):
                            residual(pair * 2 + par, par, counted(pair * 2 + par))
                            normalize_attention(pair * 2 + 2 + par, par, False)
            for b in (NB - 2, NB - 1):
                residual(b, b % 2, counted(b))
            n[0] = chained + PER * NB

            step(nc.vector.tensor_scalar(var[:], mean_var[:, :, 1], EPS, None, ALU.add))
            nc.vector.engine_nop().then_inc(var_done, 1)
            dve.wait_ge(root_done, 1)
            newton_rstd(nc, step, root[:], var[:], half[:])

            def normalize(b, par, first):
                if not first:
                    dve.wait_ge(h_done, b - 1)
                for t in range(TB):
                    tile = bass.ds(b * TB + t, 1)
                    last = nc.vector.tensor_scalar(norm[:, par, t, :], x1[:, tile, :].rearrange("p a c -> p (a c)"),
                                                   mean_var[:, tile, 0], root[:, tile], ALU.subtract, ALU.mult)
                last.then_inc(norm_done, 1)

            def add_shift(b, par, pair):
                dve.wait_ge(mult_done, b + 1)
                if pair is not None:
                    dve.wait_ge(h_out[par], pair * 16)
                    dve.wait_ge(trans_done, b - 1)
                nc.vector.tensor_tensor(h[:, par, :, :], norm[:, par, :, :],
                                        parts[:, bass.ds(b, 1), P_SB, :].broadcast_to([128, TB, D]), ALU.add).then_inc(h_done, 1)

            def copy_logits(b, par):
                dve.wait_ge(gate_done, b + 1)
                nc.vector.tensor_copy(logits[:, bass.ds(b * TB, TB), :].rearrange("p t e -> p (t e)"),
                                      gate_ps[par][:, 0:TB * E]).then_inc(logits_done, 1)

            for par in range(2):
                normalize(par, par, True)
            for par in range(2):
                add_shift(par, par, None)
            with dve.Fori(1, NB // 2) as pair:
                for par in range(2):
                    normalize(pair * 2 + par, par, False)
                for par in range(2):
                    copy_logits(pair * 2 - 2 + par, par)
                    add_shift(pair * 2 + par, par, pair)
            for b in (NB - 2, NB - 1):
                copy_logits(b, b % 2)
            dve.wait_ge(logits_done, NB)

            wide = lambda a: a[:][:, :, None].broadcast_to([128, NT, E])
            tt, ts = nc.vector.tensor_tensor, nc.vector.tensor_scalar

            def first_of(hot, values, m):
                step(nc.vector.reduce_max(m, values, AX.X))
                step(tt(tmp[:], values, wide(m), ALU.is_equal))
                step(tt(tmp[:], tmp[:], rank[:], ALU.mult))
                step(nc.vector.reduce_max(pick[:], tmp[:], AX.X))
                step(tt(hot, tmp[:], wide(pick), ALU.is_equal))

            first_of(one_hot[0][:], logits[:], top[0][:])
            step(nc.vector.scalar_tensor_tensor(tmp2[:], one_hot[0][:], -3e38, logits[:], ALU.mult, ALU.add))
            first_of(one_hot[1][:], tmp2[:], top[1][:])
            chosen3 = chosen[:].rearrange("p (t e) -> p t e", e=E)
            nc.vector.tensor_tensor(chosen3, one_hot[0][:], one_hot[1][:], ALU.add).then_inc(chosen_done, 1)
            step(tt(diff[0][:], logits[:], wide(top[0]), ALU.subtract))
            nc.vector.engine_nop().then_inc(diff_done, 1)
            step(tt(diff[1][:], logits[:], wide(top[1]), ALU.subtract))
            step(ts(diff[1][:], diff[1][:], 0.0, None, ALU.min))
            nc.vector.engine_nop().then_inc(diff_done, 1)

            dve.wait_ge(zeroed, 1)
            dve.wait_ge(within_done, 1)
            tiles_of = lambda i, shift: scan[i][:, PAD - shift:PAD - shift + NT, :]
            step(nc.vector.tensor_copy(tiles_of(0, 0), slot_ps[:, NT * E:2 * NT * E].rearrange("p (t e) -> p t e", e=E)))
            at = 0
            for k in range(5):
                step(tt(tiles_of(1 - at, 0), tiles_of(at, 0), tiles_of(at, 1 << k), ALU.add))
                at = 1 - at
            counts = scan[at][:, PAD + NT - 1, :]
            by_tile = cmp[:, 0:E * NT].rearrange("p (e t) -> p e t", t=NT)
            step(tt(by_tile, counts[:, :, None].broadcast_to([128, E, NT]), multiple[:, None, :].broadcast_to([128, E, NT]), ALU.is_gt))
            step(nc.vector.reduce_sum(base[0][:, E:2 * E], by_tile, AX.X))
            for k in range(3):
                step(tt(base[(k + 1) % 2][:, E:2 * E], base[k % 2][:, E:2 * E], base[k % 2][:, E - (1 << k):2 * E - (1 << k)], ALU.add))
            first_tile = base[1][:, E - 1:2 * E - 1]
            place = scan[1 - at][:, PAD:PAD + NT, :]
            step(tt(place, slot_ps[:, 0:NT * E].rearrange("p (t e) -> p t e", e=E), tiles_of(at, 1), ALU.add))
            step(nc.vector.scalar_tensor_tensor(place, first_tile[:, None, :].broadcast_to([128, NT, E]), 128.0, place, ALU.mult, ALU.add))
            for k in range(2):
                step(tt(tmp[:], one_hot[k][:], place, ALU.mult))
                step(nc.vector.reduce_sum(pos[:, NT * k:NT * (k + 1)], tmp[:], AX.X))
            step(nc.vector.tensor_copy(pos_int[:], pos[:]))
            step(ts(tile_int[:], pos_int[:], 7, None, ALU.arith_shift_right))
            step(ts(pos_int[:], pos_int[:], 127, None, ALU.bitwise_and))
            nc.vector.tensor_copy(tile_bf[:], tile_int[:])
            step(nc.vector.tensor_copy(lane_bf[:], pos_int[:]))
            
            def lane_one_hot(i):
                nc.vector.tensor_tensor(lanes[i], number_bf[:, None, :].broadcast_to([128, 16, 128]),
                                        lane_bf[:, 16 * i:16 * i + 16, None].broadcast_to([128, 16, 128]),
                                        ALU.is_equal).then_inc(lanes_done, 1)

            def tile_one_hot(k):
                nc.vector.tensor_tensor(hot[k][:, :, 2, :], number_bf[:, None, 0:NS].broadcast_to([128, NT, NS]),
                                        tile_bf[:, NT * k:NT * (k + 1), None].broadcast_to([128, NT, NS]),
                                        ALU.is_equal).then_inc(hot_done, 1)
                dve.wait_ge(hot_done, k + 1)
                nc.vector.tensor_tensor(hot[k][:, :, 0, :], hot[k][:, :, 2, :],
                                        number_bf[:, NT * k:NT * (k + 1), None].broadcast_to([128, NT, NS]),
                                        ALU.mult).then_inc(by_place_done, 1)

            tile_one_hot(0)
            lane_one_hot(0)
            lane_one_hot(1)
            tile_one_hot(1)
            for i in (0, 1):
                dve.wait_ge(h_out[i], 16 * NB // 2)
            lane_one_hot(2)
            lane_one_hot(3)
            e_cmp = cmp[0:1, :].rearrange("p (n e) -> p n e", e=E)
            step(tt(e_cmp, number[0:1, 0:NS, None].broadcast_to([1, NS, E]), first_tile[0:1, None, :].broadcast_to([1, NS, E]), ALU.is_ge))
            step(nc.vector.reduce_sum(ident_row[0:1, :], e_cmp, AX.X))
            step(ts(keep["expert_of"][:], ident_row[0:1, :], -1.0, None, ALU.add))

            step(nc.vector.scalar_tensor_tensor(tmp2[:], logits[:], -1.0, logits[:], ALU.mult, ALU.max))
            for i in range(2):
                step(tt(tmp[:], tmp2[:], wide(top[i]), ALU.max))
                step(nc.vector.reciprocal(tmp[:], tmp[:]))
                step(nc.vector.scalar_tensor_tensor(tmp[:], diff[i][:], -1.0, tmp[:], ALU.mult, ALU.mult))
                step(ts(tmp[:], tmp[:], 0.02, None, ALU.is_gt))
                if i:
                    step(tt(tmp[:], tmp[:], one_hot[0][:], ALU.max))
                step(ts(tmp[:], tmp[:], -1.0, 1.0, ALU.mult, ALU.add))
                dve.wait_ge(exp_done, i + 1)
                step(tt(tmp[:], tmp[:], expd[i][:], ALU.mult))
                step(nc.vector.reduce_sum(pick[:], tmp[:], AX.X))
                step(nc.vector.reciprocal(route_w[:, i, :], pick[:]))

            dve.wait_ge(inv_done, 1)
            step(nc.vector.tensor_copy(row_part[:], inv_ps[:, 0:3 * NS]))
            place_no, part_no, used = (row_part[:, NS * i:NS * (i + 1)] for i in range(3))
            step(nc.vector.scalar_tensor_tensor(ident_row[:], place_no, 128.0, part_no, ALU.mult, ALU.add))
            step(ts(place_no, ident_row[:], float(T), -float(T), ALU.is_ge, ALU.mult))
            step(tt(keep["src"][:], ident_row[:], place_no, ALU.add))
            step(ts(used, used, -1.0, 1.0, ALU.mult, ALU.add))
            step(tt(used, used, spare_row[:], ALU.mult))
            step(tt(keep["dst"][:], ident_row[:], used, ALU.add))


def expert_phase(nc, io, keep, out):
    ctx = ExitStack()
    with ctx:
        sb = lambda n, s, d=F32: ctx.enter_context(nc.sbuf_tensor("d_" + n, s, d))
        sem = lambda n: ctx.enter_context(nc.semaphore("d_" + n))
        ps = [ctx.enter_context(nc.psum_tensor(f"d_ps{i}", [128, 512], F32)) for i in range(8)]
        gate_ps, up_ps, y_ps, hT_ps, gT_ps = ps[0:2], ps[2:4], ps[4:6], ps[6], ps[7]
        ident, x1, parts, w13, w2 = (keep[n] for n in ("ident", "x1", "parts", "w13", "w2"))
        src, dst, expert_of, route_w = (keep[n] for n in ("src", "dst", "expert_of", "route_w"))
        P_GB = 3
        RING = 4
        src_now, dst_now = sb("src_now", [128, RING], U32), sb("dst_now", [128, RING], U32)
        h = sb("h", [128, RING, D])
        h_hi, h_lo = sb("h_hi", [128, 2, 128], F32R), sb("h_lo", [128, 2, 128], F32R)
        silu, g = sb("silu", [128, 2, FF]), sb("g", [128, 2, FF])
        g_hi, g_lo = sb("g_hi", [128, 2, FB, 128], F32R), sb("g_lo", [128, 2, FB, 128], F32R)
        y_low, y = sb("y_low", [128, 2, D]), sb("y", [128, RING, D])
        y_both = sb("y_both", [128, 2, NT, D])

        h_in = [sem(f"h_in{i}") for i in range(RING)]
        y_out = [sem(f"y_out{i}") for i in range(RING)]
        src_set, dst_set, waited = sem("src_set"), sem("dst_set"), sem("waited")
        hT_done, h_hi_done, h_lo_done = sem("hT_done"), sem("h_hi_done"), sem("h_lo_done")
        gate_done, up_done, silu_done, g_done = sem("gate_done"), sem("up_done"), sem("silu_done"), sem("g_done")
        gT_done, g_hi_done, g_lo_done = sem("gT_done"), sem("g_hi_done"), sem("g_lo_done")
        down_done, y_low_done, y_done = sem("down_done"), sem("y_low_done"), sem("y_done")
        both_in = [sem(f"both_in{i}") for i in range(4)]
        first_done, sum_done, gated, out_done, stored = (sem("first_done"), sem("sum_done"), sem("gated"), sem("out_done"), sem("stored"))
        block = ctx.enter_context(nc.Block())

        class Tile:
            def __init__(self, round_, slot):
                self.round, self.slot, self.par = round_, slot, slot % 2
                self.n = round_ * RING + slot
                self.fixed = isinstance(round_, int)

            def __add__(self, d):
                return Tile(self.round + (self.slot + d) // RING, (self.slot + d) % RING)

            def exists(self):
                return not self.fixed or 0 <= self.n < NS

            def past(self, k):
                return not self.fixed or self.n >= k

        def tiles(eng, step):
            for n in range(2 * RING):
                step(Tile(n // RING, n % RING))
            with eng.Fori(2, NS // RING - 1) as r:
                for slot in range(RING):
                    step(Tile(r, slot))
            for slot in range(RING):
                step(Tile(NS // RING - 1, slot))

        y_view = io["y_rows"][0:2 * T, :].rearrange("(k t p) c -> p k t c", k=2, p=128)
        TG = NT // 4

        @block.sync
        def _(sp):
            for i in range(RING):
                sp.wait_ge(y_out[i], 16 * NS // RING)
            for i in range(4):
                for k in range(2):
                    sp.dma_start(y_both[:, k, TG * i:TG * (i + 1), :], y_view[:, k, TG * i:TG * (i + 1), :]).then_inc(both_in[i], 16)
            for b in range(NB):
                sp.wait_ge(out_done, b + 1)
                sp.dma_start(out[:, TB * b:TB * (b + 1), :], x1[:, TB * b:TB * (b + 1), :]).then_inc(stored, 16)
            sp.wait_ge(stored, 16 * NB)

        @block.gpsimd
        def _(pool):
            def gather(i):
                nc.gpsimd.tensor_copy(src_now[:, i.slot:i.slot + 1], src[:, bass.ds(i.n, 1)]).then_inc(src_set, 1)
                pool.wait_ge(src_set, i.n + 1)
                pool.sem_inc(waited, 1)
                pool.indirect_dma_start(h[:, i.slot, :], None, io["h_rows"],
                                        bass.IndirectOffsetOnAxis(ap=src_now[:, i.slot:i.slot + 1], axis=0)).then_inc(h_in[i.slot], 16)

            def scatter(i):
                if i.past(RING):
                    pool.wait_ge(y_out[i.slot], i.round * 16)
                nc.gpsimd.tensor_copy(dst_now[:, i.slot:i.slot + 1], dst[:, bass.ds(i.n, 1)]).then_inc(dst_set, 1)
                pool.wait_ge(y_done, i.n + 1)
                pool.wait_ge(dst_set, i.n + 1)
                pool.sem_inc(waited, 1)
                pool.indirect_dma_start(io["y_rows"], bass.IndirectOffsetOnAxis(ap=dst_now[:, i.slot:i.slot + 1], axis=0),
                                        y[:, i.slot, :], None).then_inc(y_out[i.slot], 16)

            for slot in range(RING):
                gather(Tile(0, slot))

            def step(i):
                if (i + RING).exists():
                    pool.wait_ge(hT_done, i.n + 1)
                    gather(i + RING)
                if (i + -3).exists():
                    scatter(i + -3)

            tiles(pool, step)
            for d in (1, 2, 3):
                scatter(Tile(NS // RING - 1, d))

            for b in range(NB):
                pool.wait_ge(sum_done, TB * (b + 1))
                now = y_both[:, 0, TB * b:TB * (b + 1), :]
                nc.gpsimd.tensor_tensor(now, now, parts[:, b:b + 1, P_GB, :].broadcast_to([128, TB, D]), ALU.mult).then_inc(gated, 1)

        @block.tensor
        def _(pe):
            def transpose_h(i):
                pe.wait_ge(h_in[i.slot], i.round * 16 + 16)
                if i.past(1):
                    pe.wait_ge(h_lo_done, i.n)
                nc.tensor.transpose(hT_ps[:, 0:128], h[:, i.slot, :], ident[:]).then_inc(hT_done, 1)

            def up(i):
                e = pe.value_load(expert_of[0:1, bass.ds(i.n, 1)], min_val=0, max_val=E - 1)
                pe.wait_ge(h_lo_done, i.n + 1)
                if i.past(2):
                    pe.wait_ge(g_done, i.n - 1)
                weights = lambda w: w13[:, bass.ds(e, 1), w, :].rearrange("p a n -> p (a n)")
                hi, lo = h_hi[:, i.par, :], h_lo[:, i.par, :]
                for w, (acc, done) in enumerate(((gate_ps, gate_done), (up_ps, up_done))):
                    nc.tensor.matmul(acc[i.par][:], hi, weights(w), start=True, stop=False)
                    nc.tensor.matmul(acc[i.par][:], hi, weights(2 + w), start=False, stop=False)
                    nc.tensor.matmul(acc[i.par][:], lo, weights(w), start=False, stop=True).then_inc(done, 1)

            def transpose_g(i):
                pe.wait_ge(g_done, i.n + 1)
                if i.past(1):
                    pe.wait_ge(g_lo_done, i.n)
                for fb in range(FB):
                    last = nc.tensor.transpose(gT_ps[:, fb * 128:(fb + 1) * 128], g[:, i.par, fb * 128:(fb + 1) * 128], ident[:])
                last.then_inc(gT_done, 1)

            def down(i):
                e = pe.value_load(expert_of[0:1, bass.ds(i.n, 1)], min_val=0, max_val=E - 1)
                pe.wait_ge(g_lo_done, i.n + 1)
                if i.past(2):
                    pe.wait_ge(y_done, i.n - 1)
                for fb in range(FB):
                    both = w2[:, bass.ds(e, 1), fb, :].rearrange("p a n -> p (a n)")
                    high = w2[:, bass.ds(e, 1), fb, 0:D].rearrange("p a n -> p (a n)")
                    if fb == 0:
                        nc.tensor.matmul(y_ps[i.par][:, 0:2 * D], g_hi[:, i.par, fb, :], both, start=True, stop=False)
                    nc.tensor.matmul(y_ps[i.par][:, 0:D], g_lo[:, i.par, fb, :], high, start=False, stop=False)
                    if fb > 0:
                        last = nc.tensor.matmul(y_ps[i.par][:, 0:2 * D], g_hi[:, i.par, fb, :], both, start=False, stop=fb == FB - 1)
                last.then_inc(down_done, 1)

            transpose_h(Tile(0, 0))

            def step(i):
                if (i + 1).exists():
                    transpose_h(i + 1)
                up(i)
                if (i + -2).exists():
                    down(i + -2)
                if (i + -1).exists():
                    transpose_g(i + -1)

            tiles(pe, step)
            last_tile = Tile(NS // RING - 1, RING - 1)
            down(last_tile + -1)
            transpose_g(last_tile)
            down(last_tile)

        @block.scalar
        def _(act):
            def high_h(i):
                act.wait_ge(hT_done, i.n + 1)
                if i.past(2):
                    act.wait_ge(up_done, i.n - 1)
                nc.scalar.activation(h_hi[:, i.par, :], hT_ps[:, 0:128], ACT.Copy).then_inc(h_hi_done, 1)

            def gate(i):
                act.wait_ge(gate_done, i.n + 1)
                if i.past(2):
                    act.wait_ge(g_done, i.n - 1)
                nc.scalar.activation(silu[:, i.par, :], gate_ps[i.par][:], ACT.Silu).then_inc(silu_done, 1)

            def high_g(i):
                act.wait_ge(gT_done, i.n + 1)
                if i.past(2):
                    act.wait_ge(down_done, i.n - 1)
                nc.scalar.activation(g_hi[:, i.par, :, :].rearrange("p a c -> p (a c)"), gT_ps[:], ACT.Copy).then_inc(g_hi_done, 1)

            def low_y(i):
                act.wait_ge(down_done, i.n + 1)
                if i.past(2):
                    act.wait_ge(y_done, i.n - 1)
                nc.scalar.activation(y_low[:, i.par, :], y_ps[i.par][:, D:2 * D], ACT.Copy).then_inc(y_low_done, 1)

            high_h(Tile(0, 0))

            def step(i):
                if (i + 1).exists():
                    high_h(i + 1)
                gate(i)
                if (i + -2).exists():
                    low_y(i + -2)
                if (i + -1).exists():
                    high_g(i + -1)

            tiles(act, step)
            last_tile = Tile(NS // RING - 1, RING - 1)
            low_y(last_tile + -1)
            high_g(last_tile)
            low_y(last_tile)
            for i in range(4):
                act.wait_ge(both_in[i], 32)
                with act.Fori(TG * i, TG * (i + 1)) as t:
                    row = y_both[:, 0, bass.ds(t, 1), :].rearrange("p a c -> p (a c)")
                    nc.scalar.activation(row, row, ACT.Copy, scale=route_w[:, 0, bass.ds(t, 1)]).then_inc(first_done, 1)

        @block.vector
        def _(dve):
            def low_h(i):
                dve.wait_ge(h_hi_done, i.n + 1)
                if i.past(2):
                    dve.wait_ge(up_done, i.n - 1)
                nc.vector.tensor_tensor(h_lo[:, i.par, :], hT_ps[:, 0:128], h_hi[:, i.par, :].bitcast(F32),
                                        ALU.subtract).then_inc(h_lo_done, 1)

            def multiply(i):
                dve.wait_ge(silu_done, i.n + 1)
                dve.wait_ge(up_done, i.n + 1)
                if i.past(2):
                    dve.wait_ge(gT_done, i.n - 1)
                nc.vector.tensor_tensor(g[:, i.par, :], silu[:, i.par, :], up_ps[i.par][:], ALU.mult).then_inc(g_done, 1)

            def low_g(i):
                dve.wait_ge(g_hi_done, i.n + 1)
                if i.past(2):
                    dve.wait_ge(down_done, i.n - 1)
                nc.vector.tensor_tensor(g_lo[:, i.par, :, :].rearrange("p a c -> p (a c)"), gT_ps[:],
                                        g_hi[:, i.par, :, :].rearrange("p a c -> p (a c)").bitcast(F32),
                                        ALU.subtract).then_inc(g_lo_done, 1)

            def add_y(i):
                dve.wait_ge(y_low_done, i.n + 1)
                if i.past(RING):
                    dve.wait_ge(y_out[i.slot], i.round * 16)
                nc.vector.tensor_tensor(y[:, i.slot, :], y_ps[i.par][:, 0:D], y_low[:, i.par, :], ALU.add).then_inc(y_done, 1)

            low_h(Tile(0, 0))

            def step(i):
                if (i + 1).exists():
                    low_h(i + 1)
                multiply(i)
                if (i + -2).exists():
                    add_y(i + -2)
                if (i + -1).exists():
                    low_g(i + -1)

            tiles(dve, step)
            last_tile = Tile(NS // RING - 1, RING - 1)
            add_y(last_tile + -1)
            low_g(last_tile)
            add_y(last_tile)

            def weigh(b):
                with dve.Fori(TB * b, TB * (b + 1)) as t:
                    dve.wait_ge(first_done, t + 1)
                    rows = [y_both[:, k, bass.ds(t, 1), :].rearrange("p a c -> p (a c)") for k in range(2)]
                    nc.vector.scalar_tensor_tensor(rows[0], rows[1], route_w[:, 1, bass.ds(t, 1)], rows[0],
                                                   ALU.mult, ALU.add).then_inc(sum_done, 1)

            def residual(b):
                dve.wait_ge(gated, b + 1)
                now = slice(TB * b, TB * (b + 1))
                nc.vector.tensor_tensor(x1[:, now, :], x1[:, now, :], y_both[:, 0, now, :], ALU.add).then_inc(out_done, 1)

            weigh(0)
            for b in range(1, NB):
                weigh(b)
                residual(b - 1)
            residual(NB - 1)


def build(nc, io, out):
    io["sums"] = nc.dram_tensor("sums", (NB * G * 128, L), F32, kind="Internal").ap()
    io["recips"] = nc.dram_tensor("recips", (NB * H, L), F32, kind="Internal").ap()
    io["h_rows"] = nc.dram_tensor("h_rows", (T, D), F32, kind="Internal").ap()
    io["y_rows"] = nc.dram_tensor("y_rows", (2 * T + SLOTS, D), F32, kind="Internal").ap()
    ctx = ExitStack()
    with ctx:
        sb = lambda n, s, d=F32: ctx.enter_context(nc.sbuf_tensor(n, s, d))
        keep = dict(mod=sb("mod", [128, 6, NB]), ident=sb("ident", [128, 128]))
        with ExitStack() as attn:
            ab = lambda n, s, d=F32: attn.enter_context(nc.sbuf_tensor(n, s, d))
            for n in ("q_hi", "q_lo", "k_hi", "k_lo"):
                keep[n] = ab(n, [128, T])
            keep["q_bf"], keep["k_bf"] = ab("q_bf", [128, T], BF16), ab("k_bf", [128, T], BF16)
            keep["v_all"] = ab("v_all", [128, NT, D])
            keep["q_own"] = ab("q_own", [128, G, HG, L], BF16)
            keep["q_pack"] = ab("q_pack", [128, 2, L], F32R)
            keep["k_pack"] = ab("k_pack", [128, 2, L])
            keep["v_aug"] = ab("v_aug", [128, 2, TB, HG, 32])
            keep["head_mask"] = ab("head_mask", [128, HG])
            qkv_phase(nc, io, keep)
            if io.get("stop") == 1:
                return
            attention_phase(nc, io, keep)
            if io.get("stop") == 2:
                return
        keep.update(x1=sb("x1", [128, NT, D]), parts=sb("parts", [128, NB, 4, D]),
                    w13=sb("w13", [128, E, 4, FF], F32R), w2=sb("w2", [128, E, FB, 2 * D], F32R),
                    src=sb("src", [128, NS], U32), dst=sb("dst", [128, NS], U32), expert_of=sb("expert_of", [1, NS], I32),
                    route_w=sb("route_w", [128, 2, NT]))
        route_phase(nc, io, keep)
        if io.get("stop") == 3:
            return
        expert_phase(nc, io, keep, out)


def layouts(inputs):
    import numpy as np

    a = {k: np.asarray(v) for k, v in inputs.items()}
    rows = lambda m: np.ascontiguousarray(m.reshape(NT, 128, D).transpose(1, 0, 2))
    head_of = (np.arange(128) % S_ROW) // DK
    arrays = {
        "x": np.ascontiguousarray(a["L0_attn_x"]).reshape(T, D),
        "c_T": np.ascontiguousarray(a["L0_c"].T),
        "wmod": a["L0_wmod"],
        "wqkv": a["L0_attn_W_qkv"],
        "bias_qk": np.ascontiguousarray(a["L0_attn_b_qkv"][0:2 * D].reshape(2, D).T),
        "bias_v": np.ascontiguousarray(a["L0_attn_b_qkv"][2 * D:3 * D]),
        "wout": a["L0_attn_W_out"],
        "bias_out": a["L0_attn_b_out"],
        "gate_T": np.ascontiguousarray(a["L0_ffn_gate_w"].T),
        "w1_T": np.ascontiguousarray(a["L0_ffn_w1"].transpose(0, 2, 1)),
        "w3_T": np.ascontiguousarray(a["L0_ffn_w3"].transpose(0, 2, 1)),
        "w2_T": np.ascontiguousarray(a["L0_ffn_w2"].transpose(0, 2, 1).reshape(E, FB, 128, D).transpose(0, 2, 1, 3)),
        "ident": np.eye(128, dtype=np.float32),
        "above": (np.triu(np.ones((128, 128)), 1) * -BIG).astype(np.float32),
        "head_mask": (head_of[:, None] == np.arange(HG)[None, :]).astype(np.float32),
        "one_rows": ((np.arange(128) < S_ROW) & (np.arange(128) % DK == 0)).astype(np.float32)[:, None],
        "before": np.triu(np.ones((128, 128), np.float32), 1),
        "number": np.arange(128, dtype=np.float32)[None, :].repeat(128, 0),
        "multiple": (128 * np.arange(NT, dtype=np.float32))[None, :].repeat(128, 0),
        "partition": np.arange(128, dtype=np.float32)[:, None],
        "spare_row": (2 * T + np.arange(SLOTS, dtype=np.float32)).reshape(NS, 128).T.copy(),
        "rank": np.tile(np.arange(E, 0, -1, dtype=np.float32), NT)[None, :].repeat(128, 0),
    }
    return arrays


def kernel(**inputs):
    import numpy as np
    import concourse.bacc as bacc
    from concourse.bass_utils import run_bass_kernel_spmd

    nc = bacc.Bacc("TRN2", target_bir_lowering=False, num_devices=1)
    arrays = layouts(inputs)
    io = {n: nc.dram_tensor("in_" + n, v.shape, mybir.dt.from_np(v.dtype), kind="ExternalInput").ap() for n, v in arrays.items()}
    io["x"] = io["x"].rearrange("(t p) c -> p t c", p=128)
    out = nc.dram_tensor("out_x", (T, D), F32, kind="ExternalOutput").ap()
    build(nc, io, out.rearrange("(t p) c -> p t c", p=128))
    r = run_bass_kernel_spmd(nc, [{"in_" + n: v for n, v in arrays.items()}], core_ids=[0])
    return r.results[0]["out_x"].reshape(NB, L, D)
```

```python
import concourse.bass as bass
from concourse import mybir
from contextlib import ExitStack

F32 = mybir.dt.float32
F32R = mybir.dt.float32r
BF16 = mybir.dt.bfloat16
I32, U32 = mybir.dt.int32, mybir.dt.uint32
ALU = mybir.AluOpType
ACT = mybir.ActivationFunctionType
AX = mybir.AxisListType

NB, L, D = 8, 512, 128
H, DK = 16, 8
T = NB * L
TB = L // 128
NT = T // 128
G, HG = 4, 4
E, FF = 8, 512
FB = FF // 128
NS = 2 * NT + E
SLOTS = NS * 128
EPS = 1e-5
SA, CA, GA, SB_, CB, GB = range(6)
BIG = 1e30
S_ROW = HG * DK
CONSTS, CONST_COLS = {}, 0
for _name, _cols in (("wout", D), ("gate_T", E), ("number", 128), ("before", 128), ("multiple", NT), ("partition", 1), ("bias_v", 1),
                     ("spare_row", NS), ("rank", NT * E)):
    CONSTS[_name] = (CONST_COLS, _cols)
    CONST_COLS += _cols


def clamp_gate(nc, dve, step, gate, sign, mag):
    step(nc.vector.tensor_scalar(sign, gate, 0.0, 2.0, ALU.is_ge, ALU.mult))
    step(nc.vector.tensor_scalar(mag, gate, -1.0, None, ALU.mult))
    step(nc.vector.tensor_tensor(mag, mag, gate, ALU.max))
    step(nc.vector.tensor_scalar(mag, mag, 0.25, None, ALU.max))
    step(nc.vector.scalar_tensor_tensor(gate, sign, -1.0, mag, ALU.add, ALU.mult))


def newton_rstd(nc, step, root, var, half):
    step(nc.vector.reciprocal(root, root))
    step(nc.vector.tensor_tensor(half, root, root, ALU.mult))
    step(nc.vector.tensor_tensor(half, half, var, ALU.mult))
    step(nc.vector.tensor_scalar(half, half, -0.5, 1.5, ALU.mult, ALU.add))
    step(nc.vector.tensor_tensor(root, root, half, ALU.mult))


def qkv_phase(nc, io, keep):
    ctx = ExitStack()
    with ctx:
        sb = lambda n, s, d=F32: ctx.enter_context(nc.sbuf_tensor("a_" + n, s, d))
        sem = lambda n: ctx.enter_context(nc.semaphore("a_" + n))
        ps = [ctx.enter_context(nc.psum_tensor(f"a_ps{i}", [128, 512], F32)) for i in range(8)]
        trans_ps, q_ps, k_ps, v_ps = ps[0:2], ps[2:4], ps[4:6], ps[6:8]
        mod, ident = keep["mod"], keep["ident"]
        csil = sb("csil", [128, NB])
        q_hi, q_lo, k_hi, k_lo = (keep[n] for n in ("q_hi", "q_lo", "k_hi", "k_lo"))
        q_bf, k_bf, v_all = keep["q_bf"], keep["k_bf"], keep["v_all"]
        x = sb("x", [128, NT, D])
        norm = sb("norm", [128, 2, TB, D])
        stats = sb("stats", [128, 2 * TB, 6])
        mean_var = sb("mean_var", [128, NT, 2])
        var, root, half = sb("var", [128, NT]), sb("root", [128, NT]), sb("half", [128, NT])
        hT = sb("hT", [128, 2, L])
        wqkv, wmod = sb("wqkv", [128, 3 * D]), sb("wmod", [128, 6 * D])
        c_T = sb("c_T", [128, NB])
        bias_qk = sb("bias_qk", [128, 2])
        sign, mag = sb("sign", [128, NB]), sb("mag", [128, NB])

        x_in = [sem(f"x_in{i}") for i in range(NB // 2)]
        w_in, c_in = sem("w_in"), sem("c_in")
        silu_done, mod_done, mod_copied = sem("silu_done"), sem("mod_done"), sem("mod_copied")
        chain = sem("dve_chain")
        stats_done, var_done, root_done, norm_done = sem("stats_done"), sem("var_done"), sem("root_done"), sem("norm_done")
        aggr_done, v_copied = sem("aggr_done"), sem("v_copied")
        trans_done, hT_done = sem("trans_done"), sem("hT_done")
        q_done, k_done, v_done = sem("q_done"), sem("k_done"), sem("v_done")
        hi_done, lo_done = sem("hi_done"), sem("lo_done")
        set_in, zeroed = sem("set_in"), sem("zeroed")
        one_rows = sb("one_rows", [128, 1])
        block = ctx.enter_context(nc.Block())

        @block.gpsimd
        def _(pool):
            v_aug = keep["v_aug"]
            pool.dma_start(keep["head_mask"][:], io["head_mask"]).then_inc(set_in, 16)
            pool.dma_start(one_rows[:], io["one_rows"]).then_inc(set_in, 16)
            nc.gpsimd.memset(keep["q_own"][:].bitcast(F32), 0.0)
            nc.gpsimd.memset(keep["q_pack"][:].bitcast(F32), 0.0)
            for part, value in ((slice(0, DK), 0.0), (slice(DK, 2 * DK), 1.0), (slice(2 * DK, 32), 0.0)):
                nc.gpsimd.memset(v_aug[:, :, :, :, part].rearrange("p a t j d -> p (a t j) d"), value)
            nc.gpsimd.memset(keep["k_pack"][:], 0.0).then_inc(zeroed, 1)
            pool.wait_ge(set_in, 32)
            pool.wait_ge(zeroed, 1)
            nc.gpsimd.tensor_scalar(keep["k_pack"][:].rearrange("p a n -> p (a n)"),
                                    keep["k_pack"][:].rearrange("p a n -> p (a n)"), one_rows[:], None, ALU.add)
            with pool.Fori(0, NB) as b:
                pool.wait_ge(hi_done, b * 2 + 1)
                nc.gpsimd.tensor_copy(q_bf[:, bass.ds(b * L, L)], q_hi[:, bass.ds(b * L, L)])

        @block.sync
        def _(sp):
            for i in range(NB // 2):
                tiles = slice(2 * TB * i, 2 * TB * (i + 1))
                sp.dma_start(x[:, tiles, :], io["x"][:, tiles, :]).then_inc(x_in[i], 16)

        @block.scalar
        def _(act):
            act.dma_start(c_T[:], io["c_T"]).then_inc(c_in, 16)
            act.dma_start(wmod[:], io["wmod"]).then_inc(c_in, 16)
            act.dma_start(wqkv[:], io["wqkv"]).then_inc(w_in, 16)
            act.dma_start(bias_qk[:], io["bias_qk"]).then_inc(w_in, 16)
            act.dma_start(ident[:], io["ident"]).then_inc(w_in, 16)
            act.wait_ge(c_in, 32)
            nc.scalar.activation(csil[:], c_T[:], ACT.Silu).then_inc(silu_done, 1)

            def square_root(i):
                tiles = slice(2 * TB * i, 2 * TB * (i + 1))
                act.wait_ge(var_done, i + 1)
                nc.scalar.activation(root[:, tiles], var[:, tiles], ACT.Sqrt).then_inc(root_done, 1)

            square_root(0)
            act.wait_ge(mod_copied, 1)
            act.wait_ge(w_in, 48)

            def modulate(b):
                act.wait_ge(trans_done, b + 1)
                if b >= 2:
                    act.wait_ge(v_done, b - 1)
                nc.scalar.activation(hT[:, b % 2, :], trans_ps[b % 2][:], ACT.Identity,
                                     bias=mod[:, SA, b:b + 1], scale=mod[:, CA, b:b + 1]).then_inc(hT_done, 1)

            modulate(0)
            modulate(1)
            square_root(1)
            for b in range(NB):
                par, cols = b % 2, slice(b * L, (b + 1) * L)
                act.wait_ge(q_done, b + 1)
                nc.scalar.activation(q_hi[:, cols].bitcast(F32R), q_ps[par][:], ACT.Identity,
                                     bias=bias_qk[:, 0:1]).then_inc(hi_done, 1)
                act.wait_ge(k_done, b + 1)
                nc.scalar.activation(k_hi[:, cols].bitcast(F32R), k_ps[par][:], ACT.Identity,
                                     bias=bias_qk[:, 1:2]).then_inc(hi_done, 1)
                if b in (1, 3):
                    square_root(b // 2 + 2)
                if b + 2 < NB:
                    modulate(b + 2)
                act.wait_ge(hi_done, 2 * b + 2)
                nc.scalar.activation(k_bf[:, cols], k_hi[:, cols], ACT.Copy)
                act.wait_ge(v_done, b + 1)
                nc.scalar.activation(v_all[:, TB * b:TB * (b + 1), :].rearrange("p t c -> p (t c)"), v_ps[par][:],
                                     ACT.Copy).then_inc(v_copied, 1)

        @block.vector
        def _(dve):
            n = [0]

            def step(ins):
                n[0] += 1
                ins.then_inc(chain, 1)
                dve.wait_ge(chain, n[0])

            def statistics(i):
                tiles = slice(2 * TB * i, 2 * TB * (i + 1))
                dve.wait_ge(x_in[i], 16)
                if i:
                    dve.wait_ge(aggr_done, i)
                for t in range(2 * TB):
                    last = nc.vector.bn_stats(stats[:, t, :], x[:, 2 * TB * i + t, :])
                last.then_inc(stats_done, 1)
                dve.wait_ge(stats_done, i + 1)
                for t in range(2 * TB):
                    last = nc.vector.bn_aggr(mean_var[:, 2 * TB * i + t, :], stats[:, t, :])
                last.then_inc(aggr_done, 1)
                dve.wait_ge(aggr_done, i + 1)
                nc.vector.tensor_scalar(var[:, tiles], mean_var[:, tiles, 1], EPS, None, ALU.add).then_inc(var_done, 1)

            def inverse_root(i):
                tiles = slice(2 * TB * i, 2 * TB * (i + 1))
                dve.wait_ge(root_done, i + 1)
                newton_rstd(nc, step, root[:, tiles], var[:, tiles], half[:, tiles])

            def normalize(b):
                if b >= 2:
                    dve.wait_ge(trans_done, b - 1)
                for t in range(TB):
                    at = b * TB + t
                    last = nc.vector.tensor_scalar(norm[:, b % 2, t, :], x[:, at, :], mean_var[:, at, 0:1], root[:, at:at + 1],
                                                   ALU.subtract, ALU.mult)
                last.then_inc(norm_done, 1)

            def batch(b):
                par, cols = b % 2, slice(b * L, (b + 1) * L)
                dve.wait_ge(hi_done, 2 * b + 1)
                nc.vector.scalar_tensor_tensor(q_lo[:, cols].bitcast(F32R), q_ps[par][:], bias_qk[:, 0:1],
                                               q_hi[:, cols], ALU.add, ALU.subtract)
                dve.wait_ge(hi_done, 2 * b + 2)
                nc.vector.scalar_tensor_tensor(k_lo[:, cols].bitcast(F32R), k_ps[par][:], bias_qk[:, 1:2],
                                               k_hi[:, cols], ALU.add, ALU.subtract).then_inc(lo_done, 1)

            statistics(0)
            dve.wait_ge(mod_done, 1)
            step(nc.vector.tensor_copy(mod[:].rearrange("p a b -> p (a b)"), ps[7][:, 0:6 * NB]))
            step(nc.vector.tensor_scalar(mod[:, CA, :], mod[:, CA, :], 1.0, None, ALU.add))
            nc.vector.engine_nop().then_inc(mod_copied, 1)
            inverse_root(0)
            normalize(0)
            normalize(1)
            statistics(1)
            step(nc.vector.tensor_scalar(mod[:, CB, :], mod[:, CB, :], 1.0, None, ALU.add))
            clamp_gate(nc, dve, step, mod[:, GA, :], sign[:], mag[:])
            clamp_gate(nc, dve, step, mod[:, GB, :], sign[:], mag[:])
            dve.wait_ge(w_in, 48)
            inverse_root(1)
            for b in range(NB):
                if b + 2 < NB:
                    normalize(b + 2)
                batch(b)
                if b in (0, 2):
                    statistics(b // 2 + 2)
                if b in (1, 3):
                    inverse_root(b // 2 + 2)

        @block.tensor
        def _(pe):
            pe.wait_ge(silu_done, 1)
            for part in range(6):
                last = nc.tensor.matmul(ps[7][:, part * NB:(part + 1) * NB], wmod[:, part * D:(part + 1) * D],
                                        csil[:], start=True, stop=True)
            last.then_inc(mod_done, 1)
            pe.wait_ge(w_in, 48)
            pe.wait_ge(mod_copied, 1)

            def transpose_batch(b, par, first):
                pe.wait_ge(norm_done, b + 1)
                if not first:
                    pe.wait_ge(hT_done, b - 1)
                for t in range(TB):
                    last = nc.tensor.transpose(trans_ps[par][:, t * 128:(t + 1) * 128],
                                               norm[:, par, t, :], ident[:])
                last.then_inc(trans_done, 1)

            def project_batch(b, par, first):
                pe.wait_ge(hT_done, b + 1)
                if not first:
                    pe.wait_ge(lo_done, b - 1)
                    pe.wait_ge(v_copied, b - 1)
                nc.tensor.matmul(q_ps[par][:], wqkv[:, 0:D], hT[:, par, :], start=True, stop=True).then_inc(q_done, 1)
                nc.tensor.matmul(k_ps[par][:], wqkv[:, D:2 * D], hT[:, par, :], start=True, stop=True).then_inc(k_done, 1)
                for t in range(TB):
                    last = nc.tensor.matmul(v_ps[par][:, t * D:(t + 1) * D], hT[:, par, t * 128:(t + 1) * 128],
                                            wqkv[:, 2 * D:3 * D], start=True, stop=True)
                last.then_inc(v_done, 1)

            transpose_batch(0, 0, True)
            transpose_batch(1, 1, True)
            for b in range(2):
                project_batch(b, b, True)
                transpose_batch(b + 2, b, False)
            with pe.Fori(1, NB // 2 - 1) as pair:
                for par in range(2):
                    project_batch(pair * 2 + par, par, False)
                    transpose_batch(pair * 2 + 2 + par, par, False)
            for b in range(NB - 2, NB):
                project_batch(b, b % 2, False)


FILLS = [f for a in (0, 2) for f in (
    [(a, 3, 0)], [(a, 2, 0), (a, 0, 384)],
    [(a + 1, 3, 0)], [(a + 1, 2, 0), (a + 1, 0, 384)],
    [(a, 1, 0), (a + 1, 1, 256)])]
NF = len(FILLS)
KEY_COLS = {0: (0, 512), 1: (512, 384), 3: (896, 128)}
PAIR = 2560


SLOT_ORDER = "s0 t s1 f2 w0 f2 w1 f1 w2 w3 f2 s2 f1 s3 f2".split()
OWN_AT = (0, 2, 5, 8)


def attention_phase(nc, io, keep):
    ctx = ExitStack()
    with ctx:
        sb = lambda n, s, d=F32: ctx.enter_context(nc.sbuf_tensor("b_" + n, s, d))
        sem = lambda n: ctx.enter_context(nc.semaphore("b_" + n))
        pb = lambda n, w: ctx.enter_context(nc.psum_tensor("b_" + n, [128, w], F32))
        q_hi, q_lo, k_hi, k_lo = (keep[n] for n in ("q_hi", "q_lo", "k_hi", "k_lo"))
        q_bf, k_bf, v_all, ident = keep["q_bf"], keep["k_bf"], keep["v_all"], keep["ident"]
        q_own, q_pack, k_pack, v_aug = keep["q_own"], keep["q_pack"], keep["k_pack"], keep["v_aug"]
        head_mask, sums, den = keep["head_mask"], io["sums"], keep["den"]
        den_in, den_done, recip_out = sem("den_in"), sem("den_done"), sem("recip_out")
        k_own = sb("k_own", [128, 2, HG, L], F32R)
        probs = sb("probs", [128, 2, 2, PAIR])
        out_T = keep["out_T"]
        neg_max = sb("neg_max", [HG, 2, L])
        row_max = sb("row_max", [128, 2, TB, HG])
        above_f = sb("above_f", [128, 128])
        ident_bf, above = sb("ident_bf", [128, 128], BF16), sb("above", [128, 128], BF16)
        ab_ps, c_ps, o_ps = pb("ab_ps", 2048), pb("c_ps", 512), pb("o_ps", 512)
        max_ps = [pb("max_ps0", 512), pb("max_ps1", 512)]

        const_in, const_cast, waited = sem("const_in"), sem("const_cast"), sem("waited")
        k_in = [sem(f"k_in{i}") for i in range(2)]
        q_in = [sem(f"q_in{i}") for i in range(2)]
        sums_out = keep["sums_out"]
        q_own_done, fill_done, red_done = sem("q_own_done"), sem("fill_done"), sem("red_done")
        max_T_done, neg_done = sem("max_T_done"), sem("neg_done")
        own_pool, own_act = sem("own_pool"), sem("own_act")
        ab_done, c_done, exp_ab, exp_c = sem("ab_done"), sem("c_done"), sem("exp_ab"), sem("exp_c")
        masked, v_done, pv_done, o_copied = sem("masked"), sem("v_done"), sem("pv_done"), sem("o_copied")
        block = ctx.enter_context(nc.Block())

        U = NB * G
        PRO_FILLS = 2 * NF

        def batches(eng, slot):
            for g in range(G):
                slot(0, g, g)
            with eng.Fori(1, NB - 1) as b:
                for g in range(G):
                    slot(b, g, b * G + g)
            for g in range(G):
                slot(NB - 1, g, (NB - 1) * G + g)

        def ahead(u, n):
            return not isinstance(u, int) or u + n < U

        def first(u, n):
            return isinstance(u, int) and u < n

        def where(b, g, n):
            return b + (g + n) // G, (g + n) % G

        def uses(b, g):
            return b * 2 + g // 2 + 1

        def bank_of_fill(v, par, f):
            if isinstance(v, int) and v < 2:
                return (v * (NF + 1) + f) % 2
            return (PRO_FILLS + 1 + par * (NF + 1) + 1 + f) % 2

        def bank_of_transpose(par):
            return (PRO_FILLS + 1 + par * (NF + 1)) % 2

        @block.sync
        def _(sp):
            sp.dma_start(above_f[:], io["above"]).then_inc(const_in, 16)

            def load(b, g):
                par, src, cols = g % 2, slice(S_ROW * g, S_ROW * (g + 1)), bass.ds(b * L, L)
                for slot, piece in ((1, k_hi), (2, k_lo), (3, k_hi)):
                    sp.dma_start(k_pack[S_ROW * slot:S_ROW * (slot + 1), par, :], piece[src, cols]).then_inc(k_in[par], 16)
                for slot, piece in ((1, q_hi), (2, q_hi), (3, q_lo)):
                    sp.dma_start(q_pack[S_ROW * slot:S_ROW * (slot + 1), par, :].bitcast(F32), piece[src, cols])\
                        .then_inc(q_in[par], 16)

            def load_max(g):
                sp.dma_start(q_pack[0:S_ROW:DK, g % 2, :].bitcast(F32), neg_max[:, g % 2, :]).then_inc(q_in[g % 2], 16)

            def send_sums(b, g, u):
                sp.dma_start(sums[bass.ds(u * 128, 128), :], out_T[:, g % 2, :]).then_inc(sums_out[g % 2], 16)

            load(0, 0)
            sp.wait_ge(neg_done, 1)
            load_max(0)

            def slot(b, g, u):
                if ahead(u, 1):
                    if not first(u, 1):
                        sp.wait_ge(c_done, u * 2)
                    load(*where(b, g, 1))
                    sp.wait_ge(neg_done, u + 2)
                    load_max((g + 1) % G)
                if not first(u, 1):
                    sp.wait_ge(o_copied, u)
                    send_sums(*where(b, g, -1), u - 1)
                if isinstance(u, int) and u == (NB - 1) * G:
                    for par in range(2):
                        sp.wait_ge(sums_out[par], 16 * (u // 2))
                    sp.dma_start(den[0:96, :], sums.rearrange("(h r) n -> h r n", r=32)[0:96, DK, :]).then_inc(den_in, 16)
                if isinstance(u, int) and u == U - 1:
                    sp.wait_ge(den_done, 1)
                    sp.dma_start(io["recips"][0:96, :], den[0:96, :]).then_inc(recip_out, 16)

            batches(sp, slot)
            sp.wait_ge(recip_out, 16)
            sp.wait_ge(o_copied, U)
            send_sums(NB - 1, G - 1, U - 1)

        @block.vector
        def _(dve):
            def own_queries(b, g):
                for j in range(HG):
                    own_head(b, g, j)

            def own_head(b, g, j):
                rows = slice(S_ROW * g, S_ROW * (g + 1))
                nc.vector.tensor_scalar(q_own[rows, g, j, :], q_bf[rows, bass.ds(b * L, L)],
                                        head_mask[rows, j:j + 1], None, ALU.mult).then_inc(q_own_done, 1)

            def maxima(v, par, next_own=None):
                for f, parts in enumerate(FILLS):
                    if next_own and f in OWN_AT:
                        own_head(*next_own, OWN_AT.index(f))
                    dve.wait_ge(fill_done, v * NF + f + 1)
                    bank = max_ps[bank_of_fill(v, par, f)]
                    if len(parts) == 2 and parts[1][1] == 1:
                        last = nc.vector.reduce_max(row_max[:, par, 1, parts[0][0]:parts[0][0] + 2],
                                                    bank[:].rearrange("p (j n) -> p j n", j=2), AX.X)
                    else:
                        for j, i, c in parts:
                            last = nc.vector.reduce_max(row_max[:, par, i, j:j + 1],
                                                        bank[:, c:c + 128 * (i + 1)], AX.X)
                    last.then_inc(red_done, 1)

            nc.vector.tensor_copy(ident_bf[:], ident[:]).then_inc(const_cast, 1)
            own_queries(0, 0)
            dve.wait_ge(const_in, 16)
            nc.vector.tensor_copy(above[:], above_f[:]).then_inc(const_cast, 1)
            maxima(0, 0, (0, 1))
            maxima(1, 1, (0, 2))

            def slot(b, g, u):
                if ahead(u, 2):
                    dve.wait_ge(max_T_done, u + 1)
                    maxima(u + 2, g % 2, where(b, g, 3) if ahead(u, 3) else None)

            batches(dve, slot)
            dve.wait_ge(den_in, 16)
            nc.vector.reciprocal(den[0:96, :], den[0:96, :]).then_inc(den_done, 1)

        @block.tensor
        def _(pe):
            pe.wait_ge(const_cast, 2)

            def fill(bv, gv, v, f):
                if f == 0:
                    pe.wait_ge(q_own_done, v * HG + HG)
                if not (isinstance(v, int) and v == 0 and f < 2) and not (f == 0):
                    pe.wait_ge(red_done, v * NF + f - 1)
                if f == 1 and not (isinstance(v, int) and v == 0):
                    pe.wait_ge(neg_done, v)
                bank = max_ps[bank_of_fill(v, gv % 2, f)]
                for j, i, c in FILLS[f]:
                    nc.tensor.matmul(bank[:, c:c + 128 * (i + 1)], q_own[:, gv, j, i * 128:(i + 1) * 128],
                                     k_bf[:, bass.ds(bv * L, 128 * (i + 1))], start=True, stop=False)
                    last = nc.tensor.matmul(bank[:, c + 128 * i:c + 128 * (i + 1)], ident_bf[:], above[:],
                                            start=False, stop=True)
                last.then_inc(fill_done, 1)

            def transpose_max(v, par, bank):
                pe.wait_ge(red_done, v * NF + NF)
                for i in range(TB):
                    last = nc.tensor.transpose(max_ps[bank][0:HG, i * 128:(i + 1) * 128], row_max[:, par, i, :], ident[:])
                last.then_inc(max_T_done, 1)

            def scores(b, g, u, j):
                par, pair = g % 2, u * 2 + j // 2
                if j == 0:
                    pe.wait_ge(q_in[par], uses(b, g) * 64)
                    pe.wait_ge(own_pool, u * 2 + 2)
                if j == 2:
                    pe.wait_ge(own_act, u * 2 + 2)
                if not (first(u, 1) and j < 2):
                    pe.wait_ge(exp_ab, u * HG + j - 1)
                for kt, (c, n) in KEY_COLS.items():
                    at = 1024 * (j % 2) + c
                    last = nc.tensor.matmul(ab_ps[:, at:at + n], k_own[:, par, j, kt * 128:(kt + 1) * 128],
                                            q_pack[:, par, L - n:L], start=True, stop=True)
                last.then_inc(ab_done, 1)
                if j % 2 == 0 and not (first(u, 1) and j == 0):
                    pe.wait_ge(exp_c, pair)
                last = nc.tensor.matmul(c_ps[:, 256 * (j % 2):256 * (j % 2) + 256], k_own[:, par, j, 256:384],
                                        q_pack[:, par, 256:512], start=True, stop=True)
                if j % 2:
                    last.then_inc(c_done, 1)

            def weigh(u, par, kt):
                if kt == 0:
                    pe.wait_ge(masked, u * 10 + 10)
                    pe.wait_ge(v_done, u + 1)
                    if not first(u, 1):
                        pe.wait_ge(o_copied, u)
                for j in range(HG):
                    if kt == 2:
                        c, n = 2048 + 256 * (j % 2), 256
                    else:
                        c, n = KEY_COLS[kt][0] + 1024 * (j % 2), KEY_COLS[kt][1]
                    last = nc.tensor.matmul(o_ps[32 * j:32 * j + 32, L - n:L], v_aug[:, par, kt, j, :],
                                            probs[:, par, j // 2, c:c + n], start=(kt == 0), stop=(kt == TB - 1))
                if kt == TB - 1:
                    last.then_inc(pv_done, 1)

            for f in range(NF):
                fill(0, 0, 0, f)
            transpose_max(0, 0, NF % 2)
            for f in range(NF):
                fill(0, 1, 1, f)

            def slot(b, g, u):
                par = g % 2
                fills = list(range(NF)) if ahead(u, 2) else []

                def next_fill():
                    if fills:
                        fill(*where(b, g, 2), u + 2, fills.pop(0))

                for part in SLOT_ORDER:
                    kind, n = part[0], int(part[1:] or 0)
                    if kind == "s":
                        scores(b, g, u, n)
                    elif kind == "t" and ahead(u, 1):
                        transpose_max(u + 1, 1 - par, bank_of_transpose(par))
                    elif kind == "w" and not first(u, 1):
                        weigh(u - 1, 1 - par, n)
                    elif kind == "f":
                        for _ in range(n):
                            next_fill()

            batches(pe, slot)
            for kt in range(TB):
                weigh(U - 1, 1, kt)

        @block.scalar
        def _(act):
            scale = DK ** -0.5

            def negate_max(v, par, bank):
                act.wait_ge(max_T_done, v + 1)
                nc.scalar.activation(neg_max[:, par, :].bitcast(F32R), max_ps[bank][0:HG, :], ACT.Copy,
                                     scale=-1.0).then_inc(neg_done, 1)

            def own_keys(b, g, u):
                act.wait_ge(k_in[g % 2], uses(b, g) * 48)
                for j in (2, 3):
                    nc.scalar.activation(k_own[:, g % 2, j, :], k_pack[:, g % 2, :], ACT.Copy,
                                         scale=head_mask[:, j:j + 1]).then_inc(own_act, 1)

            def augment(b, g, u):
                if not first(u, 2):
                    act.wait_ge(pv_done, u - 1)
                nc.scalar.activation(v_aug[:, g % 2, :, :, 0:DK],
                                     v_all[:, bass.ds(b * TB, TB), S_ROW * g:S_ROW * (g + 1)]
                                     .rearrange("p t (j d) -> p t j d", d=DK), ACT.Copy).then_inc(v_done, 1)

            def exps(b, g, u, pair, between=lambda: None):
                par = g % 2
                if pair == 0 and not first(u, 2):
                    act.wait_ge(pv_done, u - 1)
                for j in (0, 1):
                    act.wait_ge(ab_done, u * HG + 2 * pair + j + 1)
                    nc.scalar.activation(probs[:, par, pair, 1024 * j:1024 * (j + 1)], ab_ps[:, 1024 * j:1024 * (j + 1)],
                                         ACT.Exp, scale=scale).then_inc(exp_ab, 1)
                    if j == 0:
                        between()
                act.wait_ge(c_done, u * 2 + pair + 1)
                nc.scalar.activation(probs[:, par, pair, 2048:PAIR], c_ps[:], ACT.Exp, scale=scale).then_inc(exp_c, 1)

            def copy_sums(b, g, u):
                act.wait_ge(pv_done, u + 1)
                if not first(u, 2):
                    act.wait_ge(sums_out[g % 2], uses(b, g) * 16 - 16)
                nc.scalar.activation(out_T[:, g % 2, :], o_ps[:], ACT.Copy).then_inc(o_copied, 1)

            negate_max(0, 0, NF % 2)
            own_keys(0, 0, 0)

            def slot(b, g, u):
                def next_maxima():
                    if ahead(u, 1):
                        negate_max(u + 1, 1 - g % 2, bank_of_transpose(g % 2))

                exps(b, g, u, 0, next_maxima)
                if ahead(u, 1):
                    if not first(u, 1):
                        act.wait_ge(c_done, u * 2)
                    own_keys(*where(b, g, 1), u + 1)
                if not first(u, 1):
                    copy_sums(*where(b, g, -1), u - 1)
                exps(b, g, u, 1)
                augment(b, g, u)

            batches(act, slot)
            copy_sums(NB - 1, G - 1, U - 1)

        @block.gpsimd
        def _(pool):
            def own_keys(b, g):
                pool.wait_ge(k_in[g % 2], uses(b, g) * 48)
                for j in (0, 1):
                    nc.gpsimd.tensor_tensor(k_own[:, g % 2, j, :], k_pack[:, g % 2, :],
                                            head_mask[:, j:j + 1].broadcast_to([128, L]), ALU.mult).then_inc(own_pool, 1)

            def causal(p, n):
                pattern = [[0, n], [1, 128]] if n > 1 else [[1, 128]]
                nc.gpsimd.affine_select(out=p, in_=p, pattern=pattern, compare_op=ALU.is_ge, fill=0.0, base=0,
                                        channel_multiplier=-1).then_inc(masked, 1)

            def mask(b, g, u, pair):
                for j in (0, 1):
                    p = probs[:, g % 2, pair, 1024 * j:1024 * (j + 1)]
                    pool.wait_ge(exp_ab, u * HG + 2 * pair + j + 1)
                    pool.sem_inc(waited, 1)
                    causal(p.rearrange("p (s n) -> p s n", s=2)[:, :, 0:128], 2)
                    causal(p[:, 896:1024], 1)
                pool.wait_ge(exp_c, u * 2 + pair + 1)
                pool.sem_inc(waited, 1)
                causal(probs[:, g % 2, pair, 2048:PAIR].rearrange("p (s n) -> p s n", s=2)[:, :, 0:128], 2)

            own_keys(0, 0)

            def slot(b, g, u):
                mask(b, g, u, 0)
                if ahead(u, 1):
                    if not first(u, 1):
                        pool.wait_ge(c_done, u * 2)
                    own_keys(*where(b, g, 1))
                mask(b, g, u, 1)

            batches(pool, slot)



def route_phase(nc, io, keep):
    ctx = ExitStack()
    with ctx:
        sb = lambda n, s, d=F32: ctx.enter_context(nc.sbuf_tensor("c_" + n, s, d))
        sem = lambda n: ctx.enter_context(nc.semaphore("c_" + n))
        ps = [ctx.enter_context(nc.psum_tensor(f"c_ps{i}", [128, 512], F32)) for i in range(8)]
        proj_ps, trans_ps, gate_ps, slot_ps, inv_ps = ps[0:2], ps[2:4], ps[4:6], ps[6], ps[7]
        mod, ident, x1, parts, w13_hi, w13_lo, w2 = (keep[n] for n in ("mod", "ident", "x1", "parts", "w13_hi", "w13_lo", "w2"))
        P_SB, P_CB, P_GB = range(3)
        pv, recip = sb("pv", [128, T]), sb("recip", [128, T])
        attn = sb("attn", [128, 2, L])
        den = keep["den"]
        consts, bias_out = sb("consts", [128, CONST_COLS]), sb("bias_out", [128, D])
        const = lambda name: consts[:, CONSTS[name][0]:CONSTS[name][0] + CONSTS[name][1]]
        wout, gate_w, number, before_f, multiple, partition, spare_row, bias_v = (
            const(n) for n in ("wout", "gate_T", "number", "before", "multiple", "partition", "spare_row", "bias_v"))
        rank = const("rank").rearrange("p (t e) -> p t e", e=E)
        wout_ga, ga_bias = sb("wout_ga", [128, NB, D]), sb("ga_bias", [128, NB, D])
        stats, mean_var = sb("stats", [128, 2, TB, 6]), sb("mean_var", [128, NT, 2])
        var, root, half = sb("var", [128, NT]), sb("root", [128, NT]), sb("half", [128, NT])
        norm, hT = sb("norm", [128, 2, TB, D]), sb("hT", [128, 2, L])
        h = recip[:].rearrange("p (t c) -> p t c", c=D)
        logits, top, one_hot, diff, expd, tmp, tmp2, pick = (keep[n] for n in
                                                             ("logits", "top", "one_hot", "diff", "expd", "tmp", "tmp2", "pick"))
        number_bf, before, ones = sb("number_bf", [128, 128], BF16), sb("before", [128, 128], BF16), sb("ones", [128, 128], BF16)
        chosen = sb("chosen", [128, NT * E], BF16)
        PAD = NT // 2
        scan = [sb(f"scan{i}", [128, PAD + NT, E]) for i in range(2)]
        base = [sb(f"base{i}", [128, 2 * E]) for i in range(2)]
        pos, pos_int = sb("pos", [128, 2 * NT]), sb("pos_int", [128, 2 * NT], I32)
        tile_int = sb("tile_int", [128, 2 * NT], I32)
        tile_bf, lane_bf = sb("tile_bf", [128, 2 * NT], BF16), sb("lane_bf", [128, 2 * NT], BF16)
        ident_row = sb("ident_row", [128, NS])
        row_part = sb("row_part", [128, 3 * NS])
        cmp = sb("cmp", [128, NS * E])

        w_in, den_in, recip_out = sem("w_in"), sem("den_in"), sem("recip_out")
        x_in = [sem(f"x_in{i}") for i in range(2)]
        sums_in = [sem(f"sums_in{b}") for b in range(NB)]
        raw_in = [sem(f"raw_in{i}") for i in range(8)]
        den_done = sem("den_done")
        parts_ps_done, parts_done, wout_ga_done, ga_bias_done, biased = (sem("parts_ps_done"), sem("parts_done"), sem("wout_ga_done"),
                                                                         sem("ga_bias_done"), sem("biased"))
        attn_done, proj_done, x1_done = sem("attn_done"), sem("proj_done"), sem("x1_done")
        stats_done, aggr_done = sem("stats_done"), sem("aggr_done")
        bias_done, bias_added = sem("bias_done"), sem("bias_added")
        chain, var_done, root_done = sem("dve_chain"), sem("var_done"), sem("root_done")
        h_done, trans_done = sem("h_done"), sem("trans_done")
        h_out = sem("h_out")
        hT_done, gate_done, logits_done = sem("hT_done"), sem("gate_done"), sem("logits_done")
        hi_done, lo_done = sem("hi_done"), sem("lo_done")
        diff_done, exp_done = sem("diff_done"), sem("exp_done")
        zeroed, chosen_done, within_done = sem("zeroed"), sem("chosen_done"), sem("within_done")
        hot_done, by_part_done, lanes_done, inv_done = (sem("hot_done"), sem("by_part_done"),
                                                                 sem("lanes_done"), sem("inv_done"))
        by_place_done, wide_done = sem("by_place_done"), sem("wide_done")
        block = ctx.enter_context(nc.Block())
        sums, recips = io["sums"], io["recips"]
        h_rows = io["h_rows"].rearrange("(t p) c -> p t c", p=128)
        W_IN = 32
        EARLY = 96 // H

        def weight_piece(piece):
            half_of, kind = slice(E // 2 * (piece // 4), E // 2 * (piece // 4 + 1)), piece % 4
            if kind < 2:
                return [(w13_hi[kind][:, half_of, :], w13_lo[kind][:, half_of, :])]
            return [(w2[fb][:, half_of, 0:D], w2[fb][:, half_of, D:2 * D]) for fb in (2 * kind - 4, 2 * kind - 3)]

        def raw_piece(piece):
            half_of, kind = slice(E // 2 * (piece // 4), E // 2 * (piece // 4 + 1)), piece % 4
            if kind < 2:
                return [io[("w1_T", "w3_T")[kind]][half_of].rearrange("e p f -> p e f")]
            return [io["w2_T"][half_of, :, fb, :].rearrange("e p c -> p e c") for fb in (2 * kind - 4, 2 * kind - 3)]

        hot = [a[:].bitcast(BF16)[:, 0:NT * 3 * NS].rearrange("p (t s n) -> p t s n", s=3, n=NS) for a in (pv, recip)]
        flat4 = lambda a: a[:].rearrange("p a t c -> p (a t c)")
        number_wide = attn[:].rearrange("p a c -> p (a c)").bitcast(BF16).rearrange("p (n t) -> p n t", t=16)
        lanes = [a.bitcast(BF16).rearrange("p (n t) -> p n t", t=16)
                 for a in (flat4(norm), wout_ga[:].rearrange("p b c -> p (b c)"), ga_bias[:].rearrange("p b c -> p (b c)"), hT[:].rearrange("p a c -> p (a c)"))]

        @block.sync
        def _(sp):
            heads = sums.rearrange("(h r) n -> h r n", r=32)
            late = slice(H * EARLY, NB * H)

            def load_x(i):
                sp.dma_start(x1[:, NT // 2 * i:NT // 2 * (i + 1), :], io["x"][:, NT // 2 * i:NT // 2 * (i + 1), :]).then_inc(x_in[i], 16)

            def load_pv(b):
                sp.dma_start(pv[:, L * b:L * (b + 1)], heads[H * b:H * (b + 1), 0:DK, :]).then_inc(sums_in[b], 16)

            def load_recip(b):
                sp.dma_start(recip[:, L * b:L * (b + 1)],
                             recips[H * b:H * (b + 1), None, :].broadcast_to([H, DK, L])).then_inc(sums_in[b], 16)

            for b in range(EARLY):
                load_pv(b)
                load_recip(b)
                if b == 0:
                    load_x(0)
                    for par in range(2):
                        sp.wait_ge(keep["sums_out"][par], 16 * (NB * G // 2))
                    sp.dma_start(den[late, :], heads[late, DK, :]).then_inc(den_in, 16)
                if b == 2:
                    load_x(1)
            for b in range(EARLY, NB):
                load_pv(b)
            sp.wait_ge(den_done, 1)
            sp.dma_start(recips[late, :], den[late, :]).then_inc(recip_out, 16)
            sp.wait_ge(recip_out, 16)
            for b in range(EARLY, NB):
                load_recip(b)
            for piece in range(8):
                for (hi, lo), raw in zip(weight_piece(piece), raw_piece(piece)):
                    sp.dma_start(lo.bitcast(F32), raw).then_inc(raw_in[piece], 16)
            for b in range(NB):
                sp.wait_ge(h_done, b + 1)
                sp.dma_start(h_rows[:, TB * b:TB * (b + 1), :], h[:, TB * b:TB * (b + 1), :]).then_inc(h_out, 16)
            sp.wait_ge(h_out, 16 * NB)

        @block.scalar
        def _(act):
            act.dma_start(consts[:], io["consts"]).then_inc(w_in, 16)
            act.dma_start(bias_out[:], io["bias_out"].partition_broadcast(128)).then_inc(w_in, 16)
            for part in range(3):
                act.wait_ge(parts_ps_done, part + 2)
                for i in range(2):
                    nc.scalar.activation(parts[:, part, 4 * i:4 * i + 4, :].rearrange("p b c -> p (b c)"), ps[2 + 2 * part + i][:],
                                         ACT.Copy).then_inc(parts_done, 1)

            def copy_hT(b):
                act.wait_ge(trans_done, b + 1)
                if b >= 2:
                    act.wait_ge(gate_done, b - 1)
                nc.scalar.activation(hT[:, b % 2, :], trans_ps[b % 2][:], ACT.Copy).then_inc(hT_done, 1)

            def copy_logits(b):
                act.wait_ge(gate_done, b + 1)
                nc.scalar.activation(logits[:, TB * b:TB * (b + 1), :].rearrange("p t e -> p (t e)"),
                                     gate_ps[b % 2][:, 0:TB * E], ACT.Copy).then_inc(logits_done, 1)

            def high_parts(piece):
                parts_of = weight_piece(piece)
                act.wait_ge(raw_in[piece], 16 * len(parts_of))
                for hi, lo in parts_of:
                    last = nc.scalar.activation(hi, lo.bitcast(F32), ACT.Copy)
                last.then_inc(hi_done, 1)

            def square_root(i):
                act.wait_ge(var_done, i + 1)
                nc.scalar.activation(root[:, NT // 2 * i:NT // 2 * (i + 1)], var[:, NT // 2 * i:NT // 2 * (i + 1)],
                                     ACT.Sqrt).then_inc(root_done, 1)

            square_root(0)
            for b in range(NB):
                if b == 2:
                    square_root(1)
                copy_hT(b)
                if b:
                    copy_logits(b - 1)
                if b < 6:
                    high_parts(b)
            copy_logits(NB - 1)
            nc.scalar.activation(number_wide, number[:, :, None].broadcast_to([128, 128, 16]), ACT.Copy).then_inc(wide_done, 1)
            for piece in (6, 7):
                high_parts(piece)
            for k in range(2):
                act.wait_ge(hot_done, k + 1)
                nc.scalar.activation(hot[k][:, :, 1, :], hot[k][:, :, 2, :], ACT.Copy, scale=partition).then_inc(by_part_done, 1)
            for i in range(2):
                act.wait_ge(diff_done, i + 1)
                nc.scalar.activation(expd[i][:], diff[i][:], ACT.Exp).then_inc(exp_done, 1)

        @block.gpsimd
        def _(pool):
            for a in (*scan, *base, ones):
                last = nc.gpsimd.memset(a[:], 1.0 if a is ones else 0.0)
            last.then_inc(zeroed, 1)

            def normalize_attention(b):
                pool.wait_ge(sums_in[b], 32)
                if b >= 2:
                    pool.wait_ge(proj_done, b - 1)
                cols = slice(L * b, L * (b + 1))
                nc.gpsimd.tensor_tensor(attn[:, b % 2, :], pv[:, cols], recip[:, cols], ALU.mult).then_inc(attn_done, 1)

            def add_bias(b):
                pool.wait_ge(x_in[b // 4], 16)
                tiles = slice(TB * b, TB * (b + 1))
                nc.gpsimd.tensor_tensor(x1[:, tiles, :], x1[:, tiles, :],
                                        ga_bias[:, b:b + 1, :].broadcast_to([128, TB, D]), ALU.add).then_inc(biased, 1)

            normalize_attention(0)
            pool.wait_ge(ga_bias_done, 2)
            for b in range(NB):
                if b + 1 < NB:
                    normalize_attention(b + 1)
                add_bias(b)
            for piece in range(8):
                pool.wait_ge(hi_done, piece + 1)
                for hi, lo in weight_piece(piece):
                    nc.gpsimd.tensor_tensor(lo, lo.bitcast(F32), hi.bitcast(F32), ALU.subtract).then_inc(lo_done, 1)
            for k in range(2):
                pool.wait_ge(hot_done, k + 1)
                nc.gpsimd.tensor_tensor(hot[k][:, :, 0, :], hot[k][:, :, 2, :],
                                        number_bf[:, NT * k:NT * (k + 1), None].broadcast_to([128, NT, NS]),
                                        ALU.mult).then_inc(by_place_done, 1)

        @block.tensor
        def _(pe):
            for n, part in enumerate((GA, SB_, CB, GB)):
                if part == SB_:
                    pe.wait_ge(w_in, W_IN)
                    nc.tensor.matmul(ps[6][:, 0:D], bias_v.broadcast_to([128, 128]), wout, start=True, stop=True).then_inc(bias_done, 1)
                if part == GB:
                    pe.wait_ge(bias_added, 1)
                for b in range(NB):
                    last = nc.tensor.matmul(ps[2 * n + b // 4][:, b % 4 * D:(b % 4 + 1) * D],
                                            mod[:, part, b:b + 1].broadcast_to([128, 128]), ident[:], start=True, stop=True)
                last.then_inc(parts_ps_done, 1)
            pe.wait_ge(w_in, W_IN)
            pe.wait_ge(wout_ga_done, 2)
            pe.wait_ge(ga_bias_done, 2)

            def project(b, par, first):
                pe.wait_ge(attn_done, b + 1)
                if not first:
                    pe.wait_ge(x1_done, b - 1)
                for t in range(TB):
                    last = nc.tensor.matmul(proj_ps[par][:, t * D:(t + 1) * D], attn[:, par, t * 128:(t + 1) * 128],
                                            wout_ga[:, bass.ds(b, 1), :].rearrange("p a c -> p (a c)"),
                                            start=True, stop=True)
                last.then_inc(proj_done, 1)

            def transpose_batch(b, par, first):
                pe.wait_ge(h_done, b + 1)
                if not first:
                    pe.wait_ge(hT_done, b - 1)
                for t in range(TB):
                    last = nc.tensor.transpose(trans_ps[par][:, t * 128:(t + 1) * 128],
                                               h[:, TB * b + t, :], ident[:])
                last.then_inc(trans_done, 1)

            def gate(b, par, first):
                pe.wait_ge(hT_done, b + 1)
                if not first:
                    pe.wait_ge(logits_done, b - 1)
                for t in range(TB):
                    last = nc.tensor.matmul(gate_ps[par][:, t * E:(t + 1) * E], hT[:, par, t * 128:(t + 1) * 128], gate_w,
                                            start=True, stop=True)
                last.then_inc(gate_done, 1)

            def pairs(stages):
                for stage in stages:
                    for par in range(2):
                        stage(par, par, True)
                with pe.Fori(1, NB // 2) as pair:
                    for stage in stages:
                        for par in range(2):
                            stage(pair * 2 + par, par, False)

            pairs([project])
            pe.wait_ge(parts_done, 6)
            for b in range(0, NB, 2):
                for stage in (transpose_batch, gate):
                    for par in range(2):
                        stage(b + par, par, b == 0)
            pe.wait_ge(chosen_done, 1)
            nc.tensor.matmul(slot_ps[:, 0:NT * E], before[:], chosen[:], start=True, stop=True)
            nc.tensor.matmul(slot_ps[:, NT * E:2 * NT * E], ones[:], chosen[:], start=True, stop=True).then_inc(within_done, 1)
            for i in range(4):
                pe.wait_ge(by_part_done, i // 2 + 1)
                pe.wait_ge(by_place_done, i // 2 + 1)
                pe.wait_ge(lanes_done, i + 1)
                for j in range(16):
                    a = 16 * i + j
                    last = nc.tensor.matmul(inv_ps[:, 0:3 * NS], lanes[i][:, :, j], hot[a // NT][:, a % NT, :, :].rearrange("p s n -> p (s n)"),
                                            start=i == 0 and j == 0, stop=i == 3 and j == 15)
            last.then_inc(inv_done, 1)

        @block.vector
        def _(dve):
            n = [0]

            def step(ins):
                n[0] += 1
                ins.then_inc(chain, 1)
                dve.wait_ge(chain, n[0])

            dve.wait_ge(w_in, W_IN)
            dve.wait_ge(parts_ps_done, 1)
            dve.wait_ge(bias_done, 1)
            nc.vector.tensor_tensor(bias_out[:], bias_out[:], ps[6][:, 0:D], ALU.add).then_inc(bias_added, 1)
            dve.wait_ge(bias_added, 1)
            for factor, product, done in ((wout, wout_ga, wout_ga_done), (bias_out[:], ga_bias, ga_bias_done)):
                for i in range(2):
                    nc.vector.tensor_tensor(product[:, 4 * i:4 * i + 4, :], ps[i][:].rearrange("p (b c) -> p b c", c=D),
                                            factor[:, None, :].broadcast_to([128, 4, D]), ALU.mult).then_inc(done, 1)
            nc.vector.tensor_copy(number_bf[:], number)
            nc.vector.tensor_copy(before[:], before_f)

            def residual(b):
                tiles = slice(TB * b, TB * (b + 1))
                dve.wait_ge(proj_done, b + 1)
                dve.wait_ge(biased, b + 1)
                nc.vector.tensor_tensor(x1[:, tiles, :], proj_ps[b % 2][:].rearrange("p (t c) -> p t c", c=D),
                                        x1[:, tiles, :], ALU.add).then_inc(x1_done, 1)
                dve.wait_ge(x1_done, b + 1)
                for t in range(TB):
                    last = nc.vector.bn_stats(stats[:, b % 2, t, :], x1[:, TB * b + t, :])
                last.then_inc(stats_done, 1)
                dve.wait_ge(stats_done, b + 1)
                for t in range(TB):
                    last = nc.vector.bn_aggr(mean_var[:, TB * b + t, :], stats[:, b % 2, t, :])
                last.then_inc(aggr_done, 1)

            def variance(i):
                half_of = slice(NT // 2 * i, NT // 2 * (i + 1))
                dve.wait_ge(aggr_done, NB // 2 * (i + 1))
                nc.vector.tensor_scalar(var[:, half_of], mean_var[:, half_of, 1], EPS, None, ALU.add).then_inc(var_done, 1)

            def inverse_root(i):
                half_of = slice(NT // 2 * i, NT // 2 * (i + 1))
                dve.wait_ge(root_done, i + 1)
                newton_rstd(nc, step, root[:, half_of], var[:, half_of], half[:, half_of])

            def second_norm(b):
                for t in range(TB):
                    at = TB * b + t
                    last = nc.vector.scalar_tensor_tensor(norm[:, b % 2, t, :], x1[:, at, :], mean_var[:, at, 0:1],
                                                          parts[:, P_CB, b, :], ALU.subtract, ALU.mult)
                step(last)
                for t in range(TB):
                    at = TB * b + t
                    last = nc.vector.scalar_tensor_tensor(h[:, at, :], norm[:, b % 2, t, :], root[:, at:at + 1],
                                                          parts[:, P_SB, b, :], ALU.mult, ALU.add)
                last.then_inc(h_done, 1)

            for b in range(4):
                residual(b)
                if b == 1:
                    late = slice(H * EARLY, NB * H)
                    dve.wait_ge(den_in, 16)
                    nc.vector.reciprocal(den[late, :], den[late, :]).then_inc(den_done, 1)
            variance(0)
            residual(4)
            inverse_root(0)
            dve.wait_ge(parts_done, 4)
            second_norm(0)
            residual(5)
            second_norm(1)
            residual(6)
            second_norm(2)
            residual(7)
            variance(1)
            second_norm(3)
            inverse_root(1)
            for b in range(4, NB):
                second_norm(b)
            dve.wait_ge(logits_done, NB)

            wide = lambda a: a[:, :, None].broadcast_to([128, NT, E])
            tt, ts = nc.vector.tensor_tensor, nc.vector.tensor_scalar

            def first_of(hot, values, m):
                step(nc.vector.reduce_max(m, values, AX.X))
                step(tt(tmp[:], values, wide(m), ALU.is_equal))
                step(tt(tmp[:], tmp[:], rank, ALU.mult))
                step(nc.vector.reduce_max(pick[:], tmp[:], AX.X))
                step(tt(hot, tmp[:], wide(pick), ALU.is_equal))

            first_of(one_hot[0][:], logits[:], top[0][:])
            step(nc.vector.scalar_tensor_tensor(tmp2[:], one_hot[0][:], -3e38, logits[:], ALU.mult, ALU.add))
            first_of(one_hot[1][:], tmp2[:], top[1][:])
            chosen3 = chosen[:].rearrange("p (t e) -> p t e", e=E)
            nc.vector.tensor_tensor(chosen3, one_hot[0][:], one_hot[1][:], ALU.add).then_inc(chosen_done, 1)
            dve.wait_ge(zeroed, 1)
            dve.wait_ge(within_done, 1)
            tiles_of = lambda i, shift: scan[i][:, PAD - shift:PAD - shift + NT, :]
            step(nc.vector.tensor_copy(tiles_of(0, 0), slot_ps[:, NT * E:2 * NT * E].rearrange("p (t e) -> p t e", e=E)))
            at = 0
            for k in range(5):
                step(tt(tiles_of(1 - at, 0), tiles_of(at, 0), tiles_of(at, 1 << k), ALU.add))
                at = 1 - at
            counts = scan[at][:, PAD + NT - 1, :]
            by_tile = cmp[:, 0:E * NT].rearrange("p (e t) -> p e t", t=NT)
            step(tt(by_tile, counts[:, :, None].broadcast_to([128, E, NT]), multiple[:, None, :].broadcast_to([128, E, NT]), ALU.is_gt))
            step(nc.vector.reduce_sum(base[0][:, E:2 * E], by_tile, AX.X))
            for k in range(3):
                step(tt(base[(k + 1) % 2][:, E:2 * E], base[k % 2][:, E:2 * E], base[k % 2][:, E - (1 << k):2 * E - (1 << k)], ALU.add))
            first_tile = base[1][:, E - 1:2 * E - 1]
            place = scan[1 - at][:, PAD:PAD + NT, :]
            step(tt(place, slot_ps[:, 0:NT * E].rearrange("p (t e) -> p t e", e=E), tiles_of(at, 1), ALU.add))
            step(nc.vector.scalar_tensor_tensor(place, first_tile[:, None, :].broadcast_to([128, NT, E]), 128.0, place, ALU.mult, ALU.add))
            for k in range(2):
                step(tt(tmp[:], one_hot[k][:], place, ALU.mult))
                step(nc.vector.reduce_sum(pos[:, NT * k:NT * (k + 1)], tmp[:], AX.X))
            step(nc.vector.tensor_copy(pos_int[:], pos[:]))
            step(ts(tile_int[:], pos_int[:], 7, None, ALU.arith_shift_right))
            step(ts(pos_int[:], pos_int[:], 127, None, ALU.bitwise_and))
            nc.vector.tensor_copy(tile_bf[:], tile_int[:])
            step(nc.vector.tensor_copy(lane_bf[:], pos_int[:]))
            
            def lane_one_hot(i):
                nc.vector.tensor_tensor(lanes[i], number_wide, lane_bf[:, None, 16 * i:16 * i + 16].broadcast_to([128, 128, 16]),
                                        ALU.is_equal).then_inc(lanes_done, 1)

            def tile_one_hot(k):
                nc.vector.tensor_tensor(hot[k][:, :, 2, :], number_bf[:, None, 0:NS].broadcast_to([128, NT, NS]),
                                        tile_bf[:, NT * k:NT * (k + 1), None].broadcast_to([128, NT, NS]),
                                        ALU.is_equal).then_inc(hot_done, 1)

            tile_one_hot(0)
            dve.wait_ge(h_out, 16 * NB)
            tile_one_hot(1)
            dve.wait_ge(wide_done, 1)
            lane_one_hot(0)
            lane_one_hot(1)
            lane_one_hot(2)
            lane_one_hot(3)
            step(tt(diff[0][:], logits[:], wide(top[0]), ALU.subtract))
            nc.vector.engine_nop().then_inc(diff_done, 1)
            step(tt(diff[1][:], logits[:], wide(top[1]), ALU.subtract))
            step(ts(diff[1][:], diff[1][:], 0.0, None, ALU.min))
            nc.vector.engine_nop().then_inc(diff_done, 1)
            e_cmp = cmp[0:1, :].rearrange("p (n e) -> p n e", e=E)
            step(tt(e_cmp, number[0:1, 0:NS, None].broadcast_to([1, NS, E]), first_tile[0:1, None, :].broadcast_to([1, NS, E]), ALU.is_ge))
            step(nc.vector.reduce_sum(ident_row[0:1, :], e_cmp, AX.X))
            step(ts(keep["expert_of"][:], ident_row[0:1, :], -1.0, None, ALU.add))

            dve.wait_ge(inv_done, 1)
            step(nc.vector.tensor_copy(row_part[:], inv_ps[:, 0:3 * NS]))
            place_no, part_no, used = (row_part[:, NS * i:NS * (i + 1)] for i in range(3))
            step(nc.vector.scalar_tensor_tensor(ident_row[:], place_no, 128.0, part_no, ALU.mult, ALU.add))
            step(ts(place_no, ident_row[:], float(T), -float(T), ALU.is_ge, ALU.mult))
            step(tt(keep["src"][:], ident_row[:], place_no, ALU.add))
            step(ts(used, used, -1.0, 1.0, ALU.mult, ALU.add))
            step(tt(used, used, spare_row[:], ALU.mult))
            step(tt(keep["dst"][:], ident_row[:], used, ALU.add))


def expert_phase(nc, io, keep, out):
    ctx = ExitStack()
    with ctx:
        sb = lambda n, s, d=F32: ctx.enter_context(nc.sbuf_tensor("d_" + n, s, d))
        sem = lambda n: ctx.enter_context(nc.semaphore("d_" + n))
        ps = [ctx.enter_context(nc.psum_tensor(f"d_ps{i}", [128, 512], F32)) for i in range(8)]
        gate_ps, up_ps, y_ps, hT_ps, gT_ps = ps[0:2], ps[2:4], ps[4:6], ps[6], ps[7]
        ident, x1, parts, w13_hi, w13_lo, w2 = (keep[n] for n in ("ident", "x1", "parts", "w13_hi", "w13_lo", "w2"))
        src, dst, expert_of, route_w = (keep[n] for n in ("src", "dst", "expert_of", "route_w"))
        P_GB = 2
        RING = 4
        src_now, dst_now = sb("src_now", [128, RING], U32), sb("dst_now", [128, RING], U32)
        h = sb("h", [128, RING, D])
        h_hi, h_lo = sb("h_hi", [128, 2, 128], F32R), sb("h_lo", [128, 2, 128], F32R)
        silu, g = sb("silu", [128, 2, FF]), sb("g", [128, 2, FF])
        g_hi, g_lo = sb("g_hi", [128, 2, FB, 128], F32R), sb("g_lo", [128, 2, FB, 128], F32R)
        y_low, y = sb("y_low", [128, 2, D]), sb("y", [128, RING, D])
        y_both = sb("y_both", [128, 2, NT, D])
        table_only = sb("table_only", [128, 1])

        h_in = [sem(f"h_in{i}") for i in range(RING)]
        y_out = [sem(f"y_out{i}") for i in range(RING)]
        src_set, dst_set, waited = sem("src_set"), sem("dst_set"), sem("waited")
        hT_done, h_hi_done, h_lo_done = sem("hT_done"), sem("h_hi_done"), sem("h_lo_done")
        gate_done, up_done, silu_done, g_done = sem("gate_done"), sem("up_done"), sem("silu_done"), sem("g_done")
        gT_done, g_hi_done, g_lo_done = sem("gT_done"), sem("g_hi_done"), sem("g_lo_done")
        down_done, y_low_done, y_done = sem("down_done"), sem("y_low_done"), sem("y_done")
        chain, weight_done = sem("dve_chain"), sem("weight_done")
        both_in = [sem(f"both_in{i}") for i in range(4)]
        first_done, sum_done, gated, out_done, stored = (sem("first_done"), sem("sum_done"), sem("gated"), sem("out_done"), sem("stored"))
        block = ctx.enter_context(nc.Block())

        BODY = 12

        class Tile:
            def __init__(self, body, step):
                self.body, self.step, self.par = body, step, step % 2
                self.n, self.place, self.turn = body * BODY + step, step % RING, body * (BODY // RING) + step // RING
                self.fixed = isinstance(body, int)

            def __add__(self, d):
                return Tile(self.body + (self.step + d) // BODY, (self.step + d) % BODY)

            def exists(self):
                return not self.fixed or 0 <= self.n < NS

            def past(self, k):
                return not self.fixed or self.n >= k

        def tiles(eng, step):
            for n in range(BODY):
                step(Tile(0, n))
            with eng.Fori(1, NS // BODY - 1) as body:
                for n in range(BODY):
                    step(Tile(body, n))
            for n in range(BODY):
                step(Tile(NS // BODY - 1, n))

        last_tile = Tile(NS // BODY - 1, BODY - 1)

        y_view = io["y_rows"][0:2 * T, :].rearrange("(k t p) c -> p k t c", k=2, p=128)
        TG = NT // 4

        @block.sync
        def _(sp):
            for i in range(RING):
                sp.wait_ge(y_out[i], 16 * NS // RING)
            for i in range(4):
                for k in range(2):
                    sp.dma_start(y_both[:, k, TG * i:TG * (i + 1), :], y_view[:, k, TG * i:TG * (i + 1), :]).then_inc(both_in[i], 16)
            for b in range(NB):
                sp.wait_ge(out_done, b + 1)
                sp.dma_start(out[:, TB * b:TB * (b + 1), :], x1[:, TB * b:TB * (b + 1), :]).then_inc(stored, 16)
            sp.wait_ge(stored, 16 * NB)

        @block.gpsimd
        def _(pool):
            def gather(i):
                nc.gpsimd.tensor_copy(src_now[:, i.place:i.place + 1], src[:, bass.ds(i.n, 1)]).then_inc(src_set, 1)
                pool.wait_ge(src_set, i.n + 1)
                pool.sem_inc(waited, 1)
                pool.indirect_dma_start(h[:, i.place, :], None, io["h_rows"],
                                        bass.IndirectOffsetOnAxis(ap=src_now[:, i.place:i.place + 1], axis=0)).then_inc(h_in[i.place], 16)

            def scatter(i):
                if i.past(RING):
                    pool.wait_ge(y_out[i.place], i.turn * 16)
                nc.gpsimd.tensor_copy(dst_now[:, i.place:i.place + 1], dst[:, bass.ds(i.n, 1)]).then_inc(dst_set, 1)
                pool.wait_ge(y_done, i.n + 1)
                pool.wait_ge(dst_set, i.n + 1)
                pool.sem_inc(waited, 1)
                pool.indirect_dma_start(io["y_rows"], bass.IndirectOffsetOnAxis(ap=dst_now[:, i.place:i.place + 1], axis=0),
                                        y[:, i.place, :], None).then_inc(y_out[i.place], 16)

            for slot in range(RING):
                gather(Tile(0, slot))

            def step(i):
                if (i + RING).exists():
                    pool.wait_ge(hT_done, i.n + 1)
                    gather(i + RING)
                if (i + -3).exists():
                    scatter(i + -3)

            tiles(pool, step)
            for d in (-2, -1, 0):
                scatter(last_tile + d)

            for b in range(NB):
                pool.wait_ge(sum_done, b + 1)
                now = y_both[:, 0, TB * b:TB * (b + 1), :]
                nc.gpsimd.tensor_tensor(now, now, parts[:, P_GB, b:b + 1, :].broadcast_to([128, TB, D]), ALU.mult).then_inc(gated, 1)

        @block.tensor
        def _(pe):
            def transpose_h(i):
                pe.wait_ge(h_in[i.place], i.turn * 16 + 16)
                if i.past(1):
                    pe.wait_ge(h_lo_done, i.n)
                nc.tensor.transpose(hT_ps[:, 0:128], h[:, i.place, :], ident[:]).then_inc(hT_done, 1)

            def up(i, e):
                pe.wait_ge(h_lo_done, i.n + 1)
                if i.past(2):
                    pe.wait_ge(g_done, i.n - 1)
                weights = lambda w: w[:, bass.ds(e, 1), :].rearrange("p a n -> p (a n)")
                hi, lo = h_hi[:, i.par, :], h_lo[:, i.par, :]
                for w, (acc, done) in enumerate(((gate_ps, gate_done), (up_ps, up_done))):
                    nc.tensor.matmul(acc[i.par][:], hi, weights(w13_hi[w]), start=True, stop=False)
                    nc.tensor.matmul(acc[i.par][:], hi, weights(w13_lo[w]), start=False, stop=False)
                    nc.tensor.matmul(acc[i.par][:], lo, weights(w13_hi[w]), start=False, stop=True).then_inc(done, 1)

            def transpose_g(i):
                pe.wait_ge(g_done, i.n + 1)
                if i.past(1):
                    pe.wait_ge(g_lo_done, i.n)
                for fb in range(FB):
                    last = nc.tensor.transpose(gT_ps[:, fb * 128:(fb + 1) * 128], g[:, i.par, fb * 128:(fb + 1) * 128], ident[:])
                last.then_inc(gT_done, 1)

            def down(i, e):
                pe.wait_ge(g_lo_done, i.n + 1)
                if i.past(2):
                    pe.wait_ge(y_done, i.n - 1)
                for fb in range(FB):
                    both = w2[fb][:, bass.ds(e, 1), :].rearrange("p a n -> p (a n)")
                    high = w2[fb][:, bass.ds(e, 1), 0:D].rearrange("p a n -> p (a n)")
                    if fb == 0:
                        nc.tensor.matmul(y_ps[i.par][:, 0:2 * D], g_hi[:, i.par, fb, :], both, start=True, stop=False)
                    nc.tensor.matmul(y_ps[i.par][:, 0:D], g_lo[:, i.par, fb, :], high, start=False, stop=False)
                    if fb > 0:
                        last = nc.tensor.matmul(y_ps[i.par][:, 0:2 * D], g_hi[:, i.par, fb, :], both, start=False, stop=fb == FB - 1)
                last.then_inc(down_done, 1)

            def expert(i):
                return pe.value_load(expert_of[0:1, bass.ds(i.n, 1)], min_val=0, max_val=E - 1)

            transpose_h(Tile(0, 0))
            known = {}

            def step(i):
                if i.step == 0:
                    known.clear()
                    known[0] = expert(i)
                if (i + 1).exists():
                    transpose_h(i + 1)
                up(i, known[i.step])
                if (i + -2).exists():
                    behind = known[i.step - 2] if i.step >= 2 else expert(i + -2)
                if (i + -1).exists():
                    transpose_g(i + -1)
                if i.step + 1 < BODY:
                    known[i.step + 1] = expert(i + 1)
                if (i + -2).exists():
                    down(i + -2, behind)

            tiles(pe, step)
            transpose_g(last_tile)
            down(last_tile + -1, expert(last_tile + -1))
            down(last_tile, expert(last_tile))

        @block.scalar
        def _(act):
            def high_h(i):
                act.wait_ge(hT_done, i.n + 1)
                if i.past(2):
                    act.wait_ge(up_done, i.n - 1)
                nc.scalar.activation(h_hi[:, i.par, :], hT_ps[:, 0:128], ACT.Copy).then_inc(h_hi_done, 1)

            def gate(i):
                act.wait_ge(gate_done, i.n + 1)
                if i.past(2):
                    act.wait_ge(g_done, i.n - 1)
                nc.scalar.activation(silu[:, i.par, :], gate_ps[i.par][:], ACT.Silu).then_inc(silu_done, 1)

            def high_g(i):
                act.wait_ge(gT_done, i.n + 1)
                if i.past(2):
                    act.wait_ge(down_done, i.n - 1)
                nc.scalar.activation(g_hi[:, i.par, :, :].rearrange("p a c -> p (a c)"), gT_ps[:], ACT.Copy).then_inc(g_hi_done, 1)

            def low_y(i):
                act.wait_ge(down_done, i.n + 1)
                if i.past(2):
                    act.wait_ge(y_done, i.n - 1)
                nc.scalar.activation(y_low[:, i.par, :], y_ps[i.par][:, D:2 * D], ACT.Copy).then_inc(y_low_done, 1)

            nc.scalar.activation(table_only[:], keep["den"][:, 0:1], ACT.Silu)
            high_h(Tile(0, 0))

            def step(i):
                if (i + 1).exists():
                    high_h(i + 1)
                gate(i)
                if (i + -1).exists():
                    high_g(i + -1)
                if (i + -2).exists():
                    low_y(i + -2)

            tiles(act, step)
            high_g(last_tile)
            low_y(last_tile + -1)
            low_y(last_tile)
            act.wait_ge(weight_done, 1)
            for b in range(NB):
                if b % 2 == 0:
                    act.wait_ge(both_in[b // 2], 32)
                for t in range(TB * b, TB * (b + 1)):
                    last = nc.scalar.activation(y_both[:, 0, t, :], y_both[:, 0, t, :], ACT.Copy, scale=route_w[:, 0, t:t + 1])
                last.then_inc(first_done, 1)

        @block.vector
        def _(dve):
            def low_h(i):
                dve.wait_ge(h_hi_done, i.n + 1)
                if i.past(2):
                    dve.wait_ge(up_done, i.n - 1)
                nc.vector.tensor_tensor(h_lo[:, i.par, :], hT_ps[:, 0:128], h_hi[:, i.par, :].bitcast(F32),
                                        ALU.subtract).then_inc(h_lo_done, 1)

            def multiply(i):
                dve.wait_ge(silu_done, i.n + 1)
                dve.wait_ge(up_done, i.n + 1)
                if i.past(2):
                    dve.wait_ge(gT_done, i.n - 1)
                nc.vector.tensor_tensor(g[:, i.par, :], silu[:, i.par, :], up_ps[i.par][:], ALU.mult).then_inc(g_done, 1)

            def low_g(i):
                dve.wait_ge(g_hi_done, i.n + 1)
                if i.past(2):
                    dve.wait_ge(down_done, i.n - 1)
                nc.vector.tensor_tensor(g_lo[:, i.par, :, :].rearrange("p a c -> p (a c)"), gT_ps[:],
                                        g_hi[:, i.par, :, :].rearrange("p a c -> p (a c)").bitcast(F32),
                                        ALU.subtract).then_inc(g_lo_done, 1)

            def add_y(i):
                dve.wait_ge(y_low_done, i.n + 1)
                if i.past(RING):
                    dve.wait_ge(y_out[i.place], i.turn * 16)
                nc.vector.tensor_tensor(y[:, i.place, :], y_ps[i.par][:, 0:D], y_low[:, i.par, :], ALU.add).then_inc(y_done, 1)

            low_h(Tile(0, 0))

            def step(i):
                if (i + 1).exists():
                    low_h(i + 1)
                multiply(i)
                if (i + -1).exists():
                    low_g(i + -1)
                if (i + -2).exists():
                    add_y(i + -2)

            tiles(dve, step)
            low_g(last_tile)
            add_y(last_tile + -1)
            add_y(last_tile)

            logits, top, one_hot, diff, expd, tmp, tmp2, pick = (keep[n] for n in
                                                                 ("logits", "top", "one_hot", "diff", "expd", "tmp", "tmp2", "pick"))
            wide = lambda a: a[:, :, None].broadcast_to([128, NT, E])
            tt, ts = nc.vector.tensor_tensor, nc.vector.tensor_scalar
            n = [0]

            def step(ins):
                n[0] += 1
                ins.then_inc(chain, 1)
                dve.wait_ge(chain, n[0])

            step(nc.vector.scalar_tensor_tensor(tmp2[:], logits[:], -1.0, logits[:], ALU.mult, ALU.max))
            for i in range(2):
                step(tt(tmp[:], tmp2[:], wide(top[i]), ALU.max))
                step(nc.vector.reciprocal(tmp[:], tmp[:]))
                step(nc.vector.scalar_tensor_tensor(tmp[:], diff[i][:], -1.0, tmp[:], ALU.mult, ALU.mult))
                step(ts(tmp[:], tmp[:], 0.02, None, ALU.is_gt))
                if i:
                    step(tt(tmp[:], tmp[:], one_hot[0][:], ALU.max))
                step(ts(tmp[:], tmp[:], -1.0, 1.0, ALU.mult, ALU.add))
                step(tt(tmp[:], tmp[:], expd[i][:], ALU.mult))
                step(nc.vector.reduce_sum(pick[:], tmp[:], AX.X))
                nc.vector.reciprocal(route_w[:, i, :], pick[:]).then_inc(weight_done, 1)
                dve.wait_ge(weight_done, i + 1)

            def weigh(b):
                dve.wait_ge(first_done, b + 1)
                for t in range(TB * b, TB * (b + 1)):
                    last = nc.vector.scalar_tensor_tensor(y_both[:, 0, t, :], y_both[:, 1, t, :], route_w[:, 1, t:t + 1],
                                                          y_both[:, 0, t, :], ALU.mult, ALU.add)
                last.then_inc(sum_done, 1)

            def residual(b):
                dve.wait_ge(gated, b + 1)
                now = slice(TB * b, TB * (b + 1))
                nc.vector.tensor_tensor(x1[:, now, :], x1[:, now, :], y_both[:, 0, now, :], ALU.add).then_inc(out_done, 1)

            weigh(0)
            for b in range(1, NB):
                weigh(b)
                residual(b - 1)
            residual(NB - 1)


def build(nc, io, out):
    io["sums"] = nc.dram_tensor("sums", (NB * G * 128, L), F32, kind="Internal").ap()
    io["recips"] = nc.dram_tensor("recips", (NB * H, L), F32, kind="Internal").ap()
    io["h_rows"] = nc.dram_tensor("h_rows", (T, D), F32, kind="Internal").ap()
    io["y_rows"] = nc.dram_tensor("y_rows", (2 * T + SLOTS, D), F32, kind="Internal").ap()
    ctx = ExitStack()
    with ctx:
        sb = lambda n, s, d=F32: ctx.enter_context(nc.sbuf_tensor(n, s, d))
        keep = dict(mod=sb("mod", [128, 6, NB]), ident=sb("ident", [128, 128]), den=sb("den", [128, L]),
                    out_T=sb("out_T", [128, 2, L]), sums_out=[ctx.enter_context(nc.semaphore(f"sums_out{i}")) for i in range(2)])
        with ExitStack() as attn:
            ab = lambda n, s, d=F32: attn.enter_context(nc.sbuf_tensor(n, s, d))
            for n in ("q_hi", "q_lo", "k_hi", "k_lo"):
                keep[n] = ab(n, [128, T])
            keep["q_bf"], keep["k_bf"] = ab("q_bf", [128, T], BF16), ab("k_bf", [128, T], BF16)
            keep["v_all"] = ab("v_all", [128, NT, D])
            keep["q_own"] = ab("q_own", [128, G, HG, L], BF16)
            keep["q_pack"] = ab("q_pack", [128, 2, L], F32R)
            keep["k_pack"] = ab("k_pack", [128, 2, L])
            keep["v_aug"] = ab("v_aug", [128, 2, TB, HG, 32])
            keep["head_mask"] = ab("head_mask", [128, HG])
            qkv_phase(nc, io, keep)
            if io.get("stop") == 1:
                return
            attention_phase(nc, io, keep)
            if io.get("stop") == 2:
                return
        keep.update(x1=sb("x1", [128, NT, D]), parts=sb("parts", [128, 3, NB, D]),
                    w13_hi=[sb(f"w{w}_hi", [128, E, FF], F32R) for w in (1, 3)], w13_lo=[sb(f"w{w}_lo", [128, E, FF], F32R) for w in (1, 3)],
                    w2=[sb(f"w2_{fb}", [128, E, 2 * D], F32R) for fb in range(FB)],
                    src=sb("src", [128, NS], U32), dst=sb("dst", [128, NS], U32), expert_of=sb("expert_of", [1, NS], I32),
                    route_w=sb("route_w", [128, 2, NT]))
        keep.update(logits=sb("logits", [128, NT, E]), tmp=sb("tmp", [128, NT, E]), tmp2=sb("tmp2", [128, NT, E]), pick=sb("pick", [128, NT]))
        keep.update({n: [sb(f"{n}{i}", [128, NT, E]) for i in range(2)] for n in ("one_hot", "diff", "expd")},
                    top=[sb(f"top{i}", [128, NT]) for i in range(2)])
        route_phase(nc, io, keep)
        if io.get("stop") == 3:
            return
        expert_phase(nc, io, keep, out)


def layouts(inputs):
    import numpy as np

    a = {k: np.asarray(v) for k, v in inputs.items()}
    rows = lambda m: np.ascontiguousarray(m.reshape(NT, 128, D).transpose(1, 0, 2))
    head_of = (np.arange(128) % S_ROW) // DK
    arrays = {
        "x": np.ascontiguousarray(a["L0_attn_x"]).reshape(T, D),
        "c_T": np.ascontiguousarray(a["L0_c"].T),
        "wmod": a["L0_wmod"],
        "wqkv": a["L0_attn_W_qkv"],
        "bias_qk": np.ascontiguousarray(a["L0_attn_b_qkv"][0:2 * D].reshape(2, D).T),
        "bias_out": a["L0_attn_b_out"],
        "w1_T": np.ascontiguousarray(a["L0_ffn_w1"].transpose(0, 2, 1)),
        "w3_T": np.ascontiguousarray(a["L0_ffn_w3"].transpose(0, 2, 1)),
        "w2_T": np.ascontiguousarray(a["L0_ffn_w2"].transpose(0, 2, 1).reshape(E, FB, 128, D).transpose(0, 2, 1, 3)),
        "ident": np.eye(128, dtype=np.float32),
        "above": (np.triu(np.ones((128, 128)), 1) * -BIG).astype(np.float32),
        "head_mask": (head_of[:, None] == np.arange(HG)[None, :]).astype(np.float32),
        "one_rows": ((np.arange(128) < S_ROW) & (np.arange(128) % DK == 0)).astype(np.float32)[:, None],
    }
    side_by_side = {
        "wout": a["L0_attn_W_out"],
        "gate_T": a["L0_ffn_gate_w"].T,
        "number": np.arange(128)[None, :].repeat(128, 0),
        "before": np.triu(np.ones((128, 128)), 1),
        "multiple": (128 * np.arange(NT))[None, :].repeat(128, 0),
        "partition": np.arange(128)[:, None],
        "bias_v": a["L0_attn_b_qkv"][2 * D:3 * D, None],
        "spare_row": (2 * T + np.arange(SLOTS)).reshape(NS, 128).T,
        "rank": np.tile(np.arange(E, 0, -1), NT)[None, :].repeat(128, 0),
    }
    arrays["consts"] = np.concatenate([side_by_side[n].astype(np.float32, copy=False) for n in CONSTS], 1)
    return arrays


def kernel(**inputs):
    import numpy as np
    import concourse.bacc as bacc
    from concourse.bass_utils import run_bass_kernel_spmd

    nc = bacc.Bacc("TRN2", target_bir_lowering=False, num_devices=1)
    arrays = layouts(inputs)
    io = {n: nc.dram_tensor("in_" + n, v.shape, mybir.dt.from_np(v.dtype), kind="ExternalInput").ap() for n, v in arrays.items()}
    io["x"] = io["x"].rearrange("(t p) c -> p t c", p=128)
    out = nc.dram_tensor("out_x", (T, D), F32, kind="ExternalOutput").ap()
    build(nc, io, out.rearrange("(t p) c -> p t c", p=128))
    r = run_bass_kernel_spmd(nc, [{"in_" + n: v for n, v in arrays.items()}], core_ids=[0])
    return r.results[0]["out_x"].reshape(NB, L, D)
```
